# Optimizing a Trainium2 kernel written in Bass

```python
import numpy as np
import jax
import jax.numpy as jnp

def _softmax(x, axis=-1):
    return jax.nn.softmax(x, axis=axis)

def _gelu(x):
    return jax.nn.gelu(x, approximate=True)

def _silu(x):
    return jax.nn.silu(x)

def _sigmoid(x):
    return jax.nn.sigmoid(x)

def _layernorm(x, axis=-1, eps=1e-05):
    m = jnp.mean(x, axis=axis, keepdims=True)
    v = jnp.var(x, axis=axis, keepdims=True)
    return (x - m) / jnp.sqrt(v + eps)

def _scatter_add(tgt, idx, src, axis=0):
    return tgt.at[idx].add(src)

def _segment_sum(src, seg, n):
    return jax.ops.segment_sum(src, seg, n)
kernel_name = 'mk_perceiver_d1_seqx_r4_fd16da'

def setup_inputs(seed: int=0):
    np.random.seed(seed)
    _w = jnp.asarray

    def _rec_inputs():
        import jax
        import jax.numpy as jnp
        _rk = jax.random.key(seed)
        x = 0.002226 + 0.9996 * jax.random.normal(jax.random.fold_in(_rk, 1), (4, 256, 256), jnp.float32)
        _lenS = 256 - jax.random.randint(jax.random.fold_in(_rk, 7), (4,), 0, max(1, 256 // 4) + 1, jnp.int32)
        _lenS2 = 4096 - jax.random.randint(jax.random.fold_in(_rk, 8), (4,), 0, max(1, 4096 // 4) + 1, jnp.int32)
        _ctx_1024P = jax.random.normal(jax.random.fold_in(_rk, 11), (4, 16, 256), jnp.float32)
        _ctx_1024c = jax.random.dirichlet(jax.random.fold_in(_rk, 511), 0.3 * jnp.ones((16,), jnp.float32), (4, 4096))
        _ctx_1024t = jnp.einsum('bsk,bkd->bsd', _ctx_1024c, _ctx_1024P)
        _ctx_1024t = _ctx_1024t * jax.lax.rsqrt(jnp.mean(jnp.square(_ctx_1024t)) + 1e-12) * 0.953939
        ctx_1024 = -0.000125008 + 0.999885 * (_ctx_1024t + 0.3 * jax.random.normal(jax.random.fold_in(_rk, 611), (4, 4096, 256), jnp.float32))
        _validS = jnp.arange(256)[None, :] < _lenS[:, None]
        _validS2 = jnp.arange(4096)[None, :] < _lenS2[:, None]
        _causal = jnp.tril(jnp.ones((256, 256), dtype=bool))
        mask_BxS2_bk0 = jnp.logical_not(jnp.broadcast_to(_validS2[:, :], (4, 4096)))
        return (x, ctx_1024, mask_BxS2_bk0)
    x, ctx_1024, mask_BxS2_bk0 = _rec_inputs()

    def _L0_xattn_setup():
        import jax, jax.numpy as jnp
        import numpy as np
        EPS = 1e-05

        def layer_norm(x, g, b):
            mu = jnp.mean(x, axis=-1, keepdims=True)
            var = jnp.mean((x - mu) ** 2, axis=-1, keepdims=True)
            return (x - mu) * jax.lax.rsqrt(var + EPS) * g + b
        key = jax.random.key(seed)
        ks = jax.random.split(key, 8)
        b, n, l, D = (8, 1024, 64, 256)
        heads, dim_head = (16, 64)
        inner = heads * dim_head
        x = jax.random.normal(ks[0], (b, n, D), dtype=jnp.float32)
        latents = jax.random.normal(ks[1], (b, l, D), dtype=jnp.float32)
        mask = jax.random.randint(ks[2], (b, n), 0, 2) > 0
        Wq = jax.random.normal(ks[3], (D, inner), dtype=jnp.float32) * D ** (-0.5)
        Wkv = jax.random.normal(ks[4], (D, 2 * inner), dtype=jnp.float32) * D ** (-0.5)
        Wout = jax.random.normal(ks[5], (inner, D), dtype=jnp.float32) * inner ** (-0.5)
        g1 = jnp.ones((D,), jnp.float32)
        b1 = jnp.zeros((D,), jnp.float32)
        g2 = jnp.ones((D,), jnp.float32)
        b2 = jnp.zeros((D,), jnp.float32)
        return {'x': x, 'latents': latents, 'mask': mask, 'g1': g1, 'b1': b1, 'g2': g2, 'b2': b2, 'Wq': Wq, 'Wkv': Wkv, 'Wout': Wout}
    _L0_xattn_all = _L0_xattn_setup()
    _L0_xattn_in = {k: v for k, v in _L0_xattn_all.items() if k in ('g1', 'b1', 'g2', 'b2', 'Wq', 'Wkv', 'Wout')}
    del _L0_xattn_all

    def _L0_attn_setup():
        import jax, jax.numpy as jnp
        import numpy as np
        C = 256
        H = 16
        K = 2
        B, N = (4, 1024)

        def _heads(t):
            shp = t.shape
            d = shp[-1] // H
            t = t.reshape(shp[:-1] + (H, d))
            return jnp.swapaxes(t, -2, -3)
        key = jax.random.key(seed)
        ks_ = jax.random.split(key, 12)
        s = 1.0 / np.sqrt(C)
        inp = {'x': jax.random.normal(ks_[0], (B, N, C), dtype=jnp.float32), 'Wq': jax.random.normal(ks_[1], (C, C), dtype=jnp.float32) * s, 'bq': jnp.zeros((C,), dtype=jnp.float32), 'Wk': jax.random.normal(ks_[2], (K, C, C), dtype=jnp.float32) * s, 'bk': jnp.zeros((K, C), dtype=jnp.float32), 'Wv': jax.random.normal(ks_[3], (K, C, C), dtype=jnp.float32) * s, 'bv': jnp.zeros((K, C), dtype=jnp.float32), 'Wo': jax.random.normal(ks_[4], (C, C), dtype=jnp.float32) * s, 'bo': jnp.zeros((C,), dtype=jnp.float32), 'ln_g': jnp.ones((C,), dtype=jnp.float32), 'ln_b': jnp.zeros((C,), dtype=jnp.float32)}
        return inp
    _L0_attn_all = _L0_attn_setup()
    _L0_attn_in = {k: v for k, v in _L0_attn_all.items() if k in ('Wq', 'bq', 'Wk', 'bk', 'Wv', 'bv', 'Wo', 'bo', 'ln_g', 'ln_b')}
    del _L0_attn_all

    def _L0_ffn_setup():
        import jax, jax.numpy as jnp
        import numpy as np
        DIM = 256
        DEPTH = 6
        HEADS = 16
        DIM_HEAD = 64
        WINDOW = 64
        INNER = HEADS * DIM_HEAD
        DIM_INNER = int(DIM * 4 * 2 / 3)
        QK_SCALE = 8.0

        def shift_tokens(t):
            a, s = jnp.split(t, 2, -1)
            s = jnp.pad(s, ((0, 0), (1, 0), (0, 0)))[:, :-1]
            return jnp.concatenate([a, s], -1)

        def l2norm(t):
            return t / jnp.maximum(jnp.linalg.norm(t, axis=-1, keepdims=True), 1e-12)

        def rotate_half(x):
            x1, x2 = jnp.split(x, 2, -1)
            return jnp.concatenate([-x2, x1], -1)

        def rotary_tables(n):
            half = jnp.arange(0, DIM_HEAD, 2, dtype=jnp.float32)
            inv_freq = 1.0 / 10000.0 ** (half / DIM_HEAD)
            t = jnp.arange(n, dtype=jnp.float32)
            freqs = t[:, None] * inv_freq[None, :]
            freqs = jnp.concatenate([freqs, freqs], -1)
            base_scale = (half + 0.4 * DIM_HEAD) / (1.4 * DIM_HEAD)
            power = (t - n // 2) / (WINDOW // 2)
            scale = base_scale[None, :] ** power[:, None]
            scale = jnp.concatenate([scale, scale], -1)
            return (freqs, scale)

        def local_attention(q, k, v):
            b, h, n, d = q.shape
            w = WINDOW
            nw = n // w
            bq = q.reshape(b, h, nw, w, d)
            bk = k.reshape(b, h, nw, w, d)
            bv = v.reshape(b, h, nw, w, d)

            def look(t):
                p = jnp.pad(t, ((0, 0), (0, 0), (1, 0), (0, 0), (0, 0)))
                return jnp.concatenate([p[:, :, :nw], p[:, :, 1:]], axis=3)
            bk2, bv2 = (look(bk), look(bv))
            seq = jnp.arange(n).reshape(nw, w)
            seq_p = jnp.pad(seq, ((1, 0), (0, 0)), constant_values=-1)
            jt = jnp.concatenate([seq_p[:nw], seq_p[1:]], axis=1)
            it = seq[:, :, None]
            jb = jt[:, None, :]
            mask = (it < jb) | (it > jb + w) | (jb == -1)
            sim = jnp.einsum('bhwie,bhwje->bhwij', bq, bk2) * QK_SCALE
            sim = jnp.where(mask, -jnp.finfo(sim.dtype).max, sim)
            attn = jax.nn.softmax(sim, -1)
            out = jnp.einsum('bhwij,bhwje->bhwie', attn, bv2)
            return out.reshape(b, h, n, d)

        def attn_layer(x, Wqkv, qs, ksc, Wo):
            b, n, _ = x.shape
            qkv = x @ Wqkv
            q, k, v = jnp.split(qkv, 3, -1)
            sh = lambda t: t.reshape(b, n, HEADS, DIM_HEAD).transpose(0, 2, 1, 3)
            q, k, v = (sh(q), sh(k), sh(v))
            q = l2norm(q) * qs
            k = l2norm(k) * ksc
            freqs, scale = rotary_tables(n)
            cos, sin = (jnp.cos(freqs), jnp.sin(freqs))
            q = q * cos * scale + rotate_half(q) * sin * scale
            inv = 1.0 / scale
            k = k * cos * inv + rotate_half(k) * sin * inv
            out = local_attention(q, k, v)
            out = out.transpose(0, 2, 1, 3).reshape(b, n, INNER)
            return out @ Wo

        def ffn_layer(x, g, bln, W1, b1, W2, b2):
            mu = x.mean(-1, keepdims=True)
            var = ((x - mu) ** 2).mean(-1, keepdims=True)
            xn = (x - mu) / jnp.sqrt(var + 1e-05) * g + bln
            hg = xn @ W1 + b1
            a, gate = jnp.split(hg, 2, -1)
            return a * jax.nn.gelu(gate, approximate=False) @ W2 + b2
        key = jax.random.key(seed)
        ks = jax.random.split(key, 8)
        B, N = (2, 512)
        init = lambda k, shape: jax.random.normal(k, shape, jnp.float32) * 0.02
        return {'x': jax.random.normal(ks[0], (B, N, DIM), jnp.float32), 'Wqkv': init(ks[1], (DEPTH, DIM, 3 * INNER)), 'q_scale': jnp.ones((DEPTH, DIM_HEAD), jnp.float32), 'k_scale': jnp.ones((DEPTH, DIM_HEAD), jnp.float32), 'Wo': init(ks[2], (DEPTH, INNER, DIM)), 'ln_g': jnp.ones((DEPTH, DIM), jnp.float32), 'ln_b': jnp.zeros((DEPTH, DIM), jnp.float32), 'W1': init(ks[3], (DEPTH, DIM, 2 * DIM_INNER)), 'b1': jnp.zeros((DEPTH, 2 * DIM_INNER), jnp.float32), 'W2': init(ks[4], (DEPTH, DIM_INNER, DIM)), 'b2': jnp.zeros((DEPTH, DIM), jnp.float32)}
    _L0_ffn_all = _L0_ffn_setup()
    _L0_ffn_in = {k: v for k, v in _L0_ffn_all.items() if k in ('Wqkv', 'q_scale', 'k_scale', 'Wo', 'ln_g', 'ln_b', 'W1', 'b1', 'W2', 'b2')}
    del _L0_ffn_all
    return {'x': x, 'ctx_1024': ctx_1024, 'mask_BxS2_bk0': mask_BxS2_bk0, 'L0_xattn_g1': _L0_xattn_in['g1'], 'L0_xattn_b1': _L0_xattn_in['b1'], 'L0_xattn_g2': _L0_xattn_in['g2'], 'L0_xattn_b2': _L0_xattn_in['b2'], 'L0_xattn_Wq': _L0_xattn_in['Wq'], 'L0_xattn_Wkv': _L0_xattn_in['Wkv'], 'L0_xattn_Wout': _L0_xattn_in['Wout'], 'L0_attn_Wq': _L0_attn_in['Wq'], 'L0_attn_bq': _L0_attn_in['bq'], 'L0_attn_Wk': _L0_attn_in['Wk'], 'L0_attn_bk': _L0_attn_in['bk'], 'L0_attn_Wv': _L0_attn_in['Wv'], 'L0_attn_bv': _L0_attn_in['bv'], 'L0_attn_Wo': _L0_attn_in['Wo'], 'L0_attn_bo': _L0_attn_in['bo'], 'L0_attn_ln_g': _L0_attn_in['ln_g'], 'L0_attn_ln_b': _L0_attn_in['ln_b'], 'L0_ffn_Wqkv': _L0_ffn_in['Wqkv'], 'L0_ffn_q_scale': _L0_ffn_in['q_scale'], 'L0_ffn_k_scale': _L0_ffn_in['k_scale'], 'L0_ffn_Wo': _L0_ffn_in['Wo'], 'L0_ffn_ln_g': _L0_ffn_in['ln_g'], 'L0_ffn_ln_b': _L0_ffn_in['ln_b'], 'L0_ffn_W1': _L0_ffn_in['W1'], 'L0_ffn_b1': _L0_ffn_in['b1'], 'L0_ffn_W2': _L0_ffn_in['W2'], 'L0_ffn_b2': _L0_ffn_in['b2']}

def reference(x, ctx_1024, mask_BxS2_bk0, L0_xattn_g1, L0_xattn_b1, L0_xattn_g2, L0_xattn_b2, L0_xattn_Wq, L0_xattn_Wkv, L0_xattn_Wout, L0_attn_Wq, L0_attn_bq, L0_attn_Wk, L0_attn_bk, L0_attn_Wv, L0_attn_bv, L0_attn_Wo, L0_attn_bo, L0_attn_ln_g, L0_attn_ln_b, L0_ffn_Wqkv, L0_ffn_q_scale, L0_ffn_k_scale, L0_ffn_Wo, L0_ffn_ln_g, L0_ffn_ln_b, L0_ffn_W1, L0_ffn_b1, L0_ffn_W2, L0_ffn_b2):
    import jax
    import jax.numpy as jnp

    def _L0_xattn_ref(x, latents, mask, g1, b1, g2, b2, Wq, Wkv, Wout):
        import jax, jax.numpy as jnp
        import numpy as np
        EPS = 1e-05

        def layer_norm(x, g, b):
            mu = jnp.mean(x, axis=-1, keepdims=True)
            var = jnp.mean((x - mu) ** 2, axis=-1, keepdims=True)
            return (x - mu) * jax.lax.rsqrt(var + EPS) * g + b
        heads, dim_head = (16, 64)
        b, n, D = x.shape
        l = latents.shape[1]
        xn = layer_norm(x, g1, b1)
        ln_lat = layer_norm(latents, g2, b2)
        q = ln_lat @ Wq
        kv = jnp.concatenate([xn, ln_lat], axis=1) @ Wkv
        k, v = jnp.split(kv, 2, axis=-1)

        def to_heads(t):
            return t.reshape(t.shape[0], t.shape[1], heads, dim_head).transpose(0, 2, 1, 3)
        q, k, v = (to_heads(q), to_heads(k), to_heads(v))
        scale = 1.0 / np.sqrt(np.sqrt(dim_head)).astype(np.float32)
        weight = jnp.einsum('bhld,bhnd->bhln', q * scale, k * scale)
        full_mask = jnp.concatenate([mask, jnp.ones((b, l), dtype=bool)], axis=1)
        neg = -jnp.finfo(weight.dtype).max
        weight = jnp.where(full_mask[:, None, None, :], weight, neg)
        weight = jax.nn.softmax(weight.astype(jnp.float32), axis=-1).astype(q.dtype)
        out = jnp.einsum('bhln,bhnd->bhld', weight, v)
        out = out.transpose(0, 2, 1, 3).reshape(b, l, heads * dim_head)
        return out @ Wout

    def _L0_attn_ref(x, Wq, bq, Wk, bk, Wv, bv, Wo, bo, ln_g, ln_b):
        import jax, jax.numpy as jnp
        import numpy as np
        C = 256
        H = 16
        K = 2
        B, N = (4, 1024)

        def _heads(t):
            shp = t.shape
            d = shp[-1] // H
            t = t.reshape(shp[:-1] + (H, d))
            return jnp.swapaxes(t, -2, -3)
        dtype = x.dtype
        q = x + jnp.einsum('bnc,cd->bnd', x, Wq) + bq
        ks = x[None] + jnp.einsum('bnc,kcd->kbnd', x, Wk) + bk[:, None, None, :]
        vs = x[None] + jnp.einsum('bnc,kcd->kbnd', x, Wv) + bv[:, None, None, :]
        q = _heads(q)
        ks = _heads(ks)
        vs = _heads(vs)
        scale = 1.0 / jnp.sqrt(jnp.asarray(N, dtype=jnp.float32))
        ks = ks.astype(jnp.float32) * scale
        vs = vs.astype(jnp.float32) * scale
        states = jnp.einsum('kbhnd,kbhne->kbhde', ks, vs)
        state = jnp.prod(states, axis=0)
        out = jnp.einsum('bhnd,bhde->bhne', q.astype(jnp.float32), state)
        out = out.astype(dtype)
        out = jnp.swapaxes(out, 1, 2).reshape(x.shape[0], x.shape[1], C)
        mu = jnp.mean(out, axis=-1, keepdims=True)
        var = jnp.var(out, axis=-1, keepdims=True)
        out = (out - mu) / jnp.sqrt(var + 1e-05) * ln_g + ln_b
        out = jnp.einsum('bnc,cd->bnd', out, Wo) + bo
        return out

    def _L0_ffn_ref(x, Wqkv, q_scale, k_scale, Wo, ln_g, ln_b, W1, b1, W2, b2):
        import jax, jax.numpy as jnp
        import numpy as np
        DIM = 256
        DEPTH = 6
        HEADS = 16
        DIM_HEAD = 64
        WINDOW = 64
        INNER = HEADS * DIM_HEAD
        DIM_INNER = int(DIM * 4 * 2 / 3)
        QK_SCALE = 8.0

        def shift_tokens(t):
            a, s = jnp.split(t, 2, -1)
            s = jnp.pad(s, ((0, 0), (1, 0), (0, 0)))[:, :-1]
            return jnp.concatenate([a, s], -1)

        def l2norm(t):
            return t / jnp.maximum(jnp.linalg.norm(t, axis=-1, keepdims=True), 1e-12)

        def rotate_half(x):
            x1, x2 = jnp.split(x, 2, -1)
            return jnp.concatenate([-x2, x1], -1)

        def rotary_tables(n):
            half = jnp.arange(0, DIM_HEAD, 2, dtype=jnp.float32)
            inv_freq = 1.0 / 10000.0 ** (half / DIM_HEAD)
            t = jnp.arange(n, dtype=jnp.float32)
            freqs = t[:, None] * inv_freq[None, :]
            freqs = jnp.concatenate([freqs, freqs], -1)
            base_scale = (half + 0.4 * DIM_HEAD) / (1.4 * DIM_HEAD)
            power = (t - n // 2) / (WINDOW // 2)
            scale = base_scale[None, :] ** power[:, None]
            scale = jnp.concatenate([scale, scale], -1)
            return (freqs, scale)

        def local_attention(q, k, v):
            b, h, n, d = q.shape
            w = WINDOW
            nw = n // w
            bq = q.reshape(b, h, nw, w, d)
            bk = k.reshape(b, h, nw, w, d)
            bv = v.reshape(b, h, nw, w, d)

            def look(t):
                p = jnp.pad(t, ((0, 0), (0, 0), (1, 0), (0, 0), (0, 0)))
                return jnp.concatenate([p[:, :, :nw], p[:, :, 1:]], axis=3)
            bk2, bv2 = (look(bk), look(bv))
            seq = jnp.arange(n).reshape(nw, w)
            seq_p = jnp.pad(seq, ((1, 0), (0, 0)), constant_values=-1)
            jt = jnp.concatenate([seq_p[:nw], seq_p[1:]], axis=1)
            it = seq[:, :, None]
            jb = jt[:, None, :]
            mask = (it < jb) | (it > jb + w) | (jb == -1)
            sim = jnp.einsum('bhwie,bhwje->bhwij', bq, bk2) * QK_SCALE
            sim = jnp.where(mask, -jnp.finfo(sim.dtype).max, sim)
            attn = jax.nn.softmax(sim, -1)
            out = jnp.einsum('bhwij,bhwje->bhwie', attn, bv2)
            return out.reshape(b, h, n, d)

        def attn_layer(x, Wqkv, qs, ksc, Wo):
            b, n, _ = x.shape
            qkv = x @ Wqkv
            q, k, v = jnp.split(qkv, 3, -1)
            sh = lambda t: t.reshape(b, n, HEADS, DIM_HEAD).transpose(0, 2, 1, 3)
            q, k, v = (sh(q), sh(k), sh(v))
            q = l2norm(q) * qs
            k = l2norm(k) * ksc
            freqs, scale = rotary_tables(n)
            cos, sin = (jnp.cos(freqs), jnp.sin(freqs))
            q = q * cos * scale + rotate_half(q) * sin * scale
            inv = 1.0 / scale
            k = k * cos * inv + rotate_half(k) * sin * inv
            out = local_attention(q, k, v)
            out = out.transpose(0, 2, 1, 3).reshape(b, n, INNER)
            return out @ Wo

        def ffn_layer(x, g, bln, W1, b1, W2, b2):
            mu = x.mean(-1, keepdims=True)
            var = ((x - mu) ** 2).mean(-1, keepdims=True)
            xn = (x - mu) / jnp.sqrt(var + 1e-05) * g + bln
            hg = xn @ W1 + b1
            a, gate = jnp.split(hg, 2, -1)
            return a * jax.nn.gelu(gate, approximate=False) @ W2 + b2
        for i in range(DEPTH):
            x = attn_layer(shift_tokens(x), Wqkv[i], q_scale[i], k_scale[i], Wo[i]) + x
            x = ffn_layer(shift_tokens(x), ln_g[i], ln_b[i], W1[i], b1[i], W2[i], b2[i]) + x
        return x
    x = x + _L0_xattn_ref(ctx_1024, _layernorm(x, axis=-1), mask_BxS2_bk0, L0_xattn_g1, L0_xattn_b1, L0_xattn_g2, L0_xattn_b2, L0_xattn_Wq, L0_xattn_Wkv, L0_xattn_Wout)
    x = x + _L0_attn_ref(_layernorm(x, axis=-1), L0_attn_Wq, L0_attn_bq, L0_attn_Wk, L0_attn_bk, L0_attn_Wv, L0_attn_bv, L0_attn_Wo, L0_attn_bo, L0_attn_ln_g, L0_attn_ln_b)
    x = x + _L0_ffn_ref(_layernorm(x, axis=-1), L0_ffn_Wqkv, L0_ffn_q_scale, L0_ffn_k_scale, L0_ffn_Wo, L0_ffn_ln_g, L0_ffn_ln_b, L0_ffn_W1, L0_ffn_b1, L0_ffn_W2, L0_ffn_b2)
    return x

_drawn_inputs = setup_inputs


def setup_inputs(seed=0):
    import zlib

    import numpy as np

    out = dict(_drawn_inputs(seed))
    spreads = {'L0_xattn_g1': (1.0, 0.2),
     'L0_xattn_b1': (0.0, 0.1),
     'L0_xattn_g2': (1.0, 0.2),
     'L0_xattn_b2': (0.0, 0.1),
     'L0_attn_bq': (0.0, 0.1),
     'L0_attn_bk': (0.0, 0.1),
     'L0_attn_bv': (0.0, 0.1),
     'L0_attn_bo': (0.0, 0.1),
     'L0_attn_ln_g': (1.0, 0.2),
     'L0_attn_ln_b': (0.0, 0.1),
     'L0_ffn_q_scale': (1.0, 0.6),
     'L0_ffn_k_scale': (1.0, 0.6),
     'L0_ffn_ln_g': (1.0, 0.6),
     'L0_ffn_ln_b': (0.0, 0.8),
     'L0_ffn_b1': (0.0, 0.576),
     'L0_ffn_b2': (0.0, 0.1)}
    factors = {}
    for name, (base, spread) in spreads.items():
        noise = np.random.default_rng([zlib.crc32(name.encode()), seed]).standard_normal(out[name].shape)
        drawn = base * np.exp(spread * noise) if base else spread * noise
        out[name] = jnp.asarray(drawn.astype(out[name].dtype))
    for name, factor in factors.items():
        out[name] = (out[name] * factor).astype(out[name].dtype)
    return out
```

```python
from contextlib import ExitStack

import concourse.bass as bass
import numpy as np
from concourse import mybir

F32 = mybir.dt.float32
I32 = mybir.dt.int32
U8 = mybir.dt.uint8
ALU = mybir.AluOpType
ACT = mybir.ActivationFunctionType
AX = mybir.AxisListType

P = 128
B, T, D = 4, 256, 256
S = 4096
H, DH = 16, 64
INNER = H * DH
PAIRS = H // 2
TT = T // P
KD = D // P
CHUNK = 256
CHUNKS = S // CHUNK
KT = CHUNK // P
LAYERS = 6
FF = int(D * 4 * 2 / 3)
FM = (FF + P - 1) // P
FWIDE = [FF // FM + (m < FF % FM) for m in range(FM)]
FAT = [sum(FWIDE[:m]) for m in range(FM)]
WINDOW = 64
LH, LD = 16, 16
EPS = 1e-5
FAR = 3.0e38
BAND = 1.0e30
QK_SCALE = 8.0

C_ID = 0
C_BAND0 = C_ID + P
C_BAND1 = C_BAND0 + P
C_BLOCK = C_BAND1 + 192
C_COS = C_BLOCK + P
C_SIN = C_COS + TT * 2 * DH
C_BIT = C_SIN + TT * 2 * DH
C_ALL = C_BIT + CHUNKS

R_G1, R_B1, R_G2, R_B2, R_BQ, R_LG, R_LB = (2 * j for j in range(7))
R_LAYER = 14
V_FG, V_FB, V_B1A, V_B1G = 0, 2, 4, 4 + FM
KINDS = 4 + 2 * FM
ROWS = R_LAYER + KINDS * LAYERS


def constants():
    c = np.zeros((P, C_ALL), np.float32)
    c[:, C_ID:C_ID + P] = np.eye(P, dtype=np.float32)
    q, k = np.arange(P)[:, None], np.arange(P)[None, :]
    c[:, C_BAND0:C_BAND0 + P] = np.where((q < k) | (q > k + WINDOW) , BAND, 0.0)
    q, k = np.arange(P, 2 * P)[:, None], np.arange(WINDOW, 2 * P)[None, :]
    c[:, C_BAND1:C_BAND1 + 192] = np.where((q < k) | (q > k + WINDOW), BAND, 0.0)
    d, e = np.arange(P)[:, None], np.arange(P)[None, :]
    c[:, C_BLOCK:C_BLOCK + P] = np.where(d // LD == e // LD, 1.0 / 1024.0 ** 2, 0.0)
    half = np.arange(0, DH, 2, dtype=np.float32)
    t = np.arange(T, dtype=np.float32)
    freqs = t[:, None] * (np.float32(1.0) / np.float32(10000.0) ** (half / np.float32(DH)))[None, :]
    freqs = np.concatenate([freqs, freqs], -1).astype(np.float32)
    base = (half + np.float32(0.4 * DH)) / np.float32(1.4 * DH)
    scale = base[None, :] ** ((t - T // 2) / np.float32(WINDOW // 2))[:, None]
    scale = np.concatenate([scale, scale], -1).astype(np.float32)
    sign = np.where(np.arange(DH) < DH // 2, -1.0, 1.0).astype(np.float32)
    both = [(np.cos(freqs) * s, np.sin(freqs) * sign * s) for s in (-np.float32(QK_SCALE) * scale, 1.0 / scale)]
    for n, at in enumerate((C_COS, C_SIN)):
        table = np.stack([both[0][n], both[1][n]], 1).astype(np.float32)
        c[:, at:at + TT * 2 * DH] = table.reshape(TT, P, 2 * DH).transpose(1, 0, 2).reshape(P, -1)
    c[:, C_BIT:C_BIT + CHUNKS] = 2.0 ** np.arange(CHUNKS)
    return c


class Chain:

    def __init__(self, eng, sem, base=0):
        self.eng, self.sem, self.base, self.n = eng, sem, base, 0

    def link(self, ins):
        self.n += 1
        ins.then_inc(self.sem, 1)
        self.eng.wait_ge(self.sem, self.base + self.n)


def hold(eng, sem):
    eng.sem_inc(sem, 1)


def begin_at(eng, count, sems):
    for sem in sems:
        eng.sem_inc(sem, count)


class Kernel:

    def __init__(self, nc, ctx, io):
        self.nc, self.io = nc, io
        self.ctx = ctx
        self.x = self.sb("x_all", [P, B * TT, D])
        self.y = self.sb("y_all", [P, B * TT, D])
        self.const = self.sb("const", [P, C_ALL])
        self.cols = self.sb("cols", [P, ROWS])
        self.ident = self.const[:, C_ID:C_ID + P]

    def sb(self, name, shape, dt=F32, ctx=None):
        return (ctx or self.ctx).enter_context(self.nc.sbuf_tensor(name, shape, dt))

    def banks(self, name, ctx):
        return ctx.enter_context(self.nc.psum_tensor(name, [P, 8, 512], F32))

    def sem(self, name):
        return self.ctx.enter_context(self.nc.semaphore(name))


def cross_attention(k):
    nc, io = k.nc, k.io
    U = 16
    with ExitStack() as ctx:
        sb = lambda name, shape, dt=F32: k.sb(name, shape, dt, ctx)
        rows = sb("rows", [P, P])
        wq = sb("wq", [P, KD, INNER])
        wkv = sb("wkv", [P, KD, 2 * INNER])
        wout = sb("wout", [P, PAIRS, D])
        mask_rows = sb("mask_rows", [B, S], U8)
        chunk_any = sb("chunk_any", [B, CHUNKS])
        word_f = sb("word_f", [B, 1])
        word_col = sb("word_col", [B, 1], I32)
        word = sb("word", [1, B], I32)
        lat = sb("lat", [P, TT, D])
        ctx_raw = sb("ctx_raw", [P, KT, D])
        chunk_mask = sb("chunk_mask", [P, CHUNK], U8)
        bias = sb("bias", [P, CHUNK])
        no_bias = sb("no_bias", [P, CHUNK])
        xn = sb("xn", [P, KT, D])
        inT = sb("inT", [P, KD, CHUNK])
        qT = sb("qT", [P, H, T])
        kT = sb("kT", [P, PAIRS, CHUNK])
        v = sb("v", [P, KT, INNER])
        prob = sb("prob", [P, TT, H, CHUNK])
        probT = sb("probT", [P, 2, KT, 512])
        oT = sb("oT", [P, PAIRS, T])
        o = sb("o", [P, TT, INNER])
        stats = sb("stats", [P, TT, 6])
        mv = sb("mv", [P, TT, 2])
        var = sb("var", [P, TT])
        rstd = sb("rstd", [P, TT])
        half = sb("half", [P, TT])
        top = sb("top", [P, TT, H])
        chunk_top = sb("chunk_top", [P, TT, H])
        new_top = sb("new_top", [P, TT, H])
        drop = sb("drop", [P, TT, H])
        alpha = sb("alpha", [P, TT, H])
        chunk_sum = sb("chunk_sum", [P, TT, H])
        total = sb("total", [P, TT, H])
        rtotal = sb("rtotal", [P, TT, H])
        ps = k.banks("ps_cross", ctx)
        PROJ, SCORE, TURN, OUT = 0, 2, 4, 6

        sem = k.sem
        const_in, x_in, mask_in, w_in = sem("const_in"), sem("x_in"), sem("mask_in"), sem("w_in")
        rows_zero, rows_in, cols_full, cols_done = sem("rows_zero"), sem("rows_in"), sem("cols_full"), sem("cols_done")
        words_out, words_in, q_zero = sem("words_out"), sem("words_in"), sem("q_zero")
        ctx_in, chunk_mask_in = sem("ctx_in"), sem("chunk_mask_in")
        ln_var, ln_rstd, lat_ready, xn_ready = sem("ln_var"), sem("ln_rstd"), sem("lat_ready"), sem("xn_ready")
        inT_full, inT_done, q_full, q_done = sem("inT_full"), sem("inT_done"), sem("q_full"), sem("q_done")
        k_full, k_done, v_full, v_done = sem("k_full"), sem("k_done"), sem("v_full"), sem("v_done")
        s_full, s_read, top_done, alpha_done = sem("s_full"), sem("s_read"), sem("top_done"), sem("alpha_done")
        p_ready, o_scaled, total_done = sem("p_ready"), sem("o_scaled"), sem("total_done")
        pT_full, pT_done, o_full, oT_done = sem("pT_full"), sem("pT_done"), sem("o_full"), sem("oT_done")
        back_full, back_done = sem("back_full"), sem("back_done")
        fin_ready, fin_full, fin_done = sem("fin_ready"), sem("fin_full"), sem("fin_done")
        x_full, x_done = sem("x_full"), sem("x_done")
        dve_step, pool_step, dve_held, pool_held = sem("dve_step"), sem("pool_step"), sem("dve_held"), sem("pool_held")

        ctx_dram = io["ctx_1024"].rearrange("b (c t p) d -> (b c) p t d", p=P, t=KT)
        mask_dram = io["mask"].rearrange("b (c n) -> (b c) n", n=CHUNK)

        def chunks(eng, b, body):
            bits = eng.value_load(word[0:1, bass.ds(b, 1)], min_val=0, max_val=2 ** CHUNKS - 1)
            with eng.Fori(0, CHUNKS) as c:
                with eng.If((bits >> c) & 1):
                    body(c)

        block = ctx.enter_context(nc.Block())

        @block.sync
        def _(sp):
            sp.dma_start(k.const[:, :], io["const"]).then_inc(const_in, 16)
            sp.dma_start(k.x[:, :, :], io["x"].rearrange("b (t p) c -> p (b t) c", p=P)).then_inc(x_in, 16)
            sp.dma_start(mask_rows[:, :], io["mask"]).then_inc(mask_in, 16)
            begin_at(sp, U, (xn_ready, ctx_in, chunk_mask_in, inT_full, inT_done, k_full, k_done, v_full, v_done, s_full, s_read,
                             top_done, alpha_done, p_ready, o_scaled, total_done, pT_full, pT_done, o_full, oT_done,
                             back_full, back_done))
            begin_at(sp, 4, (q_full, q_done, fin_full, fin_done))
            begin_at(sp, 2, (fin_ready, x_full, x_done))
            begin_at(sp, 1, (lat_ready,))
            sp.wait_ge(rows_zero, 1)
            for r, name in ((R_G1, "xattn_g1"), (R_B1, "xattn_b1"), (R_G2, "xattn_g2"), (R_B2, "xattn_b2"),
                            (R_BQ, "attn_bq"), (R_LG, "attn_ln_g"), (R_LB, "attn_ln_b")):
                sp.dma_start(rows[r:r + KD, :], io[name].rearrange("(k p) -> k p", p=P)).then_inc(rows_in, 16)
            layer_rows = [(V_FG + j, io["ffn_ln_g"][:, j * P:(j + 1) * P]) for j in range(KD)]
            layer_rows += [(V_FB + j, io["ffn_ln_b"][:, j * P:(j + 1) * P]) for j in range(KD)]
            layer_rows += [(V_B1A + m, io["ffn_b1"][:, FAT[m]:FAT[m] + FWIDE[m]]) for m in range(FM)]
            layer_rows += [(V_B1G + m, io["ffn_b1"][:, FF + FAT[m]:FF + FAT[m] + FWIDE[m]]) for m in range(FM)]
            for kind, src in layer_rows:
                r = R_LAYER + kind * LAYERS
                sp.dma_start(rows[r:r + LAYERS, 0:src.shape[1]], src).then_inc(rows_in, 16)
            sp.dma_start(wq[:, :, :], io["xattn_Wq"].rearrange("(k p) n -> p k n", p=P)).then_inc(w_in, 16)
            sp.dma_start(wkv[:, :, :], io["xattn_Wkv"].rearrange("(k p) n -> p k n", p=P)).then_inc(w_in, 16)
            sp.dma_start(wout[:, :, :], io["xattn_Wout"].rearrange("(k p) n -> p k n", p=P)).then_inc(w_in, 16)
            sp.wait_ge(words_out, 1)
            sp.dma_start(word[0:1, :], word_col[:, :]).then_inc(words_in, 16)
            sp.wait_ge(words_in, 16)
            uc_reg = sp.alloc_register("sp_uc")
            sp.reg_mov(uc_reg, U)
            with sp.Fori(1, B + 1) as turn:
                b = turn - 1
                def load(c):
                    uc = sp.snap(uc_reg)
                    sp.wait_ge(xn_ready, uc)
                    sp.dma_start(ctx_raw[:, :, :], ctx_dram[bass.ds(b * CHUNKS + c, 1)].rearrange("o p t d -> (o p) t d"))\
                        .then_inc(ctx_in, 16)
                    sp.dma_start(chunk_mask[:, :], mask_dram[bass.ds(b * CHUNKS + c, 1)].broadcast_to([P, CHUNK]))\
                        .then_inc(chunk_mask_in, 16)
                    sp.reg_add(uc_reg, uc_reg, U)
                chunks(sp, b, load)

        @block.tensor
        def _(pe):
            u_reg, uc_reg = pe.alloc_register("pe_u"), pe.alloc_register("pe_uc")
            pe.reg_mov(u_reg, U)
            pe.reg_mov(uc_reg, U)
            pe.wait_ge(const_in, 16)
            pe.wait_ge(rows_in, 16 * N_ROW_DMAS)
            pe.transpose(ps[:, OUT, 0:ROWS], rows[0:ROWS, :], k.ident[0:ROWS, 0:ROWS]).then_inc(cols_full, 1)
            pe.wait_ge(words_in, 16)

            def turn_input(src):
                for kk in range(KD):
                    for t in range(KT):
                        ins = pe.transpose(ps[:, PROJ + kk, t * P:(t + 1) * P], src[:, t, kk * P:(kk + 1) * P], k.ident)
                    ins.then_inc(inT_full, U // KD)

            def project_q(u, turn):
                pe.wait_ge(inT_done, u + U)
                for j in range(4):
                    if j >= 2:
                        pe.wait_ge(q_done, turn * 4 + j - 1)
                    for i in range(2):
                        pair = 2 * j + i
                        for kk in range(KD):
                            ins = pe.matmul(ps[:, PROJ + j % 2, i * T:(i + 1) * T], wq[:, kk, pair * P:(pair + 1) * P],
                                            inT[:, kk, :], start=kk == 0, stop=kk == KD - 1)
                    ins.then_inc(q_full, 1)

            def chunk_body(u, turn):
                pe.wait_ge(inT_done, u + U)
                pe.wait_ge(q_done, turn * 4 + 4)
                for j in range(4):
                    if j >= 2:
                        pe.wait_ge(k_done, u + 4 * (j - 1))
                    for i in range(2):
                        pair = 2 * j + i
                        for kk in range(KD):
                            ins = pe.matmul(ps[:, PROJ + j % 2, i * CHUNK:(i + 1) * CHUNK],
                                            wkv[:, kk, pair * P:(pair + 1) * P], inT[:, kk, :],
                                            start=kk == 0, stop=kk == KD - 1)
                    ins.then_inc(k_full, U // 4)
                for t in range(TT):
                    for pair in range(PAIRS):
                        s = t * PAIRS + pair
                        if t == 0 and pair % 2 == 0:
                            pe.wait_ge(k_done, u + 4 * (pair // 2 + 1))
                        pe.wait_ge(s_read, u + (s - 1 if s >= 2 else 0))
                        for i in range(2):
                            ins = pe.matmul(ps[:, SCORE + s % 2, i * CHUNK:(i + 1) * CHUNK],
                                            qT[:, 2 * pair + i, t * P:(t + 1) * P], kT[:, pair, :],
                                            start=True, stop=True)
                        ins.then_inc(s_full, 1)
                for j in range(4):
                    t, part = divmod(j, 2)
                    if j >= 2:
                        pe.wait_ge(v_done, u + 4 * (j - 1))
                    for kk in range(KD):
                        ins = pe.matmul(ps[:, PROJ + j % 2, :], inT[:, kk, t * P:(t + 1) * P],
                                        wkv[:, kk, INNER + part * 512:INNER + (part + 1) * 512],
                                        start=kk == 0, stop=kk == KD - 1)
                    ins.then_inc(v_full, U // 4)

                def weigh(pair):
                    pe.wait_ge(pT_done, u + 2 * pair + 2)
                    pe.wait_ge(oT_done, u + (2 * (pair - 1) if pair >= 2 else 0))
                    for t in range(KT):
                        for i in range(2):
                            ins = pe.matmul(ps[i * DH:(i + 1) * DH, OUT + pair % 2, 0:T],
                                            v[:, t, (2 * pair + i) * DH:(2 * pair + i + 1) * DH],
                                            probT[:, pair % 2, t, i * T:(i + 1) * T], start=t == 0, stop=t == KT - 1)
                    ins.then_inc(o_full, 2)

                def back(part):
                    pe.wait_ge(oT_done, u + 8 * (part + 1))
                    for t in range(TT):
                        if part:
                            pe.wait_ge(back_done, u + 4 * (t + 1))
                        for i in range(4):
                            ins = pe.transpose(ps[:, PROJ + t, i * P:(i + 1) * P],
                                               oT[:, 4 * part + i, t * P:(t + 1) * P], k.ident)
                        ins.then_inc(back_full, 4)

                for pair in range(PAIRS):
                    pe.wait_ge(p_ready, u + PAIRS + pair + 1)
                    for t in range(KT):
                        s = 2 * pair + t
                        pe.wait_ge(pT_done, u + (s - 1 if s >= 2 else 0))
                        for i in range(2):
                            for lt in range(TT):
                                ins = pe.transpose(ps[:, TURN + t, (i * TT + lt) * P:(i * TT + lt + 1) * P],
                                                   prob[:, lt, 2 * pair + i, t * P:(t + 1) * P], k.ident)
                        ins.then_inc(pT_full, 1)
                    if pair == 0:
                        pe.wait_ge(v_done, u + U)
                    if pair:
                        weigh(pair - 1)
                    if pair == 5:
                        back(0)
                weigh(PAIRS - 1)
                back(1)
                pe.reg_add(u_reg, u_reg, U)

            with pe.Fori(1, B + 1) as turn:
                b = turn - 1
                u = pe.snap(u_reg)
                pe.wait_ge(lat_ready, turn + 1)
                pe.wait_ge(v_done, u)
                pe.wait_ge(back_done, u)
                pe.wait_ge(w_in, 48)
                turn_input(lat)
                project_q(u, turn)
                chunk_body(u, turn)

                def step(c):
                    u, uc = pe.snap(u_reg), pe.snap(uc_reg)
                    pe.wait_ge(xn_ready, uc + U)
                    pe.wait_ge(v_done, u)
                    pe.wait_ge(back_done, u)
                    turn_input(xn)
                    chunk_body(u, turn)
                    pe.reg_add(uc_reg, uc_reg, U)
                chunks(pe, b, step)
                u = pe.snap(u_reg)
                for j in range(4):
                    t, part = divmod(j, 2)
                    pe.wait_ge(fin_ready, turn * 2 + t + 1)
                    if j < 2:
                        pe.wait_ge(back_done, u)
                    else:
                        pe.wait_ge(fin_done, turn * 4 + j - 1)
                    for i in range(4):
                        ins = pe.transpose(ps[:, PROJ + j % 2, i * P:(i + 1) * P],
                                           o[:, t, (4 * part + i) * P:(4 * part + i + 1) * P], k.ident)
                    ins.then_inc(fin_full, 1)
                for t in range(TT):
                    pe.wait_ge(fin_done, turn * 4 + 2 * (t + 1))
                    for pair in range(PAIRS):
                        ins = pe.matmul(ps[:, OUT + t, 0:D], oT[:, pair, t * P:(t + 1) * P], wout[:, pair, :],
                                        start=pair == 0, stop=pair == PAIRS - 1)
                    ins.then_inc(x_full, 1)
                pe.wait_ge(x_done, turn * 2 + 2)

        @block.scalar
        def _(act):
            u_reg = act.alloc_register("act_u")
            act.reg_mov(u_reg, U)
            act.wait_ge(cols_done, 1)
            act.wait_ge(q_zero, 1)
            act.wait_ge(words_in, 16)

            def input_out(u, g, bb):
                act.wait_ge(v_full, u)
                for kk in range(KD):
                    act.wait_ge(inT_full, u + 8 * (kk + 1))
                    act.activation(inT[:, kk, :], ps[:, PROJ + kk, 0:CHUNK], ACT.Identity,
                                   bias=k.cols[:, bb + kk:bb + kk + 1], scale=k.cols[:, g + kk:g + kk + 1])\
                        .then_inc(inT_done, U // KD)

            def chunk_body(u):
                act.wait_ge(s_full, u)
                for j in range(4):
                    act.wait_ge(k_full, u + 4 * (j + 1))
                    act.activation(kT[:, 2 * j:2 * j + 2, :], ps[:, PROJ + j % 2, :].rearrange("p (i n) -> p i n", i=2),
                                   ACT.Copy).then_inc(k_done, U // 4)
                act.wait_ge(o_scaled, u)
                act.wait_ge(total_done, u)
                for t in range(TT):
                    act.wait_ge(top_done, u + 8 * (t + 1))
                    act.activation(alpha[:, t, :], drop[:, t, :], ACT.Exp).then_inc(alpha_done, U // TT)
                    for h in range(H):
                        ins = act.activation(prob[:, t, h, :], prob[:, t, h, :], ACT.Exp, bias=new_top[:, t, h:h + 1],
                                             scale=-1.0, accum_out=chunk_sum[:, t, h:h + 1])
                        if h % 2:
                            ins.then_inc(p_ready, 1)
                act.wait_ge(back_full, u)
                for pair in range(PAIRS):
                    act.wait_ge(o_full, u + 2 * (pair + 1))
                    act.activation(oT[:, pair, :], ps[:, OUT + pair % 2, 0:T], ACT.Copy).then_inc(oT_done, 2)
                act.reg_add(u_reg, u_reg, U)

            with act.Fori(1, B + 1) as turn:
                b = turn - 1
                u = act.snap(u_reg)
                input_out(u, R_G2, R_B2)
                act.wait_ge(s_full, u)
                for j in range(4):
                    act.wait_ge(q_full, turn * 4 + j + 1)
                    for i in range(2):
                        half_q = qT[i * DH:(i + 1) * DH, :, :].rearrange("p (g e) n -> p g e n", e=2)
                        ins = act.activation(half_q[:, 2 * j:2 * j + 2, i, :],
                                             ps[i * DH:(i + 1) * DH, PROJ + j % 2, :].rearrange("p (g n) -> p g n", g=2),
                                             ACT.Copy, scale=-float(DH) ** -0.5)
                    ins.then_inc(q_done, 1)
                act.wait_ge(x_full, turn * 2)
                chunk_body(u)

                def step(c):
                    u = act.snap(u_reg)
                    input_out(u, R_G1, R_B1)
                    chunk_body(u)
                chunks(act, b, step)
                for j in range(4):
                    t, part = divmod(j, 2)
                    act.wait_ge(fin_full, turn * 4 + j + 1)
                    if j == 0:
                        act.wait_ge(back_full, act.snap(u_reg))
                    act.activation(oT[:, 4 * part:4 * part + 4, t * P:(t + 1) * P],
                                   ps[:, PROJ + j % 2, :].rearrange("p (i n) -> p i n", i=4), ACT.Copy)\
                        .then_inc(fin_done, 1)

        @block.vector
        def _(dve):
            u_reg, uc_reg, ln_reg, step_reg = (dve.alloc_register(f"dve_{n}") for n in ("u", "uc", "ln", "step"))
            for r, first in ((u_reg, U), (uc_reg, U), (ln_reg, 0)):
                dve.reg_mov(r, first)
            chain = Chain(dve, dve_step)
            chain.link(dve.memset(no_bias[:, :], 0.0))
            dve.wait_ge(cols_full, 1)
            dve.tensor_copy(k.cols[:, :], ps[:, OUT, 0:ROWS]).then_inc(cols_done, 1)
            dve.wait_ge(mask_in, 16)
            dve.wait_ge(const_in, 16)
            chain.link(dve.tensor_reduce(chunk_any[:, :], mask_rows[:, :].rearrange("b (c n) -> b c n", n=CHUNK), AX.X, ALU.max))
            chain.link(dve.tensor_tensor(chunk_any[:, :], chunk_any[:, :], k.const[0:B, C_BIT:C_BIT + CHUNKS], ALU.mult))
            chain.link(dve.tensor_reduce(word_f[:, :], chunk_any[:, :], AX.X, ALU.add))
            dve.tensor_copy(word_col[:, :], word_f[:, :]).then_inc(words_out, 1)
            dve.reg_mov(step_reg, chain.n)
            dve.wait_ge(x_in, 16)
            dve.wait_ge(words_in, 16)

            def norm(ch, src, dst, ln):
                hold(dve, dve_held)
                for t in range(TT):
                    ins = dve.bn_stats(stats[:, t, :], src(t))
                ch.link(ins)
                hold(dve, dve_held)
                for t in range(TT):
                    ins = dve.bn_aggr(mv[:, t, :], stats[:, t, :])
                ch.link(ins)
                dve.tensor_scalar(var[:, :], mv[:, :, 1], EPS, None, ALU.add).then_inc(ln_var, 1)
                dve.wait_ge(ln_rstd, ln + 1)
                return [dve.tensor_scalar(dst[:, t, :], src(t), mv[:, t, 0:1], rstd[:, t:t + 1], ALU.subtract, ALU.mult)
                        for t in range(TT)]

            def chunk_body(ch, u, key_bias):
                dve.wait_ge(pT_full, u)
                for t in range(TT):
                    for pair in range(PAIRS):
                        s = t * PAIRS + pair
                        dve.wait_ge(s_full, u + s + 1)
                        hold(dve, dve_held)
                        for i in range(2):
                            h = 2 * pair + i
                            ins = dve.tensor_tensor_reduce(
                                out=prob[:, t, h, :], in0=ps[:, SCORE + s % 2, i * CHUNK:(i + 1) * CHUNK], in1=key_bias,
                                scale=1.0, scalar=FAR, op0=ALU.add, op1=ALU.min, accum_out=chunk_top[:, t, h:h + 1])
                        ins.then_inc(s_read, 1)
                    dve.wait_ge(s_read, u + (t + 1) * PAIRS)
                    if t == 0:
                        dve.wait_ge(p_ready, u)
                    ch.link(dve.tensor_tensor(new_top[:, t, :], top[:, t, :], chunk_top[:, t, :], ALU.min))
                    dve.tensor_tensor(drop[:, t, :], new_top[:, t, :], top[:, t, :], ALU.subtract).then_inc(top_done, U // TT)
                    dve.wait_ge(top_done, u + (t + 1) * (U // TT))
                    ch.link(dve.tensor_copy(top[:, t, :], new_top[:, t, :]))
                dve.wait_ge(o_full, u)
                for j in range(4):
                    t, part = divmod(j, 2)
                    dve.wait_ge(v_full, u + 4 * (j + 1))
                    dve.tensor_copy(v[:, t, part * 512:(part + 1) * 512], ps[:, PROJ + j % 2, :]).then_inc(v_done, U // 4)

                def back(part):
                    for t in range(TT):
                        dve.wait_ge(back_full, u + 4 * (2 * part + t + 1))
                        dve.wait_ge(o_scaled, u + 8 * (t + 1))
                        out = o[:, t, part * 512:(part + 1) * 512]
                        dve.tensor_tensor(out, ps[:, PROJ + t, :], out, ALU.add).then_inc(back_done, 4)

                for pair in range(PAIRS):
                    if pair >= 2:
                        dve.wait_ge(o_full, u + 2 * (pair - 1))
                    for t in range(KT):
                        dve.wait_ge(pT_full, u + 2 * pair + t + 1)
                        dve.tensor_copy(probT[:, pair % 2, t, :], ps[:, TURN + t, :]).then_inc(pT_done, 1)
                    if pair == 5:
                        back(0)
                back(1)
                dve.reg_add(u_reg, u_reg, U)

            def done(ch):
                dve.reg_add(step_reg, step_reg, ch.n)

            with dve.Fori(1, B + 1) as turn:
                b = turn - 1
                ln, u = dve.snap(ln_reg), dve.snap(u_reg)
                ch = Chain(dve, dve_step, dve.snap(step_reg))
                dve.wait_ge(inT_full, u)
                for ins in norm(ch, lambda t: k.x[:, bass.ds(b * TT + t, 1), :].rearrange("p o d -> p (o d)"), lat, ln):
                    ch.link(ins)
                for ins in norm(ch, lambda t: lat[:, t, :], lat, ln + 1):
                    last = ins
                last.then_inc(lat_ready, 1)
                ch.link(dve.memset(top[:, :, :], FAR))
                dve.reg_add(ln_reg, ln_reg, 2)
                chunk_body(ch, u, no_bias[:, :])
                done(ch)

                def step(c):
                    u, uc, ln = dve.snap(u_reg), dve.snap(uc_reg), dve.snap(ln_reg)
                    ch = Chain(dve, dve_step, dve.snap(step_reg))
                    dve.wait_ge(chunk_mask_in, uc + U)
                    ch.link(dve.tensor_scalar(bias[:, :], chunk_mask[:, :], -1.0, -FAR, ALU.add, ALU.mult))
                    dve.wait_ge(ctx_in, uc + U)
                    dve.wait_ge(inT_full, u)
                    for ins in norm(ch, lambda t: ctx_raw[:, t, :], xn, ln):
                        ins.then_inc(xn_ready, U // KT)
                    dve.reg_add(uc_reg, uc_reg, U)
                    dve.reg_add(ln_reg, ln_reg, 1)
                    chunk_body(ch, u, bias[:, :])
                    done(ch)
                chunks(dve, b, step)
                u = dve.snap(u_reg)
                ch = Chain(dve, dve_step, dve.snap(step_reg))
                dve.wait_ge(total_done, u)
                dve.wait_ge(back_done, u)
                ch.link(dve.reciprocal(rtotal[:, :, :], total[:, :, :]))
                for t in range(TT):
                    by_head = o[:, t, :].rearrange("p (h d) -> p h d", d=DH)
                    dve.tensor_tensor(by_head, by_head, rtotal[:, t, :].unsqueeze(2).broadcast_to([P, H, DH]), ALU.mult)\
                        .then_inc(fin_ready, 1)
                for t in range(TT):
                    dve.wait_ge(x_full, turn * 2 + t + 1)
                    xt = k.x[:, bass.ds(b * TT + t, 1), :].rearrange("p o d -> p (o d)")
                    dve.tensor_tensor(xt, ps[:, OUT + t, 0:D], xt, ALU.add).then_inc(x_done, 1)
                done(ch)

        @block.gpsimd
        def _(pool):
            u_reg, ln_reg, step_reg = (pool.alloc_register(f"pool_{n}") for n in ("u", "ln", "step"))
            for r, first in ((u_reg, U), (ln_reg, 0)):
                pool.reg_mov(r, first)
            chain = Chain(pool, pool_step)
            pool.memset(rows[:, :], 0.0).then_inc(rows_zero, 1)
            pool.memset(qT[:, :, :], 0.0).then_inc(q_zero, 1)
            chain.link(pool.memset(half[:, :], -0.5))
            pool.reg_mov(step_reg, chain.n)
            pool.wait_ge(words_in, 16)

            def root(ln):
                pool.wait_ge(ln_var, ln + 1)
                pool.tensor_tensor(rstd[:, :], var[:, :], half[:, :], ALU.pow).then_inc(ln_rstd, 1)

            def chunk_body(ch, u):
                pool.wait_ge(back_done, u)
                for t in range(TT):
                    pool.wait_ge(alpha_done, u + 8 * (t + 1))
                    by_head = o[:, t, :].rearrange("p (h d) -> p h d", d=DH)
                    pool.tensor_tensor(by_head, by_head, alpha[:, t, :].unsqueeze(2).broadcast_to([P, H, DH]), ALU.mult)\
                        .then_inc(o_scaled, U // TT)
                    ch.link(pool.tensor_tensor(total[:, t, :], total[:, t, :], alpha[:, t, :], ALU.mult))
                    pool.wait_ge(p_ready, u + 8 * (t + 1))
                    pool.tensor_tensor(total[:, t, :], total[:, t, :], chunk_sum[:, t, :], ALU.add)\
                        .then_inc(total_done, U // TT)
                pool.reg_add(u_reg, u_reg, U)

            with pool.Fori(1, B + 1) as turn:
                b = turn - 1
                ch = Chain(pool, pool_step, pool.snap(step_reg))
                ln, u = pool.snap(ln_reg), pool.snap(u_reg)
                root(ln)
                root(ln + 1)
                pool.reg_add(ln_reg, ln_reg, 2)
                pool.wait_ge(fin_full, turn * 4)
                pool.wait_ge(fin_ready, turn * 2)
                hold(pool, pool_held)
                pool.memset(total[:, :, :], 0.0)
                ch.link(pool.memset(o[:, :, :], 0.0))
                chunk_body(ch, u)
                pool.reg_add(step_reg, step_reg, ch.n)

                def step(c):
                    ch = Chain(pool, pool_step, pool.snap(step_reg))
                    u, ln = pool.snap(u_reg), pool.snap(ln_reg)
                    root(ln)
                    pool.reg_add(ln_reg, ln_reg, 1)
                    pool.wait_ge(total_done, u)
                    chunk_body(ch, u)
                    pool.reg_add(step_reg, step_reg, ch.n)
                chunks(pool, b, step)


N_ROW_DMAS = 7 + KINDS


def linear_attention(k):
    nc, io = k.nc, k.io
    U = 16
    C = D
    with ExitStack() as ctx:
        sb = lambda name, shape, dt=F32: k.sb(name, shape, dt, ctx)
        wq = sb("lin_wq", [P, KD, C])
        wkv = sb("lin_wkv", [P, KD, 2, 2, C])
        wo = sb("lin_wo", [P, KD, C])
        bkv = sb("lin_bkv", [P, 2, 2, C])
        bo = sb("lin_bo", [P, C])
        xn = sb("lin_xn", [P, TT, C])
        xnT = sb("lin_xnT", [P, KD, T])
        qT = sb("lin_qT", [P, KD, T])
        kv = sb("lin_kv", [P, 2, TT, 2, C])
        state0 = sb("lin_state0", [P, KD, P])
        state = sb("lin_state", [P, KD, P])
        yn = sb("lin_yn", [P, TT, C])
        ynT = sb("lin_ynT", [P, KD, T])
        stats = sb("lin_stats", [P, TT, 6])
        mv = sb("lin_mv", [P, TT, 2])
        var = sb("lin_var", [P, TT])
        rstd = sb("lin_rstd", [P, TT])
        half = sb("lin_half", [P, TT])
        ps = k.banks("ps_lin", ctx)
        TURN, QUERY, KV, STATE, OUT, X = 0, 1, 2, 4, 5, 6

        sem = k.sem
        wq_in, wkv_in, wo_in, bias_in = sem("lin_wq_in"), sem("lin_wkv_in"), sem("lin_wo_in"), sem("lin_bias_in")
        xn_ready, xnT_full, xnT_done = sem("lin_xn_ready"), sem("lin_xnT_full"), sem("lin_xnT_done")
        q_full, q_done, kv_full, kv_done = sem("lin_q_full"), sem("lin_q_done"), sem("lin_kv_full"), sem("lin_kv_done")
        kv_read = sem("lin_kv_read")
        st_full, st_done, out_full = sem("lin_state_full"), sem("lin_state_done"), sem("lin_out_full")
        yn_ready, ynT_full, ynT_done = sem("lin_yn_ready"), sem("lin_ynT_full"), sem("lin_ynT_done")
        x_full, x_done = sem("lin_x_full"), sem("lin_x_done")
        ln_var, ln_rstd, dve_step, half_set, dve_held = sem("lin_ln_var"), sem("lin_ln_rstd"), sem("lin_dve_step"), sem("lin_half_set"), sem("lin_dve_held")

        block = ctx.enter_context(nc.Block())

        @block.sync
        def _(sp):
            begin_at(sp, U, (xn_ready, xnT_full, xnT_done, q_full, q_done, kv_full, kv_done, kv_read, st_full, st_done, out_full,
                             yn_ready, ynT_full, ynT_done, x_full, x_done))
            sp.dma_start(wq[:, :, :], io["attn_Wq"].rearrange("(k p) n -> p k n", p=P)).then_inc(wq_in, 16)
            for s in range(2):
                for n, name in enumerate(("k", "v")):
                    sp.dma_start(wkv[:, :, s, n, :], io[f"attn_W{name}"][s].rearrange("(k p) n -> p k n", p=P))\
                        .then_inc(wkv_in, 16)
                    sp.dma_start(bkv[:, s, n, :], io[f"attn_b{name}"][s:s + 1, :].broadcast_to([P, C])).then_inc(bias_in, 16)
            sp.dma_start(bo[:, :], io["attn_bo"].rearrange("(o n) -> o n", o=1).broadcast_to([P, C])).then_inc(bias_in, 16)
            sp.dma_start(wo[:, :, :], io["attn_Wo"].rearrange("(k p) n -> p k n", p=P)).then_inc(wo_in, 16)

        @block.tensor
        def _(pe):
            pe.wait_ge(wq_in, 16)
            pe.wait_ge(wkv_in, 64)
            pe.wait_ge(wo_in, 16)
            with pe.Fori(U, (B + 1) * U, U) as u:
                pe.wait_ge(xn_ready, u + U)
                pe.wait_ge(ynT_done, u)
                for kk in range(KD):
                    for t in range(TT):
                        ins = pe.transpose(ps[:, TURN, kk * T + t * P:kk * T + (t + 1) * P],
                                           xn[:, t, kk * P:(kk + 1) * P], k.ident)
                ins.then_inc(xnT_full, U)
                pe.wait_ge(xnT_done, u + U)
                pe.wait_ge(q_done, u)
                for m in range(KD):
                    for kk in range(KD):
                        ins = pe.matmul(ps[:, QUERY, m * T:(m + 1) * T], wq[:, kk, m * P:(m + 1) * P], xnT[:, kk, :],
                                        start=kk == 0, stop=kk == KD - 1)
                ins.then_inc(q_full, U)
                for s in range(2):
                    for t in range(TT):
                        j = s * TT + t
                        pe.wait_ge(kv_read, u + (4 * (j - 1) if j >= 2 else 0))
                        for kk in range(KD):
                            ins = pe.matmul(ps[:, KV + j % 2, :], xnT[:, kk, t * P:(t + 1) * P],
                                            wkv[:, kk, s, :, :].rearrange("p n c -> p (n c)"),
                                            start=kk == 0, stop=kk == KD - 1)
                        ins.then_inc(kv_full, 4)
                for s in range(2):
                    pe.wait_ge(kv_done, u + 8 * (s + 1))
                    for m in range(KD):
                        for t in range(TT):
                            ins = pe.matmul(ps[:, STATE, (s * KD + m) * P:(s * KD + m + 1) * P],
                                            kv[:, s, t, 0, m * P:(m + 1) * P], kv[:, s, t, 1, m * P:(m + 1) * P],
                                            start=t == 0, stop=t == TT - 1)
                ins.then_inc(st_full, U)
                pe.wait_ge(st_done, u + U)
                pe.wait_ge(q_done, u + U)
                for t in range(TT):
                    for m in range(KD):
                        ins = pe.matmul(ps[:, OUT, t * C + m * P:t * C + (m + 1) * P], qT[:, m, t * P:(t + 1) * P],
                                        state[:, m, :], start=True, stop=True)
                ins.then_inc(out_full, U)
                pe.wait_ge(yn_ready, u + U)
                for kk in range(KD):
                    for t in range(TT):
                        ins = pe.transpose(ps[:, TURN, kk * T + t * P:kk * T + (t + 1) * P],
                                           yn[:, t, kk * P:(kk + 1) * P], k.ident)
                ins.then_inc(ynT_full, U)
                pe.wait_ge(ynT_done, u + U)
                pe.wait_ge(x_done, u)
                for t in range(TT):
                    for kk in range(KD):
                        ins = pe.matmul(ps[:, X, t * C:(t + 1) * C], ynT[:, kk, t * P:(t + 1) * P], wo[:, kk, :],
                                        start=kk == 0, stop=kk == KD - 1)
                ins.then_inc(x_full, U)

        @block.scalar
        def _(act):
            with act.Fori(U, (B + 1) * U, U) as u:
                act.wait_ge(xnT_full, u + U)
                act.wait_ge(kv_full, u)
                act.wait_ge(q_done, u)
                act.activation(xnT[:, :, :], ps[:, TURN, :].rearrange("p (k t) -> p k t", k=KD), ACT.Copy).then_inc(xnT_done, U)
                act.wait_ge(ynT_full, u + U)
                for kk in range(KD):
                    ins = act.activation(ynT[:, kk, :], ps[:, TURN, kk * T:(kk + 1) * T], ACT.Identity,
                                         bias=k.cols[:, R_LB + kk:R_LB + kk + 1], scale=k.cols[:, R_LG + kk:R_LG + kk + 1])
                ins.then_inc(ynT_done, U)

        @block.vector
        def _(dve):
            STEPS = 9
            dve.wait_ge(bias_in, 80)
            with dve.Fori(0, B) as b:
                u = (b + 1) * U
                ch = Chain(dve, dve_step, b * STEPS)
                xt = lambda t: k.x[:, bass.ds(b * TT + t, 1), :].rearrange("p o d -> p (o d)")
                both = k.x[:, bass.ds(b * TT, TT), :]

                def norm(src, dst, n):
                    hold(dve, dve_held)
                    for t in range(TT):
                        ins = dve.bn_stats(stats[:, t, :], src(t))
                    ch.link(ins)
                    hold(dve, dve_held)
                    for t in range(TT):
                        ins = dve.bn_aggr(mv[:, t, :], stats[:, t, :])
                    ch.link(ins)
                    dve.tensor_scalar(var[:, :], mv[:, :, 1], EPS, None, ALU.add).then_inc(ln_var, 1)
                    dve.wait_ge(ln_rstd, b * 3 + n + 1)
                    for t in range(TT):
                        ins = dve.tensor_scalar(dst(t), src(t), mv[:, t, 0:1], rstd[:, t:t + 1], ALU.subtract, ALU.mult)
                    return ins

                dve.wait_ge(xnT_full, u)
                norm(xt, lambda t: xn[:, t, :], 0).then_inc(xn_ready, U)
                dve.wait_ge(xn_ready, u + U)
                dve.wait_ge(q_full, u + U)
                dve.wait_ge(xnT_done, u + U)
                dve.wait_ge(out_full, u)
                for m in range(KD):
                    ins = dve.scalar_tensor_tensor(out=qT[:, m, :], in0=ps[:, QUERY, m * T:(m + 1) * T],
                                                   scalar=k.cols[:, R_BQ + m:R_BQ + m + 1], in1=xnT[:, m, :],
                                                   op0=ALU.add, op1=ALU.add)
                ins.then_inc(q_done, U)
                dve.wait_ge(st_full, u)
                for s in range(2):
                    for t in range(TT):
                        j = s * TT + t
                        dve.wait_ge(kv_full, u + 4 * (j + 1))
                        dve.tensor_tensor(kv[:, s, t, :, :].rearrange("p n c -> p (n c)"), ps[:, KV + j % 2, :],
                                          bkv[:, s, :, :].rearrange("p n c -> p (n c)"), ALU.add).then_inc(kv_read, 4)
                        dve.wait_ge(kv_read, u + 4 * (j + 1))
                        dve.tensor_tensor(kv[:, s, t, :, :], kv[:, s, t, :, :],
                                          xn[:, t, :].unsqueeze(1).broadcast_to([P, 2, C]), ALU.add).then_inc(kv_done, 4)
                dve.wait_ge(st_full, u + U)
                block_mask = k.const[:, C_BLOCK:C_BLOCK + P].unsqueeze(1).broadcast_to([P, KD, P])
                ch.link(dve.tensor_tensor(state0[:, :, :], ps[:, STATE, 0:KD * P].rearrange("p (m e) -> p m e", m=KD),
                                          block_mask, ALU.mult))
                dve.tensor_tensor(state[:, :, :], ps[:, STATE, KD * P:2 * KD * P].rearrange("p (m e) -> p m e", m=KD),
                                  state0[:, :, :], ALU.mult).then_inc(st_done, U)
                dve.wait_ge(out_full, u + U)
                norm(lambda t: ps[:, OUT, t * C:(t + 1) * C], lambda t: yn[:, t, :], 1).then_inc(yn_ready, U)
                ch.link(dve.tensor_tensor(both, both, bo[:, :].unsqueeze(1).broadcast_to([P, TT, C]), ALU.add))
                dve.wait_ge(x_full, u + U)
                dve.tensor_tensor(both, ps[:, X, :].rearrange("p (t c) -> p t c", t=TT), both, ALU.add).then_inc(x_done, U)
                dve.wait_ge(x_done, u + U)
                ch.link(norm(xt, lambda t: k.y[:, bass.ds(b * TT + t, 1), :].rearrange("p o d -> p (o d)"), 2))
                assert ch.n == STEPS

        @block.gpsimd
        def _(pool):
            pool.memset(half[:, :], -0.5).then_inc(half_set, 1)
            pool.wait_ge(half_set, 1)
            with pool.Fori(0, B * 3) as n:
                pool.wait_ge(ln_var, n + 1)
                pool.tensor_tensor(rstd[:, :], var[:, :], half[:, :], ALU.pow).then_inc(ln_rstd, 1)




def local_layers(k):
    nc, io = k.nc, k.io
    U = 16
    LAYER = B * U
    SLOTS = 12
    with ExitStack() as ctx:
        sb = lambda name, shape, dt=F32: k.sb(name, shape, dt, ctx)
        wqkv = sb("wqkv", [P, KD, 3 * INNER])
        wo = sb("wo", [P, PAIRS, D])
        w1 = sb("w1", [P, KD, 2 * FF])
        w2 = sb("w2", [P, FM, D])
        b2 = sb("b2", [P, LAYERS, D])
        head_scale = sb("head_scale", [P, LAYERS, 2, DH])
        cos = sb("cos", [P, TT, 2, DH])
        sin = sb("sin", [P, TT, 2, DH])
        vec = sb("vec", [P, KINDS])
        xT = sb("xT", [P, KD, T])
        qk = sb("qk", [P, TT, 2 * INNER])
        v = sb("v_loc", [P, 2, TT, INNER])
        work = sb("work", [P, 2, 2 * INNER])
        square = work[:, 0, :]
        twist = work[:, 1, :]
        uT = work[:, :, 0:FM * T].rearrange("p b (m t) -> p b m t", m=FM)
        norm2 = sb("norm2", [P, 2 * H])
        norm2_floor = sb("norm2_floor", [P, 2 * H])
        half = sb("half_loc", [P, 2 * H])
        rnorm = sb("rnorm", [P, 2, TT, 2 * H])
        qT = sb("qT_loc", [P, PAIRS, T])
        kT = sb("kT_loc", [P, PAIRS, 2, T])
        prob0 = sb("prob0", [P, H, P])
        prob1 = sb("prob1", [P, H, T])
        top = sb("top_loc", [P, TT, H])
        total = sb("total_loc", [P, TT, H])
        rtotal = sb("rtotal_loc", [P, TT, H])
        pT = sb("pT", [P, 2, 2 * T + 2 * P])
        oT = sb("oT_loc", [P, PAIRS, T])
        late = sb("late", [P, B * TT, P])
        xn = sb("xn_loc", [P, TT, D])
        xnT = sb("xnT_loc", [P, 2, KD, T])
        stats = sb("stats_loc", [P, TT, 2, 6])
        mv = sb("mv_loc", [P, TT, 2])
        var = sb("var_loc", [P, TT])
        rstd = sb("rstd_loc", [P, TT])
        gate = sb("gate", [P, 2, T])
        ps = k.banks("ps_loc", ctx)
        PROJ, PAIR, SCORE, TURN = 0, 2, 4, 6

        sem = k.sem
        wqkv_in, wo_in, w1_in, w2_in = sem("wqkv_in"), sem("wo_in"), sem("w1_in"), sem("w2_in")
        b2_in, scale_in, zeros_set = sem("b2_in"), sem("scale_in"), sem("zeros_set")
        tables_done, vec_done = sem("tables_done"), sem("vec_done")
        xT_full, xT_done, qkv_full, qkv_done = sem("xT_full"), sem("xT_done"), sem("qkv_full"), sem("qkv_done")
        square_done, norm2_done, floor_done, rnorm_done = sem("square_done"), sem("norm2_done"), sem("floor_done"), sem("rnorm_done")
        twist_done, cos_done, sum_done, rope_done = sem("twist_done"), sem("cos_done"), sem("sum_done"), sem("rope_done")
        qk_full, qk_done = sem("qk_full"), sem("qk_done")
        s_full, s_read, exp_done = sem("loc_s_full"), sem("loc_s_read"), sem("exp_done")
        rtotal_done, p_done, dve_held = sem("rtotal_done"), sem("p_done"), sem("loc_dve_held")
        pT_full, pT_done, o_full, o_done = sem("loc_pT_full"), sem("loc_pT_done"), sem("loc_o_full"), sem("loc_o_done")
        y_full, y_mid, y_out = sem("y_full"), sem("y_mid"), sem("y_out")
        late_in, edge_in = [sem(f"late_in{b}") for b in range(B)], [sem(f"edge_in{b}") for b in range(B)]
        bn_done, ln_stats, ln_var, ln_rstd, xn_done = sem("bn_done"), sem("loc_ln_stats"), sem("loc_ln_var"), sem("loc_ln_rstd"), sem("xn_done")
        xnT_full, xnT_done = sem("xnT_full"), sem("xnT_done")
        f_full, gate_done, u_done = sem("f_full"), sem("gate_done"), sem("u_done")
        f2_full, b2_done, x_sum = sem("f2_full"), sem("b2_done"), sem("x_sum")

        def after(n, last):
            return n + 1 if n < last else U

        def weights(sp, i, which):
            if which == "qkv":
                src = io["ffn_Wqkv"].rearrange("i (k p) n -> i p k n", p=P)
                for kk in range(KD):
                    for j in range(2):
                        cut = slice(j * 3 * INNER // 2, (j + 1) * 3 * INNER // 2)
                        sp.dma_start(wqkv[:, kk, cut], src[bass.ds(i, 1), :, kk, cut].rearrange("o p n -> (o p) n"))\
                            .then_inc(wqkv_in, 16)
            elif which == "wo":
                src = io["ffn_Wo"].rearrange("i (k p) n -> i p k n", p=P)
                for j in range(4):
                    sp.dma_start(wo[:, 2 * j:2 * j + 2, :], src[bass.ds(i, 1), :, 2 * j:2 * j + 2, :].rearrange("o p k n -> (o p) k n"))\
                        .then_inc(wo_in, 16)
            elif which == "w1":
                src = io["ffn_W1"].rearrange("i (k p) n -> i p k n", p=P)
                for kk in range(KD):
                    for j in range(2):
                        sp.dma_start(w1[:, kk, j * FF:(j + 1) * FF], src[bass.ds(i, 1), :, kk, j * FF:(j + 1) * FF].rearrange("o p n -> (o p) n"))\
                            .then_inc(w1_in, 16)
            else:
                for m0, m1 in ((0, 2), (2, 4), (4, 5), (5, 6)):
                    src = io["ffn_W2"][bass.ds(i, 1), FAT[m0]:FAT[m1 - 1] + FWIDE[m1 - 1], :]
                    sp.dma_start(w2[0:FWIDE[m0], m0:m1, :], src.rearrange("o (m p) n -> (o p) m n", p=FWIDE[m0])).then_inc(w2_in, 16)

        block = ctx.enter_context(nc.Block())

        @block.sync
        def _(sp):
            begin_at(sp, LAYER, (vec_done, tables_done, xT_full, xT_done, qkv_full, qkv_done, square_done, norm2_done, floor_done,
                                 rnorm_done, twist_done, cos_done, sum_done, rope_done, qk_full, qk_done, s_full, s_read, exp_done,
                                 rtotal_done, p_done, pT_full, pT_done, o_full, o_done, y_full, y_mid, bn_done, ln_stats,
                                 ln_var, ln_rstd, xn_done, xnT_full, xnT_done, f_full, gate_done, u_done, f2_full, b2_done,
                                 wqkv_in, wo_in, w1_in, w2_in))
            begin_at(sp, 2 * LAYER, (y_out,))
            sp.wait_ge(zeros_set, 1)
            for which in ("qkv", "wo", "w1", "w2"):
                weights(sp, 0, which)
            for n, name in enumerate(("q", "k")):
                sp.dma_start(head_scale[:, :, n, :], io[f"ffn_{name}_scale"].rearrange("(o i) d -> o i d", o=1).broadcast_to([P, LAYERS, DH]))\
                    .then_inc(scale_in, 16)
            sp.dma_start(b2[:, :, :], io["ffn_b2"].rearrange("(o i) d -> o i d", o=1).broadcast_to([P, LAYERS, D])).then_inc(b2_in, 16)

            def shift(L, b):
                sp.wait_ge(y_mid, L + U * (b + 1))
                sp.dma_start(late[1:P, b * TT:(b + 1) * TT, :], k.y[0:P - 1, b * TT:(b + 1) * TT, P:D]).then_inc(late_in[b], 16)
                sp.dma_start(late[0:1, b * TT + 1, :], k.y[P - 1:P, b * TT, P:D]).then_inc(edge_in[b], 16)

            with sp.Fori(0, LAYERS - 1) as i:
                L = sp.snap(i * LAYER + LAYER)
                shift(L, 0)
                shift(L, 1)
                sp.wait_ge(qkv_full, L + LAYER)
                weights(sp, i + 1, "qkv")
                shift(L, 2)
                shift(L, 3)
                weights(sp, i + 1, "wo")
                sp.wait_ge(f_full, L + LAYER)
                weights(sp, i + 1, "w1")
                sp.wait_ge(f2_full, L + LAYER)
                weights(sp, i + 1, "w2")
            for b in range(B):
                shift(LAYERS * LAYER, b)

        @block.tensor
        def _(pe):
            def turn_x(L, b):
                pe.wait_ge(y_out, L + U * (b + 1))
                pe.wait_ge(qkv_done, L + U * b)
                pe.wait_ge(xnT_done, L)
                for kk in range(KD):
                    for t in range(TT):
                        ins = pe.transpose(ps[:, PROJ, kk * T + t * P:kk * T + (t + 1) * P],
                                           k.y[:, b * TT + t, kk * P:(kk + 1) * P], k.ident)
                ins.then_inc(xT_full, U)

            def project(L, b):
                if b == 0:
                    pe.wait_ge(wqkv_in, L + LAYER)
                pe.wait_ge(xT_done, L + U * (b + 1))
                for j in range(SLOTS):
                    t, part = divmod(j, 4) if j < 8 else divmod(j - 8, 2)
                    col = part * 512 if j < 8 else 2 * INNER + part * 512
                    if j >= 2:
                        pe.wait_ge(qkv_done, L + U * b + j - 1)
                    for kk in range(KD):
                        ins = pe.matmul(ps[:, PROJ + j % 2, :], xT[:, kk, t * P:(t + 1) * P], wqkv[:, kk, col:col + 512],
                                        start=kk == 0, stop=kk == KD - 1)
                    ins.then_inc(qkv_full, 1 if j < SLOTS - 1 else U - SLOTS + 1)

            def turn_qk(L, b):
                pe.wait_ge(rope_done, L + U * (b + 1))
                pe.wait_ge(o_done, L + U * b)
                pe.wait_ge(u_done, L)
                for g in range(8):
                    s, two = divmod(g, 4)
                    pe.wait_ge(qk_done, L + U * b + (2 * (g - 1) if g >= 2 else 0))
                    for i in range(2):
                        for t in range(TT):
                            col = s * INNER + (2 * two + i) * P
                            ins = pe.transpose(ps[:, PAIR + g % 2, i * T + t * P:i * T + (t + 1) * P],
                                               qk[:, t, col:col + P], k.ident)
                    ins.then_inc(qk_full, 2)

            def scores(L, b):
                pe.wait_ge(qk_done, L + U * (b + 1))
                pe.wait_ge(y_mid, L + U * b)
                pe.wait_ge(y_out, L + LAYER)
                for pair in range(PAIRS):
                    for t in range(TT):
                        s = pair * TT + t
                        pe.wait_ge(s_read, L + U * b + (s - 1 if s >= 2 else 0))
                        k0, k1 = (0, P) if t == 0 else (WINDOW, T)
                        pe.matmul(ps[:, SCORE + t, 0:2 * (k1 - k0)], qT[:, pair, t * P:(t + 1) * P], kT[:, pair, :, k0:k1],
                                  start=True, stop=True).then_inc(s_full, 1)

            def weigh(L, b):
                def out(pair):
                    pe.wait_ge(pT_done, L + U * b + 2 * pair + 2)
                    pe.wait_ge(o_done, L + U * b + (2 * (pair - 1) if pair >= 2 else 0))
                    for i in range(2):
                        col = (2 * pair + i) * DH
                        pe.matmul(ps[i * DH:(i + 1) * DH, PAIR + pair % 2, 0:T], v[:, b % 2, 0, col:col + DH],
                                  pT[:, pair % 2, i * T:(i + 1) * T], start=True, stop=False)
                    for i in range(2):
                        col = (2 * pair + i) * DH
                        ins = pe.matmul(ps[i * DH:(i + 1) * DH, PAIR + pair % 2, P:T], v[:, b % 2, 1, col:col + DH],
                                        pT[:, pair % 2, 2 * T + i * P:2 * T + (i + 1) * P], start=False, stop=True)
                    ins.then_inc(o_full, 2)

                pe.wait_ge(qk_done, L + U * (b + 1))
                pe.wait_ge(u_done, L + (U if b == B - 1 else 0))
                pe.wait_ge(qkv_done, L + U * (b + 1))
                for pair in range(PAIRS):
                    pe.wait_ge(p_done, L + U * b + 2 * pair + 2)
                    pe.wait_ge(pT_done, L + U * b + max(2 * pair - 1, 0))
                    for i in range(2):
                        h = 2 * pair + i
                        pe.transpose(ps[:, TURN, i * T:i * T + P], prob0[:, h, :], k.ident)
                        ins = pe.transpose(ps[:, TURN, i * T + P:(i + 1) * T], prob1[:, h, 0:P], k.ident)
                    ins.then_inc(pT_full, 1)
                    pe.wait_ge(pT_done, L + U * b + 2 * pair)
                    for i in range(2):
                        ins = pe.transpose(ps[:, TURN + 1, i * P:(i + 1) * P], prob1[:, 2 * pair + i, P:T], k.ident)
                    ins.then_inc(pT_full, 1)
                    if pair:
                        out(pair - 1)
                out(PAIRS - 1)

            def project_out(L, b):
                if b == 0:
                    pe.wait_ge(wo_in, L + LAYER)
                pe.wait_ge(o_done, L + U * (b + 1))
                pe.wait_ge(s_read, L + U * (b + 1))
                for t in range(TT):
                    for pair in range(PAIRS):
                        ins = pe.matmul(ps[:, SCORE, t * D:(t + 1) * D], oT[:, pair, t * P:(t + 1) * P], wo[:, pair, :],
                                        start=pair == 0, stop=pair == PAIRS - 1)
                ins.then_inc(y_full, U)

            def turn_xn(L, b):
                pe.wait_ge(xn_done, L + U * (b + 1))
                pe.wait_ge(qkv_done, L + LAYER)
                if b >= 2:
                    pe.wait_ge(xnT_done, L + U * (b - 1))
                for kk in range(KD):
                    for t in range(TT):
                        ins = pe.transpose(ps[:, PROJ + b % 2, kk * T + t * P:kk * T + (t + 1) * P],
                                           xn[:, t, kk * P:(kk + 1) * P], k.ident)
                ins.then_inc(xnT_full, U)

            def widen(L, b):
                if b == 0:
                    pe.wait_ge(w1_in, L + LAYER)
                    pe.wait_ge(qk_done, L + LAYER)
                else:
                    pe.wait_ge(o_done, L + LAYER)
                pe.wait_ge(xnT_done, L + U * (b + 1))
                for m in range(FM):
                    n = FWIDE[m]
                    pe.wait_ge(u_done, L + U * b + (m - 1 if m >= 2 else 0))
                    for part in range(2):
                        for kk in range(KD):
                            ins = pe.matmul(ps[0:n, PAIR + m % 2, part * T:(part + 1) * T],
                                            w1[:, kk, part * FF + FAT[m]:part * FF + FAT[m] + n], xnT[:, b % 2, kk, :],
                                            start=kk == 0, stop=kk == KD - 1)
                    ins.then_inc(f_full, 1 if m < FM - 1 else U - FM + 1)

            def narrow(L, b):
                if b == 0:
                    pe.wait_ge(w2_in, L + LAYER)
                pe.wait_ge(u_done, L + U * (b + 1))
                pe.wait_ge(y_mid, L + LAYER)
                if b >= 2:
                    pe.wait_ge(y_out, L + LAYER + U * (b - 1))
                for t in range(TT):
                    for m in range(FM):
                        ins = pe.matmul(ps[:, SCORE + b % 2, t * D:(t + 1) * D], uT[0:FWIDE[m], b % 2, m, t * P:(t + 1) * P], w2[0:FWIDE[m], m, :],
                                        start=m == 0, stop=m == FM - 1)
                ins.then_inc(f2_full, U)

            with pe.Fori(0, LAYERS) as i:
                L = pe.snap(i * LAYER + LAYER)
                turn_x(L, 0)
                project(L, 0)
                for b in range(B):
                    if b:
                        weigh(L, b - 1)
                        project_out(L, b - 1)
                    turn_qk(L, b)
                    if b < B - 1:
                        turn_x(L, b + 1)
                    else:
                        turn_xn(L, 0)
                    scores(L, b)
                    if b < B - 1:
                        project(L, b + 1)
                widen(L, 0)
                weigh(L, B - 1)
                project_out(L, B - 1)
                for b in range(B):
                    if b < B - 1:
                        turn_xn(L, b + 1)
                        widen(L, b + 1)
                    narrow(L, b)

        @block.scalar
        def _(act):
            def x_out(L, b):
                act.wait_ge(qkv_full, L + U * b)
                act.wait_ge(xT_full, L + U * (b + 1))
                act.activation(xT[:, 0, :], ps[:, PROJ, 0:T], ACT.Copy)
                act.activation(xT[:, 1, 1:T], ps[:, PROJ, T:2 * T - 1], ACT.Copy).then_inc(xT_done, U)

            def qkv_out(L, b, j):
                if j == 0:
                    act.wait_ge(f2_full, L)
                    act.wait_ge(qk_full, L + U * b)
                    act.wait_ge(o_full, L + U * max(b - 1, 0))
                act.wait_ge(qkv_full, L + U * b + after(j, SLOTS - 1))
                t, part = divmod(j, 4) if j < 8 else divmod(j - 8, 2)
                dst = qk[:, t, part * 512:(part + 1) * 512] if j < 8 else v[:, b % 2, t, part * 512:(part + 1) * 512]
                act.activation(dst, ps[:, PROJ + j % 2, :], ACT.Copy).then_inc(qkv_done, 1 if j < SLOTS - 1 else U - SLOTS + 1)
                if j in (3, 7):
                    act.wait_ge(qkv_done, L + U * b + j + 1)
                    act.wait_ge(norm2_done, L + U * b + 8 * t)
                    act.activation(square, qk[:, t, :], ACT.Square).then_inc(square_done, 8)

            def qk_out(L, b):
                act.wait_ge(s_full, L + U * b)
                for g in range(8):
                    s, two = divmod(g, 4)
                    act.wait_ge(qk_full, L + U * b + 2 * (g + 1))
                    bank = ps[:, PAIR + g % 2, :].rearrange("p (i t) -> p i t", i=2)
                    if s == 0:
                        ins = act.activation(qT[:, 2 * two:2 * two + 2, :], bank, ACT.Copy)
                    else:
                        for h in range(2):
                            at = slice(h * DH, (h + 1) * DH)
                            ins = act.activation(kT[at, 2 * two:2 * two + 2, h, :], bank[at], ACT.Copy)
                    ins.then_inc(qk_done, 2)

            def exps(L, b, s):
                pair, t = divmod(s, TT)
                act.wait_ge(s_read, L + U * b + s + 1)
                for h in (2 * pair, 2 * pair + 1):
                    pr = prob0[:, h, :] if t == 0 else prob1[:, h, WINDOW:T]
                    ins = act.activation(pr, pr, ACT.Exp, bias=top[:, t, h:h + 1], scale=-1.0, accum_out=total[:, t, h:h + 1])
                ins.then_inc(exp_done, 1)

            def weigh_out(L, b):
                def o_out(pair):
                    act.wait_ge(o_full, L + U * b + 2 * (pair + 1))
                    act.activation(oT[:, pair, :], ps[:, PAIR + pair % 2, 0:T], ACT.Copy).then_inc(o_done, 2)

                act.wait_ge(y_full, L + U * b)
                for pair in range(PAIRS):
                    act.wait_ge(o_full, L + U * b + (2 * (pair - 1) if pair >= 2 else 0))
                    act.wait_ge(pT_full, L + U * b + 2 * pair + 1)
                    act.activation(pT[:, pair % 2, 0:2 * T], ps[:, TURN, :], ACT.Copy).then_inc(pT_done, 1)
                    act.wait_ge(pT_full, L + U * b + 2 * pair + 2)
                    act.activation(pT[:, pair % 2, 2 * T:], ps[:, TURN + 1, 0:2 * P], ACT.Copy).then_inc(pT_done, 1)
                    if pair:
                        o_out(pair - 1)
                o_out(PAIRS - 1)

            def widen_in(L, b):
                if b == 0:
                    act.wait_ge(vec_done, L + LAYER)
                act.wait_ge(f_full, L + U * max(b - 1, 0))
                act.wait_ge(xnT_full, L + U * (b + 1))
                for kk in range(KD):
                    ins = act.activation(xnT[:, b % 2, kk, :], ps[:, PROJ + b % 2, kk * T:(kk + 1) * T], ACT.Identity,
                                         bias=vec[:, V_FB + kk:V_FB + kk + 1], scale=vec[:, V_FG + kk:V_FG + kk + 1])
                ins.then_inc(xnT_done, U)

            def gates(L, b):
                for m in range(FM):
                    n = FWIDE[m]
                    act.wait_ge(f_full, L + U * b + after(m, FM - 1))
                    act.activation(gate[0:n, m % 2, :], ps[0:n, PAIR + m % 2, T:2 * T], ACT.Gelu,
                                   bias=vec[0:n, V_B1G + m:V_B1G + m + 1]).then_inc(gate_done, 1 if m < FM - 1 else U - FM + 1)

            EARLY = 11
            act.wait_ge(zeros_set, 1)
            with act.Fori(0, LAYERS) as i:
                L = act.snap(i * LAYER + LAYER)
                x_out(L, 0)
                for j in range(SLOTS):
                    qkv_out(L, 0, j)
                for b in range(B):
                    if b:
                        weigh_out(L, b - 1)
                    qk_out(L, b)
                    if b < B - 1:
                        x_out(L, b + 1)
                    else:
                        widen_in(L, 0)
                    for s in range(U):
                        exps(L, b, s)
                        if b < B - 1 and s >= EARLY - 1:
                            qkv_out(L, b + 1, s - EARLY + 1)
                    if b < B - 1:
                        for j in range(U - EARLY + 1, SLOTS):
                            qkv_out(L, b + 1, j)
                gates(L, 0)
                weigh_out(L, B - 1)
                for b in range(1, B):
                    widen_in(L, b)
                    gates(L, b)

        @block.vector
        def _(dve):
            def rotate(L, b):
                for t in range(TT):
                    at = L + U * b + 8 * t
                    dve.wait_ge(square_done, at + 8)
                    dve.wait_ge(rnorm_done, at)
                    dve.tensor_reduce(norm2[:, :], square.rearrange("p (h d) -> p h d", d=DH), AX.X, ALU.add)\
                        .then_inc(norm2_done, 8)
                    dve.wait_ge(sum_done, at)
                    by_head = qk[:, t, :].rearrange("p (s h d) -> p s h d", s=2, d=DH)
                    to_head = twist.rearrange("p (s h d) -> p s h d", s=2, d=DH)
                    lo, hi = slice(0, DH // 2), slice(DH // 2, DH)
                    for dst, src in ((lo, hi), (hi, lo)):
                        ins = dve.tensor_tensor(to_head[:, :, :, dst], by_head[:, :, :, src],
                                                sin[:, t, :, dst].unsqueeze(2).broadcast_to([P, 2, H, DH // 2]), ALU.mult)
                    ins.then_inc(twist_done, 8)
                    dve.wait_ge(norm2_done, at + 8)
                    dve.tensor_scalar(norm2_floor[:, :], norm2[:, :], 1e-24, None, ALU.max).then_inc(floor_done, 8)
                    dve.wait_ge(twist_done, at + 8)
                    dve.tensor_tensor(by_head, by_head, cos[:, t, :, :].unsqueeze(2).broadcast_to([P, 2, H, DH]), ALU.mult)\
                        .then_inc(cos_done, 8)

            def softmax(L, b):
                def share(s):
                    if s < U:
                        pair, t = divmod(s, TT)
                        h = 2 * pair
                        dve.wait_ge(exp_done, L + U * b + s + 1)
                        dve.reciprocal(rtotal[:, t, h:h + 2], total[:, t, h:h + 2]).then_inc(rtotal_done, 1)
                    if s:
                        pair, t = divmod(s - 1, TT)
                        h = 2 * pair
                        dve.wait_ge(rtotal_done, L + U * b + s)
                        for n in range(2):
                            pr = prob0[:, h + n, :] if t == 0 else prob1[:, h + n, WINDOW:T]
                            ins = dve.tensor_scalar(pr, pr, rtotal[:, t, h + n:h + n + 1], None, ALU.mult)
                        ins.then_inc(p_done, 1)

                LAG = 3
                dve.wait_ge(rnorm_done, L + U * (b + 1))
                dve.wait_ge(pT_full, L + U * b)
                for s in range(U):
                    pair, t = divmod(s, TT)
                    n = P if t == 0 else T - WINDOW
                    band = k.const[:, C_BAND0:C_BAND0 + n] if t == 0 else k.const[:, C_BAND1:C_BAND1 + n]
                    dve.wait_ge(s_full, L + U * b + s + 1)
                    hold(dve, dve_held)
                    for e in range(2):
                        h = 2 * pair + e
                        ins = dve.tensor_tensor_reduce(
                            out=prob0[:, h, :] if t == 0 else prob1[:, h, WINDOW:T],
                            in0=ps[:, SCORE + t, e * n:(e + 1) * n], in1=band, scale=rnorm[:, b % 2, t, h:h + 1],
                            scalar=FAR, op0=ALU.add, op1=ALU.min, accum_out=top[:, t, h:h + 1])
                    ins.then_inc(s_read, 1)
                    if s >= LAG:
                        share(s - LAG)
                for s in range(U - LAG, U + 1):
                    share(s)

            def add_attention(L, b):
                dve.wait_ge(y_full, L + U * (b + 1))
                both = k.y[:, b * TT:(b + 1) * TT, :]
                dve.tensor_tensor(both, ps[:, SCORE, :].rearrange("p (t c) -> p t c", t=TT), both, ALU.add).then_inc(y_mid, U)

            def norm(L, shifts, b):
                dve.wait_ge(y_mid, L + U * (b + 1))
                dve.wait_ge(late_in[b], shifts)
                dve.wait_ge(edge_in[b], shifts)
                dve.wait_ge(xnT_full, L + U * b)
                halves = lambda t: (k.y[:, b * TT + t, 0:P], late[:, b * TT + t, :])
                for t in range(TT):
                    for n, part in enumerate(halves(t)):
                        ins = dve.bn_stats(stats[:, t, n, :], part)
                ins.then_inc(bn_done, U)
                dve.wait_ge(bn_done, L + U * (b + 1))
                hold(dve, dve_held)
                for t in range(TT):
                    ins = dve.bn_aggr(mv[:, t, :], stats[:, t, :, :].rearrange("p n s -> p (n s)"))
                ins.then_inc(ln_stats, U)
                dve.wait_ge(ln_stats, L + U * (b + 1))
                dve.tensor_scalar(var[:, :], mv[:, :, 1], EPS, None, ALU.add).then_inc(ln_var, U)
                dve.wait_ge(ln_rstd, L + U * (b + 1))
                for t in range(TT):
                    for n, part in enumerate(halves(t)):
                        ins = dve.tensor_scalar(xn[:, t, n * P:(n + 1) * P], part, mv[:, t, 0:1], rstd[:, t:t + 1],
                                                ALU.subtract, ALU.mult)
                ins.then_inc(xn_done, U)

            def gated(L, b):
                dve.wait_ge(sum_done, L + LAYER)
                dve.wait_ge(f2_full, L + U * max(b - 1, 0))
                for m in range(FM):
                    n = FWIDE[m]
                    dve.wait_ge(gate_done, L + U * b + after(m, FM - 1))
                    dve.scalar_tensor_tensor(out=uT[0:n, b % 2, m, :], in0=ps[0:n, PAIR + m % 2, 0:T],
                                             scalar=vec[0:n, V_B1A + m:V_B1A + m + 1], in1=gate[0:n, m % 2, :],
                                             op0=ALU.add, op1=ALU.mult).then_inc(u_done, 1 if m < FM - 1 else U - FM + 1)

            def add_ffn(L, b):
                dve.wait_ge(b2_done, L + U * (b + 1))
                dve.wait_ge(f2_full, L + U * (b + 1))
                both = k.y[:, b * TT:(b + 1) * TT, :]
                dve.tensor_tensor(both, ps[:, SCORE + b % 2, :].rearrange("p (t c) -> p t c", t=TT), both, ALU.add).then_inc(y_out, U)

            dve.wait_ge(zeros_set, 1)
            with dve.Fori(0, LAYERS) as i:
                L, shifts = dve.snap(i * LAYER + LAYER), dve.snap(i * 16 + 16)
                dve.wait_ge(gate_done, L)
                dve.wait_ge(u_done, L)
                kinds = k.cols[:, R_LAYER:ROWS].rearrange("p (v i) -> p v i", i=LAYERS)
                dve.tensor_copy(vec[:, :], kinds[:, :, bass.ds(i, 1)].rearrange("p v o -> p (v o)")).then_inc(vec_done, LAYER)
                dve.wait_ge(vec_done, L + LAYER)
                dve.wait_ge(tables_done, L + LAYER)
                for b in range(B):
                    rotate(L, b)
                    if b:
                        add_attention(L, b - 1)
                    if b == B - 1:
                        norm(L, shifts, 0)
                    softmax(L, b)
                gated(L, 0)
                norm(L, shifts, 1)
                add_attention(L, B - 1)
                for b in range(1, B):
                    gated(L, b)
                    if b < B - 1:
                        norm(L, shifts, b + 1)
                    add_ffn(L, b - 1)
                add_ffn(L, B - 1)
            dve.wait_ge(y_out, (LAYERS + 2) * LAYER)
            dve.tensor_tensor(k.x[:, :, :], k.x[:, :, :], k.y[:, :, :], ALU.add).then_inc(x_sum, 1)

        @block.gpsimd
        def _(pool):
            pool.memset(half[:, :], -0.5)
            for buf in (kT[:, :, :, :], prob1[:, :, :], xT[:, 1, 0:1], late[0:1, :, :]):
                ins = pool.memset(buf, 0.0)
            ins.then_inc(zeros_set, 1)
            pool.wait_ge(zeros_set, 1)
            pool.wait_ge(scale_in, 32)
            pool.wait_ge(b2_in, 16)

            def tables(L, i):
                pool.wait_ge(cos_done, L)
                scale = head_scale[:, bass.ds(i, 1), :, :].rearrange("p o s d -> p (o s) d")
                for t in range(TT):
                    row = lambda at: k.const[:, at + t * 2 * DH:at + (t + 1) * 2 * DH].rearrange("p (s d) -> p s d", s=2)
                    pool.tensor_tensor(cos[:, t, :, :], row(C_COS), scale, ALU.mult)
                    lo, hi = slice(0, DH // 2), slice(DH // 2, DH)
                    for dst, src in ((lo, hi), (hi, lo)):
                        ins = pool.tensor_tensor(sin[:, t, :, dst], row(C_SIN)[:, :, dst], scale[:, :, src], ALU.mult)
                ins.then_inc(tables_done, LAYER)

            def rotate(L, b):
                for t in range(TT):
                    at = L + U * b + 8 * t
                    pool.wait_ge(floor_done, at + 8)
                    pool.wait_ge(s_read, L + U * max(b - 1, 0))
                    pool.tensor_tensor(rnorm[:, b % 2, t, :], norm2_floor[:, :], half[:, :], ALU.pow).then_inc(rnorm_done, 8)
                    pool.wait_ge(cos_done, at + 8)
                    pool.tensor_tensor(qk[:, t, :], qk[:, t, :], twist, ALU.add).then_inc(sum_done, 8)
                    pool.wait_ge(rnorm_done, at + 8)
                    pool.wait_ge(sum_done, at + 8)
                    keys = qk[:, t, INNER:].rearrange("p (h d) -> p h d", d=DH)
                    pool.tensor_tensor(keys, keys, rnorm[:, b % 2, t, H:].unsqueeze(2).broadcast_to([P, H, DH]), ALU.mult)\
                        .then_inc(rope_done, 8)

            def norm(L, i, b):
                pool.wait_ge(ln_var, L + U * (b + 1))
                pool.tensor_tensor(rstd[:, :], var[:, :], half[:, 0:TT], ALU.pow).then_inc(ln_rstd, U)
                pool.wait_ge(xn_done, L + U * (b + 1))
                both = k.y[:, b * TT:(b + 1) * TT, :]
                pool.tensor_tensor(both, both, b2[:, bass.ds(i, 1), :].broadcast_to([P, TT, D]), ALU.add).then_inc(b2_done, U)

            with pool.Fori(0, LAYERS) as i:
                L = pool.snap(i * LAYER + LAYER)
                tables(L, i)
                for b in range(B):
                    rotate(L, b)
                for b in range(B):
                    norm(L, i, b)


def store(k):
    nc, io = k.nc, k.io
    with ExitStack() as ctx:
        out_done = k.sem("out_done")
        block = ctx.enter_context(nc.Block())

        @block.sync
        def _(sp):
            sp.dma_start(io["out"].rearrange("b (t p) c -> p (b t) c", p=P), k.x[:, :, :]).then_inc(out_done, 16)
            sp.wait_ge(out_done, 16)


STAGES = (cross_attention, linear_attention, local_layers, store)


def build(nc, io, stages=None):
    with ExitStack() as ctx:
        k = Kernel(nc, ctx, io)
        for stage in stages or STAGES:
            stage(k)


_INS = ["x", "ctx_1024", "xattn_g1", "xattn_b1", "xattn_g2", "xattn_b2", "xattn_Wq", "xattn_Wkv", "xattn_Wout",
        "attn_Wq", "attn_bq", "attn_Wk", "attn_bk", "attn_Wv", "attn_bv", "attn_Wo", "attn_bo", "attn_ln_g", "attn_ln_b",
        "ffn_Wqkv", "ffn_q_scale", "ffn_k_scale", "ffn_Wo", "ffn_ln_g", "ffn_ln_b", "ffn_W1", "ffn_b1", "ffn_W2", "ffn_b2"]


def prepare(nc, inputs):
    arrays, io = {}, {}

    def add(name, a):
        a = np.ascontiguousarray(a)
        arrays[f"in_{name}_dram"] = a
        io[name] = nc.dram_tensor(f"in_{name}_dram", a.shape, mybir.dt.from_np(a.dtype), kind="ExternalInput").ap()

    for name in _INS:
        add(name, inputs[name if name in ("x", "ctx_1024") else f"L0_{name}"])
    add("mask", np.asarray(inputs["mask_BxS2_bk0"]))
    add("const", constants())
    io["out"] = nc.dram_tensor("out_0_dram", (B, T, D), F32, kind="ExternalOutput").ap()
    return arrays, io


def kernel(**inputs):
    import concourse.bacc as _bacc
    from concourse.bass_utils import run_bass_kernel_spmd as _run

    nc = _bacc.Bacc("TRN2", target_bir_lowering=False, num_devices=1)
    arrays, io = prepare(nc, inputs)
    build(nc, io)
    r = _run(nc, [arrays], core_ids=[0])
    return r.results[0]["out_0_dram"]
```

```python
from contextlib import ExitStack

import concourse.bass as bass
import numpy as np
from concourse import mybir

F32 = mybir.dt.float32
I32 = mybir.dt.int32
U8 = mybir.dt.uint8
ALU = mybir.AluOpType
ACT = mybir.ActivationFunctionType
AX = mybir.AxisListType

P = 128
B, T, D = 4, 256, 256
S = 4096
H, DH = 16, 64
INNER = H * DH
PAIRS = H // 2
TT = T // P
KD = D // P
CHUNK = 256
CHUNKS = S // CHUNK
KT = CHUNK // P
GROUP = 4
LAYERS = 6
FF = int(D * 4 * 2 / 3)
FM = (FF + P - 1) // P
FWIDE = [FF // FM + (m < FF % FM) for m in range(FM)]
FAT = [sum(FWIDE[:m]) for m in range(FM)]
WINDOW = 64
LH, LD = 16, 16
EPS = 1e-5
FAR = 3.0e38
BAND = 1.0e30
QK_SCALE = 8.0

C_ID = 0
C_BAND0 = C_ID + P
C_BAND1 = C_BAND0 + P
C_BLOCK = C_BAND1 + 192
C_COS = C_BLOCK + P
C_SIN = C_COS + TT * 2 * DH
C_BIT = C_SIN + TT * 2 * DH
C_ALL = C_BIT + CHUNKS

R_G1, R_B1, R_G2, R_B2, R_BQ, R_LG, R_LB = (2 * j for j in range(7))
R_LAYER = 14
V_FG, V_FB, V_B1A, V_B1G = 0, 2, 4, 4 + FM
KINDS = 4 + 2 * FM
ROWS = R_LAYER + KINDS * LAYERS


def constants():
    c = np.zeros((P, C_ALL), np.float32)
    c[:, C_ID:C_ID + P] = np.eye(P, dtype=np.float32)
    q, k = np.arange(P)[:, None], np.arange(P)[None, :]
    c[:, C_BAND0:C_BAND0 + P] = np.where((q < k) | (q > k + WINDOW) , BAND, 0.0)
    q, k = np.arange(P, 2 * P)[:, None], np.arange(WINDOW, 2 * P)[None, :]
    c[:, C_BAND1:C_BAND1 + 192] = np.where((q < k) | (q > k + WINDOW), BAND, 0.0)
    d, e = np.arange(P)[:, None], np.arange(P)[None, :]
    c[:, C_BLOCK:C_BLOCK + P] = np.where(d // LD == e // LD, 1.0 / 1024.0 ** 2, 0.0)
    half = np.arange(0, DH, 2, dtype=np.float32)
    t = np.arange(T, dtype=np.float32)
    freqs = t[:, None] * (np.float32(1.0) / np.float32(10000.0) ** (half / np.float32(DH)))[None, :]
    freqs = np.concatenate([freqs, freqs], -1).astype(np.float32)
    base = (half + np.float32(0.4 * DH)) / np.float32(1.4 * DH)
    scale = base[None, :] ** ((t - T // 2) / np.float32(WINDOW // 2))[:, None]
    scale = np.concatenate([scale, scale], -1).astype(np.float32)
    sign = np.where(np.arange(DH) < DH // 2, -1.0, 1.0).astype(np.float32)
    both = [(np.cos(freqs) * s, np.sin(freqs) * sign * s) for s in (-np.float32(QK_SCALE) * scale, 1.0 / scale)]
    for n, at in enumerate((C_COS, C_SIN)):
        table = np.stack([both[0][n], both[1][n]], 1).astype(np.float32)
        c[:, at:at + TT * 2 * DH] = table.reshape(TT, P, 2 * DH).transpose(1, 0, 2).reshape(P, -1)
    c[:, C_BIT:C_BIT + CHUNKS] = 2.0 ** np.arange(CHUNKS)
    return c


class Chain:

    def __init__(self, eng, sem, base=0):
        self.eng, self.sem, self.base, self.n = eng, sem, base, 0

    def link(self, ins):
        self.n += 1
        ins.then_inc(self.sem, 1)
        self.eng.wait_ge(self.sem, self.base + self.n)


def hold(eng, sem):
    eng.sem_inc(sem, 1)


def begin_at(eng, count, sems):
    for sem in sems:
        eng.sem_inc(sem, count)


class Kernel:

    def __init__(self, nc, ctx, io):
        self.nc, self.io = nc, io
        self.ctx = ctx
        self.x = self.sb("x_all", [P, B * TT, D])
        self.y = self.sb("y_all", [P, B * TT, D])
        self.const = self.sb("const", [P, C_ALL])
        self.cols = self.sb("cols", [P, ROWS])
        self.ident = self.const[:, C_ID:C_ID + P]

    def sb(self, name, shape, dt=F32, ctx=None):
        return (ctx or self.ctx).enter_context(self.nc.sbuf_tensor(name, shape, dt))

    def banks(self, name, ctx):
        return ctx.enter_context(self.nc.psum_tensor(name, [P, 8, 512], F32))

    def sem(self, name):
        return self.ctx.enter_context(self.nc.semaphore(name))


def cross_attention(k):
    nc, io = k.nc, k.io
    U = 16
    with ExitStack() as ctx:
        sb = lambda name, shape, dt=F32: k.sb(name, shape, dt, ctx)
        rows = sb("rows", [P, P])
        wq = sb("wq", [P, KD, INNER])
        wkv = sb("wkv", [P, KD, 2 * INNER])
        wout = sb("wout", [P, PAIRS, D])
        mask_rows = sb("mask_rows", [B, S], U8)
        chunk_any = sb("chunk_any", [B, CHUNKS])
        word_f = sb("word_f", [B, 1])
        word_col = sb("word_col", [B, 1], I32)
        word = sb("word", [1, B], I32)
        lats = k.y
        lat = sb("lat", [P, TT, D])
        ctx_raw = sb("ctx_raw", [P, KT, D])
        chunk_mask = sb("chunk_mask", [P, CHUNK], U8)
        bias = sb("bias", [P, CHUNK])
        no_bias = sb("no_bias", [P, CHUNK])
        xn = sb("xn", [P, KT, D])
        inT = sb("inT", [P, KD, CHUNK])
        inT_v = sb("inT_v", [P, KD, CHUNK])
        qT = sb("qT", [P, H, T])
        kT = sb("kT", [P, PAIRS, CHUNK])
        v = sb("v", [P, KT, INNER])
        prob = sb("prob", [P, TT, H, CHUNK])
        probT = sb("probT", [P, 2, KT, 512])
        oT = sb("oT", [P, PAIRS, T])
        o = sb("o", [P, TT, INNER])
        stats = sb("stats", [P, B * TT, 6])
        mv = sb("mv", [P, B * TT, 2])
        var = sb("var", [P, B * TT])
        rstd = sb("rstd", [P, B * TT])
        half = sb("half", [P, B * TT])
        top = sb("top", [P, TT, H])
        chunk_top = sb("chunk_top", [P, TT, H])
        new_top = sb("new_top", [P, TT, H])
        drop = sb("drop", [P, TT, H])
        alpha = sb("alpha", [P, TT, H])
        chunk_sum = sb("chunk_sum", [P, TT, H])
        total = sb("total", [P, TT, H])
        rtotal = sb("rtotal", [P, TT, H])
        ps = k.banks("ps_cross", ctx)
        PROJ, SCORE, TURN, OUT = 0, 2, 4, 6

        sem = k.sem
        const_in, x_in, mask_in, w_in = sem("const_in"), sem("x_in"), sem("mask_in"), sem("w_in")
        rows_zero, rows_in, cols_full = sem("rows_zero"), sem("rows_in"), sem("cols_full")
        words_out, words_in, q_zero = sem("words_out"), sem("words_in"), sem("q_zero")
        ctx_in, chunk_mask_in, bias_done = sem("ctx_in"), sem("chunk_mask_in"), sem("bias_done")
        ln_var, ln_rstd, lat_ready, xn_ready = sem("ln_var"), sem("ln_rstd"), sem("lat_ready"), sem("xn_ready")
        inT_full, inT_done, inT_copied, q_full, q_done = sem("inT_full"), sem("inT_done"), sem("inT_copied"), sem("q_full"), sem("q_done")
        k_full, k_done, v_full, v_done = sem("k_full"), sem("k_done"), sem("v_full"), sem("v_done")
        s_full, s_read, top_done, alpha_done = sem("s_full"), sem("s_read"), sem("top_done"), sem("alpha_done")
        p_ready, o_scaled, total_done = sem("p_ready"), sem("o_scaled"), sem("total_done")
        pT_full, pT_done, o_full, oT_done = sem("pT_full"), sem("pT_done"), sem("o_full"), sem("oT_done")
        back_full, back_done = sem("back_full"), sem("back_done")
        fin_ready, fin_full, fin_done = sem("fin_ready"), sem("fin_full"), sem("fin_done")
        x_full, x_done = sem("x_full"), sem("x_done")
        dve_step, pool_step, dve_held, pool_held, lats_done = (
            sem(f"cross_{n}") for n in ("dve_step", "pool_step", "dve_held", "pool_held", "lats_done"))

        ctx_dram = io["ctx_1024"].rearrange("b (c t p) d -> (b c) p t d", p=P, t=KT)
        mask_dram = io["mask"].rearrange("b (c n) -> (b c) n", n=CHUNK)

        def attended(eng, b):
            return eng.value_load(word[0:1, bass.ds(b, 1)], min_val=0, max_val=2 ** CHUNKS - 1)

        def chunks(eng, bits, body):
            with eng.Fori(0, CHUNKS // GROUP) as g:
                with eng.If((bits >> (g * GROUP)) & (2 ** GROUP - 1)):
                    with eng.Fori(0, GROUP) as n:
                        c = eng.snap(g * GROUP + n)
                        with eng.If((bits >> c) & 1):
                            body(c)

        block = ctx.enter_context(nc.Block())

        @block.sync
        def _(sp):
            sp.dma_start(k.const[:, :], io["const"]).then_inc(const_in, 16)
            sp.dma_start(k.x[:, :, :], io["x"].rearrange("b (t p) c -> p (b t) c", p=P)).then_inc(x_in, 16)
            sp.dma_start(mask_rows[:, :], io["mask"]).then_inc(mask_in, 16)
            begin_at(sp, U, (xn_ready, bias_done, ctx_in, chunk_mask_in, inT_full, inT_done, inT_copied, k_full, k_done, v_full, v_done, s_full, s_read,
                             top_done, alpha_done, p_ready, o_scaled, total_done, pT_full, pT_done, o_full, oT_done,
                             back_full, back_done))
            begin_at(sp, 4, (q_full, q_done, fin_full, fin_done))
            begin_at(sp, 2, (fin_ready, x_full, x_done))
            sp.wait_ge(rows_zero, 1)
            for r, name in ((R_G1, "xattn_g1"), (R_B1, "xattn_b1"), (R_G2, "xattn_g2"), (R_B2, "xattn_b2"),
                            (R_BQ, "attn_bq"), (R_LG, "attn_ln_g"), (R_LB, "attn_ln_b")):
                sp.dma_start(rows[r:r + KD, :], io[name].rearrange("(k p) -> k p", p=P)).then_inc(rows_in, 16)
            layer_rows = [(V_FG + j, io["ffn_ln_g"][:, j * P:(j + 1) * P]) for j in range(KD)]
            layer_rows += [(V_FB + j, io["ffn_ln_b"][:, j * P:(j + 1) * P]) for j in range(KD)]
            layer_rows += [(V_B1A + m, io["ffn_b1"][:, FAT[m]:FAT[m] + FWIDE[m]]) for m in range(FM)]
            layer_rows += [(V_B1G + m, io["ffn_b1"][:, FF + FAT[m]:FF + FAT[m] + FWIDE[m]]) for m in range(FM)]
            for kind, src in layer_rows:
                r = R_LAYER + kind * LAYERS
                sp.dma_start(rows[r:r + LAYERS, 0:src.shape[1]], src).then_inc(rows_in, 16)
            sp.wait_ge(words_out, 1)
            sp.dma_start(word[0:1, :], word_col[:, :]).then_inc(words_in, 16)
            sp.wait_ge(words_in, 16)
            uc_reg = sp.alloc_register("sp_uc")
            sp.reg_mov(uc_reg, U)
            with sp.Fori(1, B + 1) as turn:
                b = turn - 1
                def load(c):
                    uc = sp.snap(uc_reg)
                    sp.wait_ge(xn_ready, uc)
                    sp.wait_ge(bias_done, uc)
                    sp.dma_start(ctx_raw[:, :, :], ctx_dram[bass.ds(b * CHUNKS + c, 1)].rearrange("o p t d -> (o p) t d"))\
                        .then_inc(ctx_in, 16)
                    sp.dma_start(chunk_mask[:, :], mask_dram[bass.ds(b * CHUNKS + c, 1)].broadcast_to([P, CHUNK]))\
                        .then_inc(chunk_mask_in, 16)
                    sp.reg_add(uc_reg, uc_reg, U)
                chunks(sp, attended(sp, b), load)

        @block.tensor
        def _(pe):
            u_reg, uc_reg = pe.alloc_register("pe_u"), pe.alloc_register("pe_uc")
            pe.reg_mov(u_reg, U)
            pe.reg_mov(uc_reg, U)
            pe.wait_ge(const_in, 16)
            pe.wait_ge(rows_in, 16 * N_ROW_DMAS)
            pe.transpose(ps[:, OUT, 0:ROWS], rows[0:ROWS, :], k.ident[0:ROWS, 0:ROWS]).then_inc(cols_full, 1)
            pe.wait_ge(words_in, 16)

            def turn_input(src):
                for kk in range(KD):
                    for t in range(KT):
                        ins = pe.transpose(ps[:, TURN + kk, t * P:(t + 1) * P], src(t, kk), k.ident)
                    ins.then_inc(inT_full, U // KD)

            def project_q(u, turn):
                pe.wait_ge(inT_done, u + U)
                for j in range(4):
                    if j >= 2:
                        pe.wait_ge(q_done, turn * 4 + j - 1)
                    for i in range(2):
                        pair = 2 * j + i
                        for kk in range(KD):
                            ins = pe.matmul(ps[:, PROJ + j % 2, i * T:(i + 1) * T], wq[:, kk, pair * P:(pair + 1) * P],
                                            inT[:, kk, :], start=kk == 0, stop=kk == KD - 1)
                    ins.then_inc(q_full, 1)

            def keys(u, turn):
                pe.wait_ge(inT_done, u + U)
                pe.wait_ge(q_done, turn * 4 + 4)
                for j in range(4):
                    if j < 2:
                        pe.wait_ge(v_done, u - 4 + 4 * j)
                    else:
                        pe.wait_ge(k_done, u + 4 * (j - 1))
                    for i in range(2):
                        pair = 2 * j + i
                        for kk in range(KD):
                            ins = pe.matmul(ps[:, PROJ + j % 2, i * CHUNK:(i + 1) * CHUNK],
                                            wkv[:, kk, pair * P:(pair + 1) * P], inT[:, kk, :],
                                            start=kk == 0, stop=kk == KD - 1)
                    ins.then_inc(k_full, U // 4)

            def scores(u, t, pair):
                s = t * PAIRS + pair
                if t == 0 and pair % 2 == 0:
                    pe.wait_ge(k_done, u + 4 * (pair // 2 + 1))
                pe.wait_ge(s_read, u + (s - 1 if s >= 2 else 0))
                for i in range(2):
                    ins = pe.matmul(ps[:, SCORE + s % 2, i * CHUNK:(i + 1) * CHUNK],
                                    qT[:, 2 * pair + i, t * P:(t + 1) * P], kT[:, pair, :], start=True, stop=True)
                ins.then_inc(s_full, 1)

            def values(u, js):
                for j in js:
                    t, part = divmod(j, 2)
                    if j == 0:
                        pe.wait_ge(inT_copied, u + U)
                    if j >= 2:
                        pe.wait_ge(v_done, u + 4 * (j - 1))
                    for kk in range(KD):
                        ins = pe.matmul(ps[:, PROJ + j % 2, :], inT_v[:, kk, t * P:(t + 1) * P],
                                        wkv[:, kk, INNER + part * 512:INNER + (part + 1) * 512],
                                        start=kk == 0, stop=kk == KD - 1)
                    ins.then_inc(v_full, U // 4)

            def turn_probs(u, pair):
                pe.wait_ge(p_ready, u + PAIRS + pair + 1)
                for t in range(KT):
                    s = 2 * pair + t
                    pe.wait_ge(pT_done, u + (s - 1 if s >= 2 else 0))
                    for i in range(2):
                        for lt in range(TT):
                            ins = pe.transpose(ps[:, TURN + t, (i * TT + lt) * P:(i * TT + lt + 1) * P],
                                               prob[:, lt, 2 * pair + i, t * P:(t + 1) * P], k.ident)
                    ins.then_inc(pT_full, 1)

            def weigh(u, pair):
                if pair == 0:
                    pe.wait_ge(v_done, u + U)
                pe.wait_ge(pT_done, u + 2 * pair + 2)
                pe.wait_ge(oT_done, u + (2 * (pair - 1) if pair >= 2 else 0))
                for t in range(KT):
                    for i in range(2):
                        ins = pe.matmul(ps[i * DH:(i + 1) * DH, OUT + pair % 2, 0:T],
                                        v[:, t, (2 * pair + i) * DH:(2 * pair + i + 1) * DH],
                                        probT[:, pair % 2, t, i * T:(i + 1) * T], start=t == 0, stop=t == KT - 1)
                ins.then_inc(o_full, 2)

            def back(u, part):
                pe.wait_ge(oT_done, u + 8 * (part + 1))
                for t in range(TT):
                    if part:
                        pe.wait_ge(back_done, u + 4 * (t + 1))
                    for i in range(4):
                        ins = pe.transpose(ps[:, PROJ + t, i * P:(i + 1) * P],
                                           oT[:, 4 * part + i, t * P:(t + 1) * P], k.ident)
                    ins.then_inc(back_full, 4)

            with pe.Fori(1, B + 1) as turn:
                b = turn - 1
                u = pe.snap(u_reg)
                pe.wait_ge(lat_ready, turn)
                pe.wait_ge(v_done, u)
                pe.wait_ge(back_done, u)
                pe.wait_ge(pT_done, u)
                pe.wait_ge(w_in, 48)
                turn_input(lambda t, kk: lat[:, t, kk * P:(kk + 1) * P])
                project_q(u, turn)
                keys(u, turn)
                for pair in range(PAIRS):
                    scores(u, 0, pair)
                for pair in range(PAIRS):
                    scores(u, 1, pair)
                    if pair == 5:
                        values(u, (0, 1))
                pe.reg_add(u_reg, u_reg, U)

                def step(c):
                    u, uc, last = pe.snap(u_reg), pe.snap(uc_reg), pe.snap(pe.snap(u_reg) - U)
                    pe.wait_ge(xn_ready, uc + U)
                    pe.wait_ge(pT_done, last)
                    turn_input(lambda t, kk: xn[:, t, kk * P:(kk + 1) * P])
                    values(last, (2, 3))
                    keys(u, turn)
                    for pair in range(PAIRS):
                        turn_probs(last, pair)
                        if pair:
                            weigh(last, pair - 1)
                        scores(u, 0, pair)
                        if pair == 6:
                            pe.wait_ge(k_done, u + U)
                            back(last, 0)
                    weigh(last, PAIRS - 1)
                    for pair in range(PAIRS):
                        scores(u, 1, pair)
                        if pair == 2:
                            back(last, 1)
                        if pair == 5:
                            pe.wait_ge(back_done, u)
                            values(u, (0, 1))
                    pe.reg_add(u_reg, u_reg, U)
                    pe.reg_add(uc_reg, uc_reg, U)
                chunks(pe, attended(pe, b), step)
                u, last = pe.snap(u_reg), pe.snap(pe.snap(u_reg) - U)
                values(last, (2, 3))
                for pair in range(PAIRS):
                    turn_probs(last, pair)
                    if pair:
                        weigh(last, pair - 1)
                    if pair == 5:
                        pe.wait_ge(v_done, u)
                        back(last, 0)
                weigh(last, PAIRS - 1)
                back(last, 1)
                for j in range(4):
                    t, part = divmod(j, 2)
                    pe.wait_ge(fin_ready, turn * 2 + t + 1)
                    if j < 2:
                        pe.wait_ge(back_done, u)
                    else:
                        pe.wait_ge(fin_done, turn * 4 + j - 1)
                    for i in range(4):
                        ins = pe.transpose(ps[:, PROJ + j % 2, i * P:(i + 1) * P],
                                           o[:, t, (4 * part + i) * P:(4 * part + i + 1) * P], k.ident)
                    ins.then_inc(fin_full, 1)
                for t in range(TT):
                    pe.wait_ge(fin_done, turn * 4 + 2 * (t + 1))
                    for pair in range(PAIRS):
                        ins = pe.matmul(ps[:, OUT + t, 0:D], oT[:, pair, t * P:(t + 1) * P], wout[:, pair, :],
                                        start=pair == 0, stop=pair == PAIRS - 1)
                    ins.then_inc(x_full, 1)
                pe.wait_ge(x_done, turn * 2 + 2)

        @block.scalar
        def _(act):
            u_reg = act.alloc_register("act_u")
            act.reg_mov(u_reg, U)
            act.dma_start(wq[:, :, :], io["xattn_Wq"].rearrange("(k p) n -> p k n", p=P)).then_inc(w_in, 16)
            act.dma_start(wkv[:, :, :], io["xattn_Wkv"].rearrange("(k p) n -> p k n", p=P)).then_inc(w_in, 16)
            act.dma_start(wout[:, :, :], io["xattn_Wout"].rearrange("(k p) n -> p k n", p=P)).then_inc(w_in, 16)
            act.wait_ge(q_zero, 1)
            act.wait_ge(words_in, 16)

            def keys_out(u):
                act.wait_ge(s_full, u)
                for j in range(4):
                    act.wait_ge(k_full, u + 4 * (j + 1))
                    act.activation(kT[:, 2 * j:2 * j + 2, :], ps[:, PROJ + j % 2, :].rearrange("p (i n) -> p i n", i=2),
                                   ACT.Copy).then_inc(k_done, U // 4)
                act.wait_ge(inT_done, u + U)
                act.wait_ge(v_full, u)
                act.activation(inT_v[:, :, :], inT[:, :, :], ACT.Copy).then_inc(inT_copied, U)

            def exps(u):
                act.wait_ge(o_scaled, u)
                act.wait_ge(total_done, u)
                for t in range(TT):
                    act.wait_ge(top_done, u + 8 * (t + 1))
                    act.activation(alpha[:, t, :], drop[:, t, :], ACT.Exp).then_inc(alpha_done, U // TT)
                    for h in range(H):
                        ins = act.activation(prob[:, t, h, :], prob[:, t, h, :], ACT.Exp, bias=new_top[:, t, h:h + 1],
                                             scale=-1.0, accum_out=chunk_sum[:, t, h:h + 1])
                        if h % 2:
                            ins.then_inc(p_ready, 1)

            def output_out(u):
                act.wait_ge(back_full, u)
                for pair in range(PAIRS):
                    act.wait_ge(o_full, u + 2 * (pair + 1))
                    act.activation(oT[:, pair, :], ps[:, OUT + pair % 2, 0:T], ACT.Copy).then_inc(oT_done, 2)

            with act.Fori(1, B + 1) as turn:
                b = turn - 1
                u = act.snap(u_reg)
                act.wait_ge(s_full, u)
                for j in range(4):
                    act.wait_ge(q_full, turn * 4 + j + 1)
                    for i in range(2):
                        half_q = qT[i * DH:(i + 1) * DH, :, :].rearrange("p (g e) n -> p g e n", e=2)
                        ins = act.activation(half_q[:, 2 * j:2 * j + 2, i, :],
                                             ps[i * DH:(i + 1) * DH, PROJ + j % 2, :].rearrange("p (g n) -> p g n", g=2),
                                             ACT.Copy, scale=-float(DH) ** -0.5)
                    ins.then_inc(q_done, 1)
                keys_out(u)
                exps(u)
                act.wait_ge(x_full, turn * 2)
                act.reg_add(u_reg, u_reg, U)

                def step(c):
                    u = act.snap(u_reg)
                    keys_out(u)
                    output_out(act.snap(act.snap(u_reg) - U))
                    exps(u)
                    act.reg_add(u_reg, u_reg, U)
                chunks(act, attended(act, b), step)
                output_out(act.snap(act.snap(u_reg) - U))
                for j in range(4):
                    t, part = divmod(j, 2)
                    act.wait_ge(fin_full, turn * 4 + j + 1)
                    if j == 0:
                        act.wait_ge(back_full, act.snap(u_reg))
                    act.activation(oT[:, 4 * part:4 * part + 4, t * P:(t + 1) * P],
                                   ps[:, PROJ + j % 2, :].rearrange("p (i n) -> p i n", i=4), ACT.Copy)\
                        .then_inc(fin_done, 1)

        @block.vector
        def _(dve):
            u_reg, uc_reg, ln_reg, step_reg = (dve.alloc_register(f"dve_{n}") for n in ("u", "uc", "ln", "step"))
            for r, first in ((u_reg, U), (uc_reg, U), (ln_reg, 2)):
                dve.reg_mov(r, first)
            chain = Chain(dve, dve_step)
            chain.link(dve.memset(no_bias[:, :], 0.0))
            dve.wait_ge(mask_in, 16)
            dve.wait_ge(const_in, 16)
            chain.link(dve.tensor_reduce(chunk_any[:, :], mask_rows[:, :].rearrange("b (c n) -> b c n", n=CHUNK), AX.X, ALU.max))
            chain.link(dve.tensor_tensor(chunk_any[:, :], chunk_any[:, :], k.const[0:B, C_BIT:C_BIT + CHUNKS], ALU.mult))
            chain.link(dve.tensor_reduce(word_f[:, :], chunk_any[:, :], AX.X, ALU.add))
            dve.tensor_copy(word_col[:, :], word_f[:, :]).then_inc(words_out, 1)
            def norm(ch, src, dst, ln, tiles):
                for t in tiles:
                    ins = dve.bn_stats(stats[:, t, :], src(t))
                ch.link(ins)
                hold(dve, dve_held)
                for t in tiles:
                    ins = dve.bn_aggr(mv[:, t, :], stats[:, t, :])
                ch.link(ins)
                dve.tensor_scalar(var[:, 0:len(tiles)], mv[:, 0:len(tiles), 1], EPS, None, ALU.add).then_inc(ln_var, 1)
                dve.wait_ge(ln_rstd, ln + 1)
                return [dve.tensor_scalar(dst[:, t, :], src(t), mv[:, t, 0:1], rstd[:, t:t + 1], ALU.subtract, ALU.mult)
                        for t in tiles]

            dve.wait_ge(x_in, 16)
            for n, src in enumerate((k.x, lats)):
                *_, last = norm(chain, lambda t: src[:, t, :], lats, n, range(B * TT))
                if n == 0:
                    chain.link(last)
                else:
                    last.then_inc(lats_done, 1)
            dve.wait_ge(cols_full, 1)
            chain.link(dve.tensor_copy(k.cols[:, :], ps[:, OUT, 0:ROWS]))
            dve.reg_mov(step_reg, chain.n)
            dve.wait_ge(words_in, 16)

            def input_out(u, g, bb):
                dve.wait_ge(k_full, u)
                dve.wait_ge(inT_copied, u)
                for kk in range(KD):
                    dve.wait_ge(inT_full, u + 8 * (kk + 1))
                    dve.tensor_scalar(inT[:, kk, :], ps[:, TURN + kk, 0:CHUNK], k.cols[:, g + kk:g + kk + 1],
                                      k.cols[:, bb + kk:bb + kk + 1], ALU.mult, ALU.add).then_inc(inT_done, U // KD)

            def minima(u, t, pair, key_bias):
                s = t * PAIRS + pair
                dve.wait_ge(s_full, u + s + 1)
                hold(dve, dve_held)
                for i in range(2):
                    h = 2 * pair + i
                    ins = dve.tensor_tensor_reduce(
                        out=prob[:, t, h, :], in0=ps[:, SCORE + s % 2, i * CHUNK:(i + 1) * CHUNK], in1=key_bias,
                        scale=1.0, scalar=FAR, op0=ALU.add, op1=ALU.min, accum_out=chunk_top[:, t, h:h + 1])
                ins.then_inc(s_read, 1)

            def running(ch, u, t):
                dve.wait_ge(s_read, u + (t + 1) * PAIRS)
                if t == 0:
                    dve.wait_ge(p_ready, u)
                ch.link(dve.tensor_tensor(new_top[:, t, :], top[:, t, :], chunk_top[:, t, :], ALU.min))
                dve.tensor_tensor(drop[:, t, :], new_top[:, t, :], top[:, t, :], ALU.subtract).then_inc(top_done, U // TT)
                dve.wait_ge(top_done, u + (t + 1) * (U // TT))
                ch.link(dve.tensor_copy(top[:, t, :], new_top[:, t, :]))

            def values_out(u, js):
                dve.wait_ge(o_full, u)
                for j in js:
                    t, part = divmod(j, 2)
                    dve.wait_ge(v_full, u + 4 * (j + 1))
                    dve.tensor_copy(v[:, t, part * 512:(part + 1) * 512], ps[:, PROJ + j % 2, :]).then_inc(v_done, U // 4)

            def probs_out(u, pair):
                if pair >= 2:
                    dve.wait_ge(o_full, u + 2 * (pair - 1))
                for t in range(KT):
                    dve.wait_ge(pT_full, u + 2 * pair + t + 1)
                    dve.tensor_copy(probT[:, pair % 2, t, :], ps[:, TURN + t, :]).then_inc(pT_done, 1)

            def back(u, part):
                for t in range(TT):
                    dve.wait_ge(back_full, u + 4 * (2 * part + t + 1))
                    dve.wait_ge(o_scaled, u + 8 * (t + 1))
                    out = o[:, t, part * 512:(part + 1) * 512]
                    dve.tensor_tensor(out, ps[:, PROJ + t, :], out, ALU.add).then_inc(back_done, 4)

            def prepare_next(more):
                with dve.If(more):
                    uc, ln = dve.snap(uc_reg), dve.snap(ln_reg)
                    ch = Chain(dve, dve_step, dve.snap(step_reg))
                    dve.wait_ge(ctx_in, uc + U)
                    hold(dve, dve_held)
                    for ins in norm(ch, lambda t: ctx_raw[:, t, :], xn, ln, range(KT)):
                        ins.then_inc(xn_ready, U // KT)
                    dve.reg_add(uc_reg, uc_reg, U)
                    dve.reg_add(ln_reg, ln_reg, 1)
                    done(ch)

            def done(ch):
                dve.reg_add(step_reg, step_reg, ch.n)

            with dve.Fori(1, B + 1) as turn:
                b = turn - 1
                u = dve.snap(u_reg)
                ch = Chain(dve, dve_step, dve.snap(step_reg))
                dve.wait_ge(p_ready, u)
                hold(dve, dve_held)
                ch.link(dve.memset(top[:, :, :], FAR))
                input_out(u, R_G2, R_B2)
                done(ch)
                bits = attended(dve, b)
                prepare_next(bits > 0)
                ch = Chain(dve, dve_step, dve.snap(step_reg))
                for pair in range(PAIRS):
                    minima(u, 0, pair, no_bias[:, :])
                running(ch, u, 0)
                for pair in range(PAIRS):
                    minima(u, 1, pair, no_bias[:, :])
                    if pair in (5, 6):
                        values_out(u, (pair - 5,))
                running(ch, u, 1)
                done(ch)
                dve.reg_add(u_reg, u_reg, U)

                def step(c):
                    u, last, uc = dve.snap(u_reg), dve.snap(dve.snap(u_reg) - U), dve.snap(uc_reg)
                    dve.wait_ge(chunk_mask_in, uc)
                    dve.tensor_scalar(bias[:, :], chunk_mask[:, :], -1.0, -FAR, ALU.add, ALU.mult).then_inc(bias_done, U)
                    input_out(u, R_G1, R_B1)
                    values_out(last, (2, 3))
                    prepare_next((bits >> c) > 1)
                    ch = Chain(dve, dve_step, dve.snap(step_reg))
                    for pair in range(PAIRS):
                        probs_out(last, pair)
                        if pair == 0:
                            dve.wait_ge(bias_done, uc)
                        minima(u, 0, pair, bias[:, :])
                    running(ch, u, 0)
                    for pair in range(PAIRS):
                        minima(u, 1, pair, bias[:, :])
                        if pair in (1, 3):
                            back(last, pair // 2)
                        if pair in (5, 6):
                            values_out(u, (pair - 5,))
                    running(ch, u, 1)
                    done(ch)
                    dve.reg_add(u_reg, u_reg, U)
                chunks(dve, bits, step)
                last = dve.snap(dve.snap(u_reg) - U)
                values_out(last, (2, 3))
                for pair in range(PAIRS):
                    probs_out(last, pair)
                back(last, 0)
                back(last, 1)
                u = dve.snap(u_reg)
                ch = Chain(dve, dve_step, dve.snap(step_reg))
                dve.wait_ge(total_done, u)
                dve.wait_ge(back_done, u)
                ch.link(dve.reciprocal(rtotal[:, :, :], total[:, :, :]))
                for t in range(TT):
                    by_head = o[:, t, :].rearrange("p (h d) -> p h d", d=DH)
                    dve.tensor_tensor(by_head, by_head, rtotal[:, t, :].unsqueeze(2).broadcast_to([P, H, DH]), ALU.mult)\
                        .then_inc(fin_ready, 1)
                for t in range(TT):
                    dve.wait_ge(x_full, turn * 2 + t + 1)
                    xt = k.x[:, bass.ds(b * TT + t, 1), :].rearrange("p o d -> p (o d)")
                    dve.tensor_tensor(xt, ps[:, OUT + t, 0:D], xt, ALU.add).then_inc(x_done, 1)
                done(ch)

        @block.gpsimd
        def _(pool):
            u_reg, ln_reg, step_reg = (pool.alloc_register(f"pool_{n}") for n in ("u", "ln", "step"))
            for r, first in ((u_reg, U), (ln_reg, 2)):
                pool.reg_mov(r, first)
            chain = Chain(pool, pool_step)
            pool.memset(rows[:, :], 0.0).then_inc(rows_zero, 1)
            pool.memset(qT[:, :, :], 0.0).then_inc(q_zero, 1)
            chain.link(pool.memset(half[:, :], -0.5))
            pool.reg_mov(step_reg, chain.n)
            def root(ln, n):
                pool.wait_ge(ln_var, ln + 1)
                pool.tensor_tensor(rstd[:, 0:n], var[:, 0:n], half[:, 0:n], ALU.pow).then_inc(ln_rstd, 1)

            def rescale(ch, u, t):
                pool.wait_ge(alpha_done, u + 8 * (t + 1))
                by_head = o[:, t, :].rearrange("p (h d) -> p h d", d=DH)
                pool.tensor_tensor(by_head, by_head, alpha[:, t, :].unsqueeze(2).broadcast_to([P, H, DH]), ALU.mult)\
                    .then_inc(o_scaled, U // TT)
                ch.link(pool.tensor_tensor(total[:, t, :], total[:, t, :], alpha[:, t, :], ALU.mult))

            def chunk_body(ch, u, more):
                with pool.If(more):
                    ln = pool.snap(ln_reg)
                    root(ln, KT)
                    pool.reg_add(ln_reg, ln_reg, 1)
                pool.wait_ge(total_done, u)
                pool.wait_ge(back_done, u)
                rescale(ch, u, 0)
                rescale(ch, u, 1)
                for t in range(TT):
                    pool.wait_ge(p_ready, u + 8 * (t + 1))
                    pool.tensor_tensor(total[:, t, :], total[:, t, :], chunk_sum[:, t, :], ALU.add)\
                        .then_inc(total_done, U // TT)
                pool.reg_add(u_reg, u_reg, U)

            for n in range(2):
                root(n, B * TT)
            pool.wait_ge(lats_done, 1)
            pool.wait_ge(words_in, 16)
            with pool.Fori(1, B + 1) as turn:
                b = turn - 1
                ch = Chain(pool, pool_step, pool.snap(step_reg))
                u = pool.snap(u_reg)
                pool.wait_ge(inT_full, u)
                hold(pool, pool_held)
                pool.tensor_copy(lat[:, :, :], lats[:, bass.ds(b * TT, TT), :]).then_inc(lat_ready, 1)
                pool.wait_ge(fin_full, turn * 4)
                pool.wait_ge(fin_ready, turn * 2)
                hold(pool, pool_held)
                pool.memset(total[:, :, :], 0.0)
                ch.link(pool.memset(o[:, :, :], 0.0))
                bits = attended(pool, b)
                chunk_body(ch, u, bits > 0)
                pool.reg_add(step_reg, step_reg, ch.n)

                def step(c):
                    ch = Chain(pool, pool_step, pool.snap(step_reg))
                    u = pool.snap(u_reg)
                    chunk_body(ch, u, (bits >> c) > 1)
                    pool.reg_add(step_reg, step_reg, ch.n)
                chunks(pool, bits, step)


N_ROW_DMAS = 7 + KINDS


def linear_attention(k):
    nc, io = k.nc, k.io
    U = 16
    C = D
    with ExitStack() as ctx:
        sb = lambda name, shape, dt=F32: k.sb(name, shape, dt, ctx)
        wq = sb("lin_wq", [P, KD, C])
        wkv = sb("lin_wkv", [P, KD, 2, 2, C])
        wo = sb("lin_wo", [P, KD, C])
        bkv = sb("lin_bkv", [P, 2, 2, C])
        bo = sb("lin_bo", [P, C])
        xn = sb("lin_xn", [P, TT, C])
        xnT = sb("lin_xnT", [P, KD, T])
        qT = sb("lin_qT", [P, KD, T])
        kv = sb("lin_kv", [P, 2, TT, 2, C])
        state0 = sb("lin_state0", [P, KD, P])
        state = sb("lin_state", [P, KD, P])
        yn = sb("lin_yn", [P, TT, C])
        ynT = sb("lin_ynT", [P, KD, T])
        stats = sb("lin_stats", [P, TT, 6])
        mv = sb("lin_mv", [P, TT, 2])
        var = sb("lin_var", [P, TT])
        rstd = sb("lin_rstd", [P, TT])
        half = sb("lin_half", [P, TT])
        ps = k.banks("ps_lin", ctx)
        TURN, QUERY, KV, STATE, OUT, X = 0, 1, 2, 4, 5, 6

        sem = k.sem
        wq_in, wkv_in, wo_in, bias_in = sem("lin_wq_in"), sem("lin_wkv_in"), sem("lin_wo_in"), sem("lin_bias_in")
        xn_ready, xnT_full, xnT_done = sem("lin_xn_ready"), sem("lin_xnT_full"), sem("lin_xnT_done")
        q_full, q_done, kv_full, kv_done = sem("lin_q_full"), sem("lin_q_done"), sem("lin_kv_full"), sem("lin_kv_done")
        kv_read = sem("lin_kv_read")
        st_full, st_done, out_full = sem("lin_state_full"), sem("lin_state_done"), sem("lin_out_full")
        yn_ready, ynT_full, ynT_done = sem("lin_yn_ready"), sem("lin_ynT_full"), sem("lin_ynT_done")
        x_full, x_done = sem("lin_x_full"), sem("lin_x_done")
        ln_var, ln_rstd, dve_step, half_set, dve_held = sem("lin_ln_var"), sem("lin_ln_rstd"), sem("lin_dve_step"), sem("lin_half_set"), sem("lin_dve_held")

        block = ctx.enter_context(nc.Block())

        @block.sync
        def _(sp):
            begin_at(sp, U, (xn_ready, xnT_full, xnT_done, q_full, q_done, kv_full, kv_done, kv_read, st_full, st_done, out_full,
                             yn_ready, ynT_full, ynT_done, x_full, x_done))
            sp.dma_start(wq[:, :, :], io["attn_Wq"].rearrange("(k p) n -> p k n", p=P)).then_inc(wq_in, 16)
            for s in range(2):
                for n, name in enumerate(("k", "v")):
                    sp.dma_start(wkv[:, :, s, n, :], io[f"attn_W{name}"][s].rearrange("(k p) n -> p k n", p=P))\
                        .then_inc(wkv_in, 16)
                    sp.dma_start(bkv[:, s, n, :], io[f"attn_b{name}"][s:s + 1, :].broadcast_to([P, C])).then_inc(bias_in, 16)
            sp.dma_start(bo[:, :], io["attn_bo"].rearrange("(o n) -> o n", o=1).broadcast_to([P, C])).then_inc(bias_in, 16)
            sp.dma_start(wo[:, :, :], io["attn_Wo"].rearrange("(k p) n -> p k n", p=P)).then_inc(wo_in, 16)

        @block.tensor
        def _(pe):
            pe.wait_ge(wq_in, 16)
            pe.wait_ge(wkv_in, 64)
            pe.wait_ge(wo_in, 16)
            with pe.Fori(U, (B + 1) * U, U) as u:
                pe.wait_ge(xn_ready, u + U)
                pe.wait_ge(ynT_done, u)
                for kk in range(KD):
                    for t in range(TT):
                        ins = pe.transpose(ps[:, TURN, kk * T + t * P:kk * T + (t + 1) * P],
                                           xn[:, t, kk * P:(kk + 1) * P], k.ident)
                ins.then_inc(xnT_full, U)
                pe.wait_ge(xnT_done, u + U)
                pe.wait_ge(q_done, u)
                for m in range(KD):
                    for kk in range(KD):
                        ins = pe.matmul(ps[:, QUERY, m * T:(m + 1) * T], wq[:, kk, m * P:(m + 1) * P], xnT[:, kk, :],
                                        start=kk == 0, stop=kk == KD - 1)
                ins.then_inc(q_full, U)
                for s in range(2):
                    for t in range(TT):
                        j = s * TT + t
                        pe.wait_ge(kv_read, u + (4 * (j - 1) if j >= 2 else 0))
                        for kk in range(KD):
                            ins = pe.matmul(ps[:, KV + j % 2, :], xnT[:, kk, t * P:(t + 1) * P],
                                            wkv[:, kk, s, :, :].rearrange("p n c -> p (n c)"),
                                            start=kk == 0, stop=kk == KD - 1)
                        ins.then_inc(kv_full, 4)
                for s in range(2):
                    pe.wait_ge(kv_done, u + 8 * (s + 1))
                    for m in range(KD):
                        for t in range(TT):
                            ins = pe.matmul(ps[:, STATE, (s * KD + m) * P:(s * KD + m + 1) * P],
                                            kv[:, s, t, 0, m * P:(m + 1) * P], kv[:, s, t, 1, m * P:(m + 1) * P],
                                            start=t == 0, stop=t == TT - 1)
                ins.then_inc(st_full, U)
                pe.wait_ge(st_done, u + U)
                pe.wait_ge(q_done, u + U)
                for t in range(TT):
                    for m in range(KD):
                        ins = pe.matmul(ps[:, OUT, t * C + m * P:t * C + (m + 1) * P], qT[:, m, t * P:(t + 1) * P],
                                        state[:, m, :], start=True, stop=True)
                ins.then_inc(out_full, U)
                pe.wait_ge(yn_ready, u + U)
                for kk in range(KD):
                    for t in range(TT):
                        ins = pe.transpose(ps[:, TURN, kk * T + t * P:kk * T + (t + 1) * P],
                                           yn[:, t, kk * P:(kk + 1) * P], k.ident)
                ins.then_inc(ynT_full, U)
                pe.wait_ge(ynT_done, u + U)
                pe.wait_ge(x_done, u)
                for t in range(TT):
                    for kk in range(KD):
                        ins = pe.matmul(ps[:, X, t * C:(t + 1) * C], ynT[:, kk, t * P:(t + 1) * P], wo[:, kk, :],
                                        start=kk == 0, stop=kk == KD - 1)
                ins.then_inc(x_full, U)

        @block.scalar
        def _(act):
            with act.Fori(U, (B + 1) * U, U) as u:
                act.wait_ge(xnT_full, u + U)
                act.wait_ge(kv_full, u)
                act.wait_ge(q_done, u)
                act.activation(xnT[:, :, :], ps[:, TURN, :].rearrange("p (k t) -> p k t", k=KD), ACT.Copy).then_inc(xnT_done, U)
                act.wait_ge(ynT_full, u + U)
                for kk in range(KD):
                    ins = act.activation(ynT[:, kk, :], ps[:, TURN, kk * T:(kk + 1) * T], ACT.Identity,
                                         bias=k.cols[:, R_LB + kk:R_LB + kk + 1], scale=k.cols[:, R_LG + kk:R_LG + kk + 1])
                ins.then_inc(ynT_done, U)

        @block.vector
        def _(dve):
            STEPS = 9
            dve.wait_ge(bias_in, 80)
            with dve.Fori(0, B) as b:
                u = (b + 1) * U
                ch = Chain(dve, dve_step, b * STEPS)
                xt = lambda t: k.x[:, bass.ds(b * TT + t, 1), :].rearrange("p o d -> p (o d)")
                both = k.x[:, bass.ds(b * TT, TT), :]

                def norm(src, dst, n):
                    hold(dve, dve_held)
                    for t in range(TT):
                        ins = dve.bn_stats(stats[:, t, :], src(t))
                    ch.link(ins)
                    hold(dve, dve_held)
                    for t in range(TT):
                        ins = dve.bn_aggr(mv[:, t, :], stats[:, t, :])
                    ch.link(ins)
                    dve.tensor_scalar(var[:, :], mv[:, :, 1], EPS, None, ALU.add).then_inc(ln_var, 1)
                    dve.wait_ge(ln_rstd, b * 3 + n + 1)
                    for t in range(TT):
                        ins = dve.tensor_scalar(dst(t), src(t), mv[:, t, 0:1], rstd[:, t:t + 1], ALU.subtract, ALU.mult)
                    return ins

                dve.wait_ge(xnT_full, u)
                norm(xt, lambda t: xn[:, t, :], 0).then_inc(xn_ready, U)
                dve.wait_ge(xn_ready, u + U)
                dve.wait_ge(q_full, u + U)
                dve.wait_ge(xnT_done, u + U)
                dve.wait_ge(out_full, u)
                for m in range(KD):
                    ins = dve.scalar_tensor_tensor(out=qT[:, m, :], in0=ps[:, QUERY, m * T:(m + 1) * T],
                                                   scalar=k.cols[:, R_BQ + m:R_BQ + m + 1], in1=xnT[:, m, :],
                                                   op0=ALU.add, op1=ALU.add)
                ins.then_inc(q_done, U)
                dve.wait_ge(st_full, u)
                for s in range(2):
                    for t in range(TT):
                        j = s * TT + t
                        dve.wait_ge(kv_full, u + 4 * (j + 1))
                        dve.tensor_tensor(kv[:, s, t, :, :].rearrange("p n c -> p (n c)"), ps[:, KV + j % 2, :],
                                          bkv[:, s, :, :].rearrange("p n c -> p (n c)"), ALU.add).then_inc(kv_read, 4)
                        dve.wait_ge(kv_read, u + 4 * (j + 1))
                        dve.tensor_tensor(kv[:, s, t, :, :], kv[:, s, t, :, :],
                                          xn[:, t, :].unsqueeze(1).broadcast_to([P, 2, C]), ALU.add).then_inc(kv_done, 4)
                dve.wait_ge(st_full, u + U)
                block_mask = k.const[:, C_BLOCK:C_BLOCK + P].unsqueeze(1).broadcast_to([P, KD, P])
                ch.link(dve.tensor_tensor(state0[:, :, :], ps[:, STATE, 0:KD * P].rearrange("p (m e) -> p m e", m=KD),
                                          block_mask, ALU.mult))
                dve.tensor_tensor(state[:, :, :], ps[:, STATE, KD * P:2 * KD * P].rearrange("p (m e) -> p m e", m=KD),
                                  state0[:, :, :], ALU.mult).then_inc(st_done, U)
                dve.wait_ge(out_full, u + U)
                norm(lambda t: ps[:, OUT, t * C:(t + 1) * C], lambda t: yn[:, t, :], 1).then_inc(yn_ready, U)
                ch.link(dve.tensor_tensor(both, both, bo[:, :].unsqueeze(1).broadcast_to([P, TT, C]), ALU.add))
                dve.wait_ge(x_full, u + U)
                dve.tensor_tensor(both, ps[:, X, :].rearrange("p (t c) -> p t c", t=TT), both, ALU.add).then_inc(x_done, U)
                dve.wait_ge(x_done, u + U)
                ch.link(norm(xt, lambda t: k.y[:, bass.ds(b * TT + t, 1), :].rearrange("p o d -> p (o d)"), 2))
                assert ch.n == STEPS

        @block.gpsimd
        def _(pool):
            pool.memset(half[:, :], -0.5).then_inc(half_set, 1)
            pool.wait_ge(half_set, 1)
            with pool.Fori(0, B * 3) as n:
                pool.wait_ge(ln_var, n + 1)
                pool.tensor_tensor(rstd[:, :], var[:, :], half[:, :], ALU.pow).then_inc(ln_rstd, 1)




def local_layers(k):
    nc, io = k.nc, k.io
    U = 16
    LAYER = B * U
    AHEAD = 4
    SLOTS = 12
    with ExitStack() as ctx:
        sb = lambda name, shape, dt=F32: k.sb(name, shape, dt, ctx)
        wqkv = sb("wqkv", [P, KD, 3 * INNER])
        wo = sb("wo", [P, PAIRS, D])
        w1 = sb("w1", [P, KD, 2 * FF])
        w2 = sb("w2", [P, FM, D])
        b2 = sb("b2", [P, LAYERS, D])
        head_scale = sb("head_scale", [P, LAYERS, 2, DH])
        cos = sb("cos", [P, TT, 2, DH])
        sin = sb("sin", [P, TT, 2, DH])
        vec = sb("vec", [P, KINDS])
        xT = sb("xT", [P, KD, T])
        qk = sb("qk", [P, TT, 2 * INNER])
        v = sb("v_loc", [P, 2, TT, INNER])
        work = sb("work", [P, 2, 2 * INNER])
        square = work[:, 0, :]
        twist = work[:, 1, :]
        norm2 = sb("norm2", [P, 2 * H])
        norm2_floor = sb("norm2_floor", [P, 2 * H])
        half = sb("half_loc", [P, 2 * H])
        rnorm = sb("rnorm", [P, 2, TT, 2 * H])
        qT = sb("qT_loc", [P, PAIRS, T])
        kT = sb("kT_loc", [P, PAIRS, 2, T])
        prob0 = sb("prob0", [P, H, P])
        uT = (qT[:, 0:FM, :], prob0[:, 0:2 * FM, :].rearrange("p (m a) t -> p m (a t)", a=2))
        prob1 = sb("prob1", [P, H, T])
        top = sb("top_loc", [P, TT, H])
        total = sb("total_loc", [P, TT, H])
        rtotal = sb("rtotal_loc", [P, TT, H])
        pT = sb("pT", [P, 2, 2 * T + 2 * P])
        oT = sb("oT_loc", [P, PAIRS, T])
        late = sb("late", [P, B * TT, P])
        xn = sb("xn_loc", [P, TT, D])
        xnT = sb("xnT_loc", [P, 2, KD, T])
        stats = sb("stats_loc", [P, TT, 2, 6])
        mv = sb("mv_loc", [P, TT, 2])
        var = sb("var_loc", [P, TT])
        rstd = sb("rstd_loc", [P, TT])
        gate = sb("gate", [P, 2, T])
        ps = k.banks("ps_loc", ctx)
        PROJ, PAIR, SCORE, TURN = 0, 2, 4, 6
        TURN_QK = (PAIR, PAIR + 1, TURN, TURN + 1)

        sem = k.sem
        wqkv_in, wo_in, w1_in, w2_in = sem("wqkv_in"), sem("wo_in"), sem("w1_in"), sem("w2_in")
        b2_in, scale_in, zeros_set = sem("b2_in"), sem("scale_in"), sem("zeros_set")
        tables_done, vec_done = sem("tables_done"), sem("vec_done")
        xT_full, xT_done, qkv_full, qkv_done = sem("xT_full"), sem("xT_done"), sem("qkv_full"), sem("qkv_done")
        square_done, norm2_done, floor_done, rnorm_done = sem("square_done"), sem("norm2_done"), sem("floor_done"), sem("rnorm_done")
        twist_done, cos_done, sum_done, rope_done = sem("twist_done"), sem("cos_done"), sem("sum_done"), sem("rope_done")
        qk_full, qk_done, k1_done = sem("qk_full"), sem("qk_done"), sem("k1_done")
        s_full, s_read, exp_done = sem("loc_s_full"), sem("loc_s_read"), sem("exp_done")
        rtotal_done, p_done, dve_held = sem("rtotal_done"), sem("p_done"), sem("loc_dve_held")
        pT_full, pT_done, o_full, o_done = sem("loc_pT_full"), sem("loc_pT_done"), sem("loc_o_full"), sem("loc_o_done")
        y_full, y_mid, y_out = sem("y_full"), sem("y_mid"), sem("y_out")
        late_in, edge_in = [sem(f"late_in{b}") for b in range(B)], [sem(f"edge_in{b}") for b in range(B)]
        bn_done, ln_stats, ln_var, ln_rstd, xn_done = sem("bn_done"), sem("loc_ln_stats"), sem("loc_ln_var"), sem("loc_ln_rstd"), sem("xn_done")
        xnT_full, xnT_done = sem("xnT_full"), sem("xnT_done")
        f_full, gate_done, u_done = sem("f_full"), sem("gate_done"), sem("u_done")
        f2_full, b2_done, x_sum = sem("f2_full"), sem("b2_done"), sem("x_sum")

        def after(n, last):
            return n + 1 if n < last else U

        def wide_bank(b, m):
            return (PAIR, PAIR + 1, TURN, TURN + 1, PROJ + 1, PROJ)[m] if b == 0 else PAIR + m % 2

        def weights(sp, i, which):
            if which == "qkv":
                src = io["ffn_Wqkv"].rearrange("i (k p) n -> i p k n", p=P)
                for kk in range(KD):
                    for j in range(2):
                        cut = slice(j * 3 * INNER // 2, (j + 1) * 3 * INNER // 2)
                        sp.dma_start(wqkv[:, kk, cut], src[bass.ds(i, 1), :, kk, cut].rearrange("o p n -> (o p) n"))\
                            .then_inc(wqkv_in, 16)
            elif which == "wo":
                src = io["ffn_Wo"].rearrange("i (k p) n -> i p k n", p=P)
                for j in range(4):
                    sp.dma_start(wo[:, 2 * j:2 * j + 2, :], src[bass.ds(i, 1), :, 2 * j:2 * j + 2, :].rearrange("o p k n -> (o p) k n"))\
                        .then_inc(wo_in, 16)
            elif which == "w1":
                src = io["ffn_W1"].rearrange("i (k p) n -> i p k n", p=P)
                for kk in range(KD):
                    for j in range(2):
                        sp.dma_start(w1[:, kk, j * FF:(j + 1) * FF], src[bass.ds(i, 1), :, kk, j * FF:(j + 1) * FF].rearrange("o p n -> (o p) n"))\
                            .then_inc(w1_in, 16)
            else:
                for m0, m1 in ((0, 2), (2, 4), (4, 5), (5, 6)):
                    src = io["ffn_W2"][bass.ds(i, 1), FAT[m0]:FAT[m1 - 1] + FWIDE[m1 - 1], :]
                    sp.dma_start(w2[0:FWIDE[m0], m0:m1, :], src.rearrange("o (m p) n -> (o p) m n", p=FWIDE[m0])).then_inc(w2_in, 16)

        block = ctx.enter_context(nc.Block())

        @block.sync
        def _(sp):
            begin_at(sp, LAYER, (vec_done, tables_done, xT_full, xT_done, qkv_full, qkv_done, square_done, norm2_done, floor_done,
                                 rnorm_done, twist_done, cos_done, sum_done, rope_done, qk_full, qk_done, k1_done, s_full, s_read, exp_done,
                                 rtotal_done, p_done, pT_full, pT_done, o_full, o_done, y_full, y_mid, bn_done, ln_stats,
                                 ln_var, ln_rstd, xn_done, xnT_full, xnT_done, f_full, gate_done, u_done, f2_full, b2_done,
                                 wqkv_in, wo_in, w1_in, w2_in))
            begin_at(sp, 2 * LAYER, (y_out,))
            sp.wait_ge(zeros_set, 1)
            for which in ("qkv", "wo", "w1", "w2"):
                weights(sp, 0, which)
            for n, name in enumerate(("q", "k")):
                sp.dma_start(head_scale[:, :, n, :], io[f"ffn_{name}_scale"].rearrange("(o i) d -> o i d", o=1).broadcast_to([P, LAYERS, DH]))\
                    .then_inc(scale_in, 16)
            sp.dma_start(b2[:, :, :], io["ffn_b2"].rearrange("(o i) d -> o i d", o=1).broadcast_to([P, LAYERS, D])).then_inc(b2_in, 16)

            def shift(L, b):
                sp.wait_ge(y_mid, L + U * (b + 1))
                sp.dma_start(late[1:P, b * TT:(b + 1) * TT, :], k.y[0:P - 1, b * TT:(b + 1) * TT, P:D]).then_inc(late_in[b], 16)
                sp.dma_start(late[0:1, b * TT + 1, :], k.y[P - 1:P, b * TT, P:D]).then_inc(edge_in[b], 16)

            with sp.Fori(0, LAYERS - 1) as i:
                L = sp.snap(i * LAYER + LAYER)
                shift(L, 0)
                shift(L, 1)
                sp.wait_ge(qkv_full, L + LAYER)
                weights(sp, i + 1, "qkv")
                shift(L, 2)
                shift(L, 3)
                weights(sp, i + 1, "wo")
                sp.wait_ge(f_full, L + LAYER)
                weights(sp, i + 1, "w1")
                sp.wait_ge(f2_full, L + LAYER)
                weights(sp, i + 1, "w2")
            for b in range(B):
                shift(LAYERS * LAYER, b)

        @block.tensor
        def _(pe):
            def turn_x(L, b):
                pe.wait_ge(y_out, L + U * (b + 1))
                pe.wait_ge(qkv_done, L + U * b)
                if b == 0:
                    pe.wait_ge(xnT_done, L - U)
                for kk in range(KD):
                    for t in range(TT):
                        ins = pe.transpose(ps[:, PROJ, kk * T + t * P:kk * T + (t + 1) * P],
                                           k.y[:, b * TT + t, kk * P:(kk + 1) * P], k.ident)
                ins.then_inc(xT_full, U)

            def project(L, b, j):
                if j == 0:
                    if b == 0:
                        pe.wait_ge(wqkv_in, L + LAYER)
                        pe.wait_ge(xnT_done, L)
                    pe.wait_ge(xT_done, L + U * (b + 1))
                t, part = divmod(j, 4) if j < 8 else divmod(j - 8, 2)
                col = part * 512 if j < 8 else 2 * INNER + part * 512
                if j >= 2:
                    pe.wait_ge(qkv_done, L + U * b + j - 1)
                for kk in range(KD):
                    ins = pe.matmul(ps[:, PROJ + j % 2, :], xT[:, kk, t * P:(t + 1) * P], wqkv[:, kk, col:col + 512],
                                    start=kk == 0, stop=kk == KD - 1)
                ins.then_inc(qkv_full, 1 if j < SLOTS - 1 else U - SLOTS + 1)

            def turn_qk(L, b):
                pe.wait_ge(rope_done, L + U * (b + 1))
                pe.wait_ge(o_done, L + U * b)
                pe.wait_ge(pT_done, L + U * b)
                if b == 0:
                    pe.wait_ge(u_done, L)
                for g in range(8):
                    two, s = divmod(g, 2)
                    if g >= 4:
                        pe.wait_ge(qk_done, L + U * b + 2 * (g - 3))
                        if s:
                            pe.wait_ge(k1_done, L + U * b + 4 * (two - 1))
                    for i in range(2):
                        for t in range(TT):
                            col = s * INNER + (2 * two + i) * P
                            ins = pe.transpose(ps[:, TURN_QK[g % 4], i * T + t * P:i * T + (t + 1) * P],
                                               qk[:, t, col:col + P], k.ident)
                    ins.then_inc(qk_full, 2)

            def scores(L, b, s):
                pair, t = divmod(s, TT)
                if s == 0:
                    pe.wait_ge(y_mid, L + U * min(b, B - 2))
                    pe.wait_ge(y_out, L + LAYER)
                if s % (2 * TT) == 0:
                    pe.wait_ge(qk_done, L + U * b + 4 * (pair // 2 + 1))
                    pe.wait_ge(k1_done, L + U * b + 4 * (pair // 2 + 1))
                pe.wait_ge(s_read, L + U * b + (s - 1 if s >= 2 else 0))
                k0, k1 = (0, P) if t == 0 else (WINDOW, T)
                pe.matmul(ps[:, SCORE + t, 0:2 * (k1 - k0)], qT[:, pair, t * P:(t + 1) * P], kT[:, pair, :, k0:k1],
                          start=True, stop=True).then_inc(s_full, 1)

            def out(L, b, pair):
                pe.wait_ge(pT_done, L + U * b + 2 * pair + 2)
                pe.wait_ge(o_done, L + U * b + (2 * (pair - 1) if pair >= 2 else 0))
                for i in range(2):
                    col = (2 * pair + i) * DH
                    pe.matmul(ps[i * DH:(i + 1) * DH, PAIR + pair % 2, 0:T], v[:, b % 2, 0, col:col + DH],
                              pT[:, pair % 2, i * T:(i + 1) * T], start=True, stop=False)
                for i in range(2):
                    col = (2 * pair + i) * DH
                    ins = pe.matmul(ps[i * DH:(i + 1) * DH, PAIR + pair % 2, P:T], v[:, b % 2, 1, col:col + DH],
                                    pT[:, pair % 2, 2 * T + i * P:2 * T + (i + 1) * P], start=False, stop=True)
                ins.then_inc(o_full, 2)

            def weigh(L, b, pair):
                if pair == 0:
                    pe.wait_ge(qk_done, L + U * (b + 1))
                    pe.wait_ge(k1_done, L + U * (b + 1))
                    pe.wait_ge(u_done, L + (U if b == B - 1 else 0))
                    pe.wait_ge(qkv_done, L + U * (b + 1))
                pe.wait_ge(p_done, L + U * b + 2 * pair + 2)
                pe.wait_ge(pT_done, L + U * b + max(2 * pair - 1, 0))
                for i in range(2):
                    h = 2 * pair + i
                    pe.transpose(ps[:, TURN, i * T:i * T + P], prob0[:, h, :], k.ident)
                    ins = pe.transpose(ps[:, TURN, i * T + P:(i + 1) * T], prob1[:, h, 0:P], k.ident)
                ins.then_inc(pT_full, 1)
                pe.wait_ge(pT_done, L + U * b + 2 * pair)
                for i in range(2):
                    ins = pe.transpose(ps[:, TURN + 1, i * P:(i + 1) * P], prob1[:, 2 * pair + i, P:T], k.ident)
                ins.then_inc(pT_full, 1)
                if pair:
                    out(L, b, pair - 1)

            def project_out(L, b):
                if b == 0:
                    pe.wait_ge(wo_in, L + LAYER)
                pe.wait_ge(s_read, L + U * (b + 1 if b < B - 2 else B))
                if b == B - 1:
                    pe.wait_ge(y_mid, L + U * b)
                for pairs in (range(PAIRS - 1), (PAIRS - 1,)):
                    for t in range(TT):
                        for pair in pairs:
                            if t == 0:
                                pe.wait_ge(o_done, L + U * b + 2 * (pair + 1))
                            ins = pe.matmul(ps[:, SCORE + t, 0:D], oT[:, pair, t * P:(t + 1) * P], wo[:, pair, :],
                                            start=pair == 0, stop=pair == PAIRS - 1)
                ins.then_inc(y_full, U)

            def turn_xn(L, b):
                pe.wait_ge(xn_done, L + U * (b + 1))
                pe.wait_ge(qkv_done, L + LAYER)
                if b:
                    pe.wait_ge(u_done, L + U)
                if b >= 2:
                    pe.wait_ge(xnT_done, L + U * (b - 1))
                for kk in range(KD):
                    for t in range(TT):
                        ins = pe.transpose(ps[:, PROJ + b % 2, kk * T + t * P:kk * T + (t + 1) * P],
                                           xn[:, t, kk * P:(kk + 1) * P], k.ident)
                ins.then_inc(xnT_full, U)

            def widen(L, b, m):
                n = FWIDE[m]
                if m == 0:
                    if b == 0:
                        pe.wait_ge(w1_in, L + LAYER)
                        pe.wait_ge(qk_done, L + LAYER)
                        pe.wait_ge(k1_done, L + LAYER)
                    else:
                        pe.wait_ge(o_done, L + LAYER)
                    pe.wait_ge(xnT_done, L + U * (b + 1))
                if b:
                    pe.wait_ge(u_done, L + U * b + (m - 1 if m >= 2 else 0))
                for part in range(2):
                    for kk in range(KD):
                        ins = pe.matmul(ps[0:n, wide_bank(b, m), part * T:(part + 1) * T],
                                        w1[:, kk, part * FF + FAT[m]:part * FF + FAT[m] + n], xnT[:, b % 2, kk, :],
                                        start=kk == 0, stop=kk == KD - 1)
                ins.then_inc(f_full, 1 if m < FM - 1 else U - FM + 1)

            def narrow(L, b):
                if b == 0:
                    pe.wait_ge(w2_in, L + LAYER)
                pe.wait_ge(u_done, L + U * (b + 1))
                pe.wait_ge(y_mid, L + LAYER)
                if b >= 2:
                    pe.wait_ge(y_out, L + LAYER + U * (b - 1))
                for t in range(TT):
                    for m in range(FM):
                        ins = pe.matmul(ps[:, SCORE + b % 2, t * D:(t + 1) * D], uT[b % 2][0:FWIDE[m], m, t * P:(t + 1) * P], w2[0:FWIDE[m], m, :],
                                        start=m == 0, stop=m == FM - 1)
                ins.then_inc(f2_full, U)

            def weigh_all(L, b):
                for pair in range(PAIRS):
                    weigh(L, b, pair)
                out(L, b, PAIRS - 1)

            def widen_all(L, b):
                for m in range(FM):
                    widen(L, b, m)

            def layer(L, last):
                for b in range(B):
                    if b:
                        weigh_all(L, b - 1)
                    if 0 < b < B - 1:
                        project_out(L, b - 1)
                    turn_qk(L, b)
                    if b < B - 1:
                        turn_x(L, b + 1)
                        for s in range(U):
                            scores(L, b, s)
                            if 0 <= s - AHEAD < SLOTS:
                                project(L, b + 1, s - AHEAD)
                    else:
                        turn_xn(L, 0)
                        for s in range(U):
                            scores(L, b, s)
                            if s % 2 and s < 2 * FM:
                                widen(L, 0, s // 2)
                project_out(L, B - 2)
                turn_xn(L, 1)
                weigh_all(L, B - 1)
                project_out(L, B - 1)
                widen_all(L, 1)
                turn_xn(L, 2)
                narrow(L, 0)
                widen_all(L, 2)
                turn_xn(L, 3)
                if not last:
                    turn_x(L + LAYER, 0)
                narrow(L, 1)
                if not last:
                    for j in range(SLOTS):
                        project(L + LAYER, 0, j)
                widen_all(L, 3)
                narrow(L, 2)
                narrow(L, 3)

            turn_x(LAYER, 0)
            for j in range(SLOTS):
                project(LAYER, 0, j)
            with pe.Fori(0, LAYERS - 1) as i:
                layer(pe.snap(i * LAYER + LAYER), False)
            layer(LAYERS * LAYER, True)

        @block.scalar
        def _(act):
            def x_out(L, b):
                act.wait_ge(qkv_full, L + U * b)
                act.wait_ge(xT_full, L + U * (b + 1))
                act.activation(xT[:, 0, :], ps[:, PROJ, 0:T], ACT.Copy)
                act.activation(xT[:, 1, 1:T], ps[:, PROJ, T:2 * T - 1], ACT.Copy).then_inc(xT_done, U)

            def qkv_out(L, b, j):
                if j == 0:
                    act.wait_ge(qk_full, L + U * b)
                    act.wait_ge(o_full, L + U * max(b - 1, 0))
                act.wait_ge(qkv_full, L + U * b + after(j, SLOTS - 1))
                t, part = divmod(j, 4) if j < 8 else divmod(j - 8, 2)
                dst = qk[:, t, part * 512:(part + 1) * 512] if j < 8 else v[:, b % 2, t, part * 512:(part + 1) * 512]
                act.activation(dst, ps[:, PROJ + j % 2, :], ACT.Copy).then_inc(qkv_done, 1 if j < SLOTS - 1 else U - SLOTS + 1)
                if j in (3, 7):
                    act.wait_ge(qkv_done, L + U * b + j + 1)
                    act.wait_ge(norm2_done, L + U * b + 8 * t)
                    act.activation(square, qk[:, t, :], ACT.Square).then_inc(square_done, 8)

            def qk_out(L, b):
                act.wait_ge(s_full, L + U * b)
                if b == 0:
                    act.wait_ge(f2_full, L - U)
                for g in range(8):
                    two, s = divmod(g, 2)
                    act.wait_ge(qk_full, L + U * b + 2 * (g + 1))
                    bank = ps[:, TURN_QK[g % 4], :].rearrange("p (i t) -> p i t", i=2)
                    if s == 0:
                        ins = act.activation(qT[:, 2 * two:2 * two + 2, :], bank, ACT.Copy)
                    else:
                        ins = act.activation(kT[0:DH, 2 * two:2 * two + 2, 0, :], bank[0:DH], ACT.Copy)
                    ins.then_inc(qk_done, 2)

            def exps(L, b, s):
                pair, t = divmod(s, TT)
                act.wait_ge(s_read, L + U * b + s + 1)
                for h in (2 * pair, 2 * pair + 1):
                    pr = prob0[:, h, :] if t == 0 else prob1[:, h, WINDOW:T]
                    ins = act.activation(pr, pr, ACT.Exp, bias=top[:, t, h:h + 1], scale=-1.0, accum_out=total[:, t, h:h + 1])
                ins.then_inc(exp_done, 1)

            def o_out(L, b, pair):
                act.wait_ge(o_full, L + U * b + 2 * (pair + 1))
                act.activation(oT[:, pair, :], ps[:, PAIR + pair % 2, 0:T], ACT.Copy).then_inc(o_done, 2)

            def weigh_out(L, b, pair):
                if pair == 0:
                    act.wait_ge(y_full, L + U * b)
                act.wait_ge(o_full, L + U * b + (2 * (pair - 1) if pair >= 2 else 0))
                act.wait_ge(pT_full, L + U * b + 2 * pair + 1)
                act.activation(pT[:, pair % 2, 0:2 * T], ps[:, TURN, :], ACT.Copy).then_inc(pT_done, 1)
                act.wait_ge(pT_full, L + U * b + 2 * pair + 2)
                act.activation(pT[:, pair % 2, 2 * T:], ps[:, TURN + 1, 0:2 * P], ACT.Copy).then_inc(pT_done, 1)
                if pair:
                    o_out(L, b, pair - 1)

            def widen_in(L, b):
                if b == 0:
                    act.wait_ge(vec_done, L + LAYER)
                act.wait_ge(f_full, L + U * max(b - 1, 0))
                act.wait_ge(xnT_full, L + U * (b + 1))
                for kk in range(KD):
                    ins = act.activation(xnT[:, b % 2, kk, :], ps[:, PROJ + b % 2, kk * T:(kk + 1) * T], ACT.Identity,
                                         bias=vec[:, V_FB + kk:V_FB + kk + 1], scale=vec[:, V_FG + kk:V_FG + kk + 1])
                ins.then_inc(xnT_done, U)

            def gates(L, b):
                for m in range(FM):
                    n = FWIDE[m]
                    if b == 0 and m >= 2:
                        act.wait_ge(u_done, L + m - 1)
                    act.wait_ge(f_full, L + U * b + after(m, FM - 1))
                    act.activation(gate[0:n, m % 2, :], ps[0:n, wide_bank(b, m), T:2 * T], ACT.Gelu,
                                   bias=vec[0:n, V_B1G + m:V_B1G + m + 1]).then_inc(gate_done, 1 if m < FM - 1 else U - FM + 1)

            def first(L):
                x_out(L, 0)
                for j in range(SLOTS):
                    qkv_out(L, 0, j)

            def weigh_out_all(L, b):
                for pair in range(PAIRS):
                    weigh_out(L, b, pair)
                o_out(L, b, PAIRS - 1)

            def layer(L, last):
                for b in range(B):
                    if b:
                        weigh_out_all(L, b - 1)
                    qk_out(L, b)
                    if b < B - 1:
                        x_out(L, b + 1)
                    else:
                        widen_in(L, 0)
                    for s in range(U):
                        exps(L, b, s)
                        if b < B - 1 and 0 <= s - AHEAD < SLOTS:
                            qkv_out(L, b + 1, s - AHEAD)
                gates(L, 0)
                widen_in(L, 1)
                weigh_out_all(L, B - 1)
                gates(L, 1)
                widen_in(L, 2)
                gates(L, 2)
                widen_in(L, 3)
                if not last:
                    first(L + LAYER)
                gates(L, 3)

            act.wait_ge(zeros_set, 1)
            first(LAYER)
            with act.Fori(0, LAYERS - 1) as i:
                layer(act.snap(i * LAYER + LAYER), False)
            layer(LAYERS * LAYER, True)

        @block.vector
        def _(dve):
            def rotate(L, b, t, step):
                at = L + U * b + 8 * t
                by_head = qk[:, t, :].rearrange("p (s h d) -> p s h d", s=2, d=DH)
                if step == 0:
                    dve.wait_ge(square_done, at + 8)
                    dve.wait_ge(rnorm_done, at)
                    dve.tensor_reduce(norm2[:, :], square.rearrange("p (h d) -> p h d", d=DH), AX.X, ALU.add)\
                        .then_inc(norm2_done, 8)
                    dve.wait_ge(norm2_done, at + 8)
                    dve.tensor_scalar(norm2_floor[:, :], norm2[:, :], 1e-24, None, ALU.max).then_inc(floor_done, 8)
                elif step == 1:
                    dve.wait_ge(tables_done, L + LAYER)
                    dve.wait_ge(sum_done, at)
                    to_head = twist.rearrange("p (s h d) -> p s h d", s=2, d=DH)
                    lo, hi = slice(0, DH // 2), slice(DH // 2, DH)
                    for dst, src in ((lo, hi), (hi, lo)):
                        ins = dve.tensor_tensor(to_head[:, :, :, dst], by_head[:, :, :, src],
                                                sin[:, t, :, dst].unsqueeze(2).broadcast_to([P, 2, H, DH // 2]), ALU.mult)
                    ins.then_inc(twist_done, 8)
                else:
                    dve.wait_ge(twist_done, at + 8)
                    dve.tensor_tensor(by_head, by_head, cos[:, t, :, :].unsqueeze(2).broadcast_to([P, 2, H, DH]), ALU.mult)\
                        .then_inc(cos_done, 8)

            def k1_out(L, b):
                dve.wait_ge(s_full, L + U * b)
                for two in range(4):
                    dve.wait_ge(qk_full, L + U * b + 4 * (two + 1))
                    bank = ps[DH:P, TURN_QK[(2 * two + 1) % 4], :].rearrange("p (i t) -> p i t", i=2)
                    dve.tensor_copy(kT[DH:P, 2 * two:2 * two + 2, 1, :], bank).then_inc(k1_done, 4)

            def softmax(L, b):
                def share(s):
                    if s < U:
                        pair, t = divmod(s, TT)
                        h = 2 * pair
                        dve.wait_ge(exp_done, L + U * b + s + 1)
                        dve.reciprocal(rtotal[:, t, h:h + 2], total[:, t, h:h + 2]).then_inc(rtotal_done, 1)
                    if s:
                        pair, t = divmod(s - 1, TT)
                        h = 2 * pair
                        dve.wait_ge(rtotal_done, L + U * b + s)
                        for n in range(2):
                            pr = prob0[:, h + n, :] if t == 0 else prob1[:, h + n, WINDOW:T]
                            ins = dve.tensor_scalar(pr, pr, rtotal[:, t, h + n:h + n + 1], None, ALU.mult)
                        ins.then_inc(p_done, 1)

                LAG = 3
                dve.wait_ge(rnorm_done, L + U * (b + 1))
                if b == 0:
                    dve.wait_ge(pT_full, L)
                    dve.wait_ge(f2_full, L)
                between = {9: (0, 0), 11: (0, 1), 13: (0, 2)} if b < B - 1 else {}
                for s in range(U):
                    pair, t = divmod(s, TT)
                    if b and t == 0:
                        dve.wait_ge(pT_full, L + U * (b - 1) + 2 * (pair + 1))
                    n = P if t == 0 else T - WINDOW
                    band = k.const[:, C_BAND0:C_BAND0 + n] if t == 0 else k.const[:, C_BAND1:C_BAND1 + n]
                    dve.wait_ge(s_full, L + U * b + s + 1)
                    hold(dve, dve_held)
                    for e in range(2):
                        h = 2 * pair + e
                        ins = dve.tensor_tensor_reduce(
                            out=prob0[:, h, :] if t == 0 else prob1[:, h, WINDOW:T],
                            in0=ps[:, SCORE + t, e * n:(e + 1) * n], in1=band, scale=rnorm[:, b % 2, t, h:h + 1],
                            scalar=FAR, op0=ALU.add, op1=ALU.min, accum_out=top[:, t, h:h + 1])
                    ins.then_inc(s_read, 1)
                    if s >= LAG:
                        share(s - LAG)
                    if s in between:
                        rotate(L, b + 1, *between[s])
                for s in range(U - LAG, U + 1):
                    share(s)
                if b < B - 1:
                    for t in range(TT):
                        for step in range(3):
                            if (t, step) not in between.values():
                                rotate(L, b + 1, t, step)

            def add_attention(L, b):
                dve.wait_ge(y_full, L + U * (b + 1))
                both = k.y[:, b * TT:(b + 1) * TT, :]
                dve.tensor_tensor(both, ps[:, SCORE:SCORE + TT, 0:D], both, ALU.add).then_inc(y_mid, U)

            def norm(L, shifts, b):
                dve.wait_ge(y_mid, L + U * (b + 1))
                dve.wait_ge(late_in[b], shifts)
                dve.wait_ge(edge_in[b], shifts)
                dve.wait_ge(xnT_full, L + U * b)
                halves = lambda t: (k.y[:, b * TT + t, 0:P], late[:, b * TT + t, :])
                for t in range(TT):
                    for n, part in enumerate(halves(t)):
                        ins = dve.bn_stats(stats[:, t, n, :], part)
                ins.then_inc(bn_done, U)
                dve.wait_ge(bn_done, L + U * (b + 1))
                hold(dve, dve_held)
                for t in range(TT):
                    ins = dve.bn_aggr(mv[:, t, :], stats[:, t, :, :].rearrange("p n s -> p (n s)"))
                ins.then_inc(ln_stats, U)
                dve.wait_ge(ln_stats, L + U * (b + 1))
                dve.tensor_scalar(var[:, :], mv[:, :, 1], EPS, None, ALU.add).then_inc(ln_var, U)
                dve.wait_ge(ln_rstd, L + U * (b + 1))
                for t in range(TT):
                    for n, part in enumerate(halves(t)):
                        ins = dve.tensor_scalar(xn[:, t, n * P:(n + 1) * P], part, mv[:, t, 0:1], rstd[:, t:t + 1],
                                                ALU.subtract, ALU.mult)
                ins.then_inc(xn_done, U)

            def gated(L, b):
                if b >= 2:
                    dve.wait_ge(f2_full, L + U * (b - 1))
                elif b == 1:
                    dve.wait_ge(pT_full, L + LAYER)
                else:
                    dve.wait_ge(s_full, L + LAYER)
                for m in range(FM):
                    n = FWIDE[m]
                    dve.wait_ge(gate_done, L + U * b + after(m, FM - 1))
                    dve.scalar_tensor_tensor(out=uT[b % 2][0:n, m, :], in0=ps[0:n, wide_bank(b, m), 0:T],
                                             scalar=vec[0:n, V_B1A + m:V_B1A + m + 1], in1=gate[0:n, m % 2, :],
                                             op0=ALU.add, op1=ALU.mult).then_inc(u_done, 1 if m < FM - 1 else U - FM + 1)

            def add_ffn(L, b):
                dve.wait_ge(b2_done, L + U * (b + 1))
                dve.wait_ge(f2_full, L + U * (b + 1))
                both = k.y[:, b * TT:(b + 1) * TT, :]
                dve.tensor_tensor(both, ps[:, SCORE + b % 2, :].rearrange("p (t c) -> p t c", t=TT), both, ALU.add).then_inc(y_out, U)

            dve.wait_ge(zeros_set, 1)
            def first(L):
                for t in range(TT):
                    for step in range(3):
                        rotate(L, 0, t, step)

            def layer(i, L, shifts, last):
                dve.wait_ge(gate_done, L)
                dve.wait_ge(u_done, L)
                kinds = k.cols[:, R_LAYER:ROWS].rearrange("p (v i) -> p v i", i=LAYERS)
                dve.tensor_copy(vec[:, :], kinds[:, :, bass.ds(i, 1)].rearrange("p v o -> p (v o)")).then_inc(vec_done, LAYER)
                dve.wait_ge(vec_done, L + LAYER)
                for b in range(B):
                    if 0 < b < B - 1:
                        add_attention(L, b - 1)
                    if b == B - 1:
                        norm(L, shifts, 0)
                    k1_out(L, b)
                    softmax(L, b)
                gated(L, 0)
                norm(L, shifts, 1)
                add_attention(L, B - 2)
                add_attention(L, B - 1)
                norm(L, shifts, 2)
                gated(L, 1)
                norm(L, shifts, 3)
                add_ffn(L, 0)
                gated(L, 2)
                add_ffn(L, 1)
                if not last:
                    first(L + LAYER)
                gated(L, 3)
                add_ffn(L, 2)
                add_ffn(L, 3)

            first(LAYER)
            with dve.Fori(0, LAYERS - 1) as i:
                layer(i, dve.snap(i * LAYER + LAYER), dve.snap(i * 16 + 16), False)
            layer(LAYERS - 1, LAYERS * LAYER, LAYERS * 16, True)
            dve.wait_ge(y_out, (LAYERS + 2) * LAYER)
            dve.tensor_tensor(k.x[:, :, :], k.x[:, :, :], k.y[:, :, :], ALU.add).then_inc(x_sum, 1)

        @block.gpsimd
        def _(pool):
            pool.memset(half[:, :], -0.5)
            for buf in (kT[:, :, :, :], prob1[:, :, :], xT[:, 1, 0:1], late[0:1, :, :]):
                ins = pool.memset(buf, 0.0)
            ins.then_inc(zeros_set, 1)
            pool.wait_ge(zeros_set, 1)
            pool.wait_ge(scale_in, 32)
            pool.wait_ge(b2_in, 16)

            def tables(L, i):
                pool.wait_ge(cos_done, L)
                scale = head_scale[:, bass.ds(i, 1), :, :].rearrange("p o s d -> p (o s) d")
                for t in range(TT):
                    row = lambda at: k.const[:, at + t * 2 * DH:at + (t + 1) * 2 * DH].rearrange("p (s d) -> p s d", s=2)
                    pool.tensor_tensor(cos[:, t, :, :], row(C_COS), scale, ALU.mult)
                    lo, hi = slice(0, DH // 2), slice(DH // 2, DH)
                    for dst, src in ((lo, hi), (hi, lo)):
                        ins = pool.tensor_tensor(sin[:, t, :, dst], row(C_SIN)[:, :, dst], scale[:, :, src], ALU.mult)
                ins.then_inc(tables_done, LAYER)

            def rotate(L, b):
                for t in range(TT):
                    at = L + U * b + 8 * t
                    pool.wait_ge(floor_done, at + 8)
                    pool.wait_ge(s_read, L + U * max(b - 1, 0))
                    pool.tensor_tensor(rnorm[:, b % 2, t, :], norm2_floor[:, :], half[:, :], ALU.pow).then_inc(rnorm_done, 8)
                    pool.wait_ge(cos_done, at + 8)
                    pool.tensor_tensor(qk[:, t, :], qk[:, t, :], twist, ALU.add).then_inc(sum_done, 8)
                    pool.wait_ge(rnorm_done, at + 8)
                    pool.wait_ge(sum_done, at + 8)
                    keys = qk[:, t, INNER:].rearrange("p (h d) -> p h d", d=DH)
                    pool.tensor_tensor(keys, keys, rnorm[:, b % 2, t, H:].unsqueeze(2).broadcast_to([P, H, DH]), ALU.mult)\
                        .then_inc(rope_done, 8)

            def norm(L, i, b):
                pool.wait_ge(ln_var, L + U * (b + 1))
                pool.tensor_tensor(rstd[:, :], var[:, :], half[:, 0:TT], ALU.pow).then_inc(ln_rstd, U)
                pool.wait_ge(xn_done, L + U * (b + 1))
                both = k.y[:, b * TT:(b + 1) * TT, :]
                pool.tensor_tensor(both, both, b2[:, bass.ds(i, 1), :].broadcast_to([P, TT, D]), ALU.add).then_inc(b2_done, U)

            def layer(i, L, last):
                for b in range(1, B):
                    rotate(L, b)
                if not last:
                    tables(L + LAYER, i + 1)
                for b in range(B):
                    norm(L, i, b)
                if not last:
                    rotate(L + LAYER, 0)

            tables(LAYER, 0)
            rotate(LAYER, 0)
            with pool.Fori(0, LAYERS - 1) as i:
                layer(i, pool.snap(i * LAYER + LAYER), False)
            layer(LAYERS - 1, LAYERS * LAYER, True)




def store(k):
    nc, io = k.nc, k.io
    with ExitStack() as ctx:
        out_done = k.sem("out_done")
        block = ctx.enter_context(nc.Block())

        @block.sync
        def _(sp):
            sp.dma_start(io["out"].rearrange("b (t p) c -> p (b t) c", p=P), k.x[:, :, :]).then_inc(out_done, 16)
            sp.wait_ge(out_done, 16)


STAGES = (cross_attention, linear_attention, local_layers, store)


def build(nc, io, stages=None):
    with ExitStack() as ctx:
        k = Kernel(nc, ctx, io)
        for stage in stages or STAGES:
            stage(k)


_INS = ["x", "ctx_1024", "xattn_g1", "xattn_b1", "xattn_g2", "xattn_b2", "xattn_Wq", "xattn_Wkv", "xattn_Wout",
        "attn_Wq", "attn_bq", "attn_Wk", "attn_bk", "attn_Wv", "attn_bv", "attn_Wo", "attn_bo", "attn_ln_g", "attn_ln_b",
        "ffn_Wqkv", "ffn_q_scale", "ffn_k_scale", "ffn_Wo", "ffn_ln_g", "ffn_ln_b", "ffn_W1", "ffn_b1", "ffn_W2", "ffn_b2"]


def prepare(nc, inputs):
    arrays, io = {}, {}

    def add(name, a):
        a = np.ascontiguousarray(a)
        arrays[f"in_{name}_dram"] = a
        io[name] = nc.dram_tensor(f"in_{name}_dram", a.shape, mybir.dt.from_np(a.dtype), kind="ExternalInput").ap()

    for name in _INS:
        add(name, inputs[name if name in ("x", "ctx_1024") else f"L0_{name}"])
    add("mask", np.asarray(inputs["mask_BxS2_bk0"]))
    add("const", constants())
    io["out"] = nc.dram_tensor("out_0_dram", (B, T, D), F32, kind="ExternalOutput").ap()
    return arrays, io


def kernel(**inputs):
    import concourse.bacc as _bacc
    from concourse.bass_utils import run_bass_kernel_spmd as _run

    nc = _bacc.Bacc("TRN2", target_bir_lowering=False, num_devices=1)
    arrays, io = prepare(nc, inputs)
    build(nc, io)
    r = _run(nc, [arrays], core_ids=[0])
    return r.results[0]["out_0_dram"]
```

```python
from contextlib import ExitStack

import concourse.bass as bass
import numpy as np
from concourse import mybir

F32 = mybir.dt.float32
F32R = mybir.dt.float32r
I32 = mybir.dt.int32
U8 = mybir.dt.uint8
ALU = mybir.AluOpType
ACT = mybir.ActivationFunctionType
AX = mybir.AxisListType

P = 128
B, T, D = 4, 256, 256
S = 4096
H, DH = 16, 64
INNER = H * DH
PAIRS = H // 2
TT = T // P
KD = D // P
CHUNK = 256
CHUNKS = S // CHUNK
KT = CHUNK // P
GROUP = 4
LAYERS = 6
FF = int(D * 4 * 2 / 3)
FM = (FF + P - 1) // P
FWIDE = [FF // FM + (m < FF % FM) for m in range(FM)]
FAT = [sum(FWIDE[:m]) for m in range(FM)]
WINDOW = 64
LH, LD = 16, 16
EPS = 1e-5
HIGH, LOW = 0, 1
PARTS = ((HIGH, HIGH), (LOW, HIGH), (HIGH, LOW))
FAR = 3.0e38
BAND = 1.0e30
QK_SCALE = 8.0

C_ID = 0
C_BAND0 = C_ID + P
C_BAND1 = C_BAND0 + P
C_BLOCK = C_BAND1 + 192
C_COS = C_BLOCK + P
C_SIN = C_COS + TT * 2 * DH
C_BIT = C_SIN + TT * 2 * DH
C_ALL = C_BIT + CHUNKS

R_G1, R_B1, R_G2, R_B2, R_BQ, R_LG, R_LB = (2 * j for j in range(7))
R_LAYER = 14
V_FG, V_FB, V_B1A, V_B1G = 0, 2, 4, 4 + FM
KINDS = 4 + 2 * FM
ROWS = R_LAYER + KINDS * LAYERS


def constants():
    c = np.zeros((P, C_ALL), np.float32)
    c[:, C_ID:C_ID + P] = np.eye(P, dtype=np.float32)
    q, k = np.arange(P)[:, None], np.arange(P)[None, :]
    c[:, C_BAND0:C_BAND0 + P] = np.where((q < k) | (q > k + WINDOW) , BAND, 0.0)
    q, k = np.arange(P, 2 * P)[:, None], np.arange(WINDOW, 2 * P)[None, :]
    c[:, C_BAND1:C_BAND1 + 192] = np.where((q < k) | (q > k + WINDOW), BAND, 0.0)
    d, e = np.arange(P)[:, None], np.arange(P)[None, :]
    c[:, C_BLOCK:C_BLOCK + P] = np.where(d // LD == e // LD, 1.0 / 1024.0 ** 2, 0.0)
    half = np.arange(0, DH, 2, dtype=np.float32)
    t = np.arange(T, dtype=np.float32)
    freqs = t[:, None] * (np.float32(1.0) / np.float32(10000.0) ** (half / np.float32(DH)))[None, :]
    freqs = np.concatenate([freqs, freqs], -1).astype(np.float32)
    base = (half + np.float32(0.4 * DH)) / np.float32(1.4 * DH)
    scale = base[None, :] ** ((t - T // 2) / np.float32(WINDOW // 2))[:, None]
    scale = np.concatenate([scale, scale], -1).astype(np.float32)
    sign = np.where(np.arange(DH) < DH // 2, -1.0, 1.0).astype(np.float32)
    both = [(np.cos(freqs) * s, np.sin(freqs) * sign * s) for s in (-np.float32(QK_SCALE) * scale, 1.0 / scale)]
    for n, at in enumerate((C_COS, C_SIN)):
        table = np.stack([both[0][n], both[1][n]], 1).astype(np.float32)
        c[:, at:at + TT * 2 * DH] = table.reshape(TT, P, 2 * DH).transpose(1, 0, 2).reshape(P, -1)
    c[:, C_BIT:C_BIT + CHUNKS] = 2.0 ** np.arange(CHUNKS)
    return c


class Chain:

    def __init__(self, eng, sem, base=0):
        self.eng, self.sem, self.base, self.n = eng, sem, base, 0

    def link(self, ins):
        self.n += 1
        ins.then_inc(self.sem, 1)
        self.eng.wait_ge(self.sem, self.base + self.n)


def hold(eng, sem):
    eng.sem_inc(sem, 1)


def begin_at(eng, count, sems):
    for sem in sems:
        eng.sem_inc(sem, count)


class Kernel:

    def __init__(self, nc, ctx, io):
        self.nc, self.io = nc, io
        self.ctx = ctx
        self.x = self.sb("x_all", [P, B * TT, D])
        self.y = self.sb("y_all", [P, B * TT, D])
        self.const = self.sb("const", [P, C_ALL])
        self.cols = self.sb("cols", [P, ROWS])
        self.ident = self.const[:, C_ID:C_ID + P]

    def place_linear_weights(self):
        self.lin_place = ExitStack()
        self.wkv_in = self.sb("wkv_in", [P, KD, 2 * INNER], ctx=self.lin_place, side="right")
        self.lin_wq = self.wkv_in[:, 0, 0:KD * D].rearrange("p (k n) -> p k n", k=KD)
        self.lin_wkv = self.wkv_in[:, 1, 0:KD * 4 * D].rearrange("p (k s n c) -> p k s n c", k=KD, s=2, n=2)
        self.lin_wq_in, self.lin_wkv_in = self.sem("lin_wq_in"), self.sem("lin_wkv_in")

    def load_linear_weights(self, eng):
        io = self.io
        eng.dma_start(self.lin_wq[:, :, :], io["attn_Wq"].rearrange("(k p) n -> p k n", p=P)).then_inc(self.lin_wq_in, 16)
        for s in range(2):
            for n, name in enumerate(("k", "v")):
                eng.dma_start(self.lin_wkv[:, :, s, n, :], io[f"attn_W{name}"][s].rearrange("(k p) n -> p k n", p=P))\
                    .then_inc(self.lin_wkv_in, 16)

    def place_layer_weights(self):
        self.wqkv = self.sb("wqkv", [P, KD, 3 * INNER])
        self.wo = self.sb("wo", [P, PAIRS, D])
        self.w1 = self.sb("w1", [P, KD, 2 * FF])
        self.w2 = self.sb("w2", [P, FM, D])
        self.b2 = self.sb("b2", [P, LAYERS, D])
        self.head_scale = self.sb("head_scale", [P, LAYERS, 2, DH])
        self.wqkv_in, self.wo_in, self.w1_in, self.w2_in = (self.sem(n) for n in ("wqkv_in", "wo_in", "w1_in", "w2_in"))
        self.b2_in, self.scale_in = self.sem("b2_in"), self.sem("scale_in")

    def load_layer_weights(self, eng, i, which):
        io, one = self.io, bass.ds(i, 1)
        if which == "qkv":
            src = io["ffn_Wqkv"].rearrange("i (k p) n -> i p k n", p=P)
            for kk in range(KD):
                for j in range(2):
                    cut = slice(j * 3 * INNER // 2, (j + 1) * 3 * INNER // 2)
                    eng.dma_start(self.wqkv[:, kk, cut], src[one, :, kk, cut].rearrange("o p n -> (o p) n")).then_inc(self.wqkv_in, 16)
        elif which == "wo":
            src = io["ffn_Wo"].rearrange("i (k p) n -> i p k n", p=P)
            for j in range(4):
                eng.dma_start(self.wo[:, 2 * j:2 * j + 2, :], src[one, :, 2 * j:2 * j + 2, :].rearrange("o p k n -> (o p) k n"))\
                    .then_inc(self.wo_in, 16)
        elif which == "w1":
            src = io["ffn_W1"].rearrange("i (k p) n -> i p k n", p=P)
            for kk in range(KD):
                for j in range(2):
                    cut = slice(j * FF, (j + 1) * FF)
                    eng.dma_start(self.w1[:, kk, cut], src[one, :, kk, cut].rearrange("o p n -> (o p) n")).then_inc(self.w1_in, 16)
        else:
            for m0, m1 in ((0, 2), (2, 4), (4, 5), (5, 6)):
                src = io["ffn_W2"][one, FAT[m0]:FAT[m1 - 1] + FWIDE[m1 - 1], :]
                eng.dma_start(self.w2[0:FWIDE[m0], m0:m1, :], src.rearrange("o (m p) n -> (o p) m n", p=FWIDE[m0]))\
                    .then_inc(self.w2_in, 16)

    def load_layer_vectors(self, eng):
        io = self.io
        for n, name in enumerate(("q", "k")):
            src = io[f"ffn_{name}_scale"].rearrange("(o i) d -> o i d", o=1).broadcast_to([P, LAYERS, DH])
            eng.dma_start(self.head_scale[:, :, n, :], src).then_inc(self.scale_in, 16)
        src = io["ffn_b2"].rearrange("(o i) d -> o i d", o=1).broadcast_to([P, LAYERS, D])
        eng.dma_start(self.b2[:, :, :], src).then_inc(self.b2_in, 16)

    def sb(self, name, shape, dt=F32, ctx=None, side=None):
        return (ctx or self.ctx).enter_context(self.nc.sbuf_tensor(name, shape, dt, side=side))

    def banks(self, name, ctx):
        return ctx.enter_context(self.nc.psum_tensor(name, [P, 8, 512], F32))

    def sem(self, name):
        return self.ctx.enter_context(self.nc.semaphore(name))


def cross_attention(k):
    nc, io = k.nc, k.io
    k.place_linear_weights()
    U = 16
    with ExitStack() as ctx:
        sb = lambda name, shape, dt=F32: k.sb(name, shape, dt, ctx)
        rows = sb("rows", [P, P])
        wq = sb("wq", [P, KD, INNER])
        wkv_in = k.wkv_in
        wkv = sb("wkv", [P, 2, KD, 2 * INNER], F32R)
        wout = sb("wout", [P, PAIRS, D])
        mask_rows = sb("mask_rows", [B, S], U8)
        chunk_any = sb("chunk_any", [B, CHUNKS])
        word_f = sb("word_f", [B, 1])
        word_col = sb("word_col", [B, 1], I32)
        word = sb("word", [1, B], I32)
        lats = k.y
        lat = sb("lat", [P, TT, D])
        ctx_raw = sb("ctx_raw", [P, KT, D])
        chunk_mask = sb("chunk_mask", [P, CHUNK], U8)
        bias = sb("bias", [P, CHUNK])
        no_bias = sb("no_bias", [P, CHUNK])
        xn = sb("xn", [P, KT, D])
        inT = sb("inT", [P, KD, CHUNK])
        inT_parts = sb("inT_parts", [P, 2, KD, CHUNK], F32R)
        inT_v = sb("inT_v", [P, 2, KD, CHUNK], F32R)
        qT = sb("qT", [P, H, T])
        kT = sb("kT", [P, PAIRS, CHUNK])
        v = sb("v", [P, KT, INNER])
        prob = sb("prob", [P, TT, H, CHUNK])
        probT = sb("probT", [P, 2, KT, 512])
        oT = sb("oT", [P, PAIRS, T])
        o = sb("o", [P, TT, INNER])
        stats = sb("stats", [P, B * TT, 6])
        mv = sb("mv", [P, B * TT, 2])
        var = sb("var", [P, B * TT])
        rstd = sb("rstd", [P, B * TT])
        half = sb("half", [P, B * TT])
        top = sb("top", [P, TT, H])
        chunk_top = sb("chunk_top", [P, TT, H])
        new_top = sb("new_top", [P, TT, H])
        drop = sb("drop", [P, TT, H])
        alpha = sb("alpha", [P, TT, H])
        chunk_sum = sb("chunk_sum", [P, TT, H])
        total = sb("total", [P, TT, H])
        rtotal = sb("rtotal", [P, TT, H])
        ps = k.banks("ps_cross", ctx)
        PROJ, SCORE, TURN, OUT = 0, 2, 4, 6

        sem = k.sem
        const_in, x_in, mask_in, w_in = sem("const_in"), sem("x_in"), sem("mask_in"), sem("w_in")
        rows_zero, rows_in, cols_full = sem("rows_zero"), sem("rows_in"), sem("cols_full")
        words_out, words_in, q_zero, wkv_loaded, w_high, w_split = (
            sem(n) for n in ("words_out", "words_in", "q_zero", "wkv_loaded", "w_high", "w_split"))
        ctx_in, chunk_mask_in, bias_done = sem("ctx_in"), sem("chunk_mask_in"), sem("bias_done")
        ln_var, ln_rstd, lat_ready, xn_ready = sem("ln_var"), sem("ln_rstd"), sem("lat_ready"), sem("xn_ready")
        inT_full, inT_done, high_done, parts_done, inT_copied, q_full, q_done = sem("inT_full"), sem("inT_done"), sem("high_done"), sem("parts_done"), sem("inT_copied"), sem("q_full"), sem("q_done")
        k_full, k01_done, k_done, v_full, v_done = sem("k_full"), sem("k01_done"), sem("k_done"), sem("v_full"), sem("v_done")
        s_full, s_read, top_done, alpha_done = sem("s_full"), sem("s_read"), sem("top_done"), sem("alpha_done")
        p_ready, o_scaled, total_done = sem("p_ready"), sem("o_scaled"), sem("total_done")
        pT_full, pT_done, o_full, oT_done = sem("pT_full"), sem("pT_done"), sem("o_full"), sem("oT_done")
        back_full, back_done = sem("back_full"), sem("back_done")
        fin_ready, fin_full, fin_done = sem("fin_ready"), sem("fin_full"), sem("fin_done")
        x_full, x_done = sem("x_full"), sem("x_done")
        dve_step, pool_step, sp_held, dve_held, pool_held, lats_done = (
            sem(f"cross_{n}") for n in ("dve_step", "pool_step", "sp_held", "dve_held", "pool_held", "lats_done"))

        ctx_dram = io["ctx_1024"].rearrange("b (c t p) d -> (b c) p t d", p=P, t=KT)
        mask_dram = io["mask"].rearrange("b (c n) -> (b c) n", n=CHUNK)

        def attended(eng, b):
            return eng.value_load(word[0:1, bass.ds(b, 1)], min_val=0, max_val=2 ** CHUNKS - 1)

        def chunks(eng, bits, body):
            with eng.Fori(0, CHUNKS // GROUP) as g:
                with eng.If((bits >> (g * GROUP)) & (2 ** GROUP - 1)):
                    with eng.Fori(0, GROUP) as n:
                        c = eng.snap(g * GROUP + n)
                        with eng.If((bits >> c) & 1):
                            body(c)

        block = ctx.enter_context(nc.Block())

        @block.sync
        def _(sp):
            sp.dma_start(k.const[:, :], io["const"]).then_inc(const_in, 16)
            sp.dma_start(k.x[:, :, :], io["x"].rearrange("b (t p) c -> p (b t) c", p=P)).then_inc(x_in, 16)
            sp.dma_start(mask_rows[:, :], io["mask"]).then_inc(mask_in, 16)
            begin_at(sp, U, (xn_ready, bias_done, ctx_in, chunk_mask_in, inT_full, inT_done, high_done, parts_done, inT_copied,
                             k_full, k01_done, k_done, v_full, v_done,
                             s_full, s_read, top_done, alpha_done, p_ready, o_scaled, total_done, pT_full, pT_done, o_full, oT_done,
                             back_full, back_done))
            begin_at(sp, 4, (q_full, q_done, fin_full, fin_done))
            begin_at(sp, 2, (fin_ready, x_full, x_done))
            sp.wait_ge(rows_zero, 1)
            for r, name in ((R_G1, "xattn_g1"), (R_B1, "xattn_b1"), (R_G2, "xattn_g2"), (R_B2, "xattn_b2"),
                            (R_BQ, "attn_bq"), (R_LG, "attn_ln_g"), (R_LB, "attn_ln_b")):
                sp.dma_start(rows[r:r + KD, :], io[name].rearrange("(k p) -> k p", p=P)).then_inc(rows_in, 16)
            layer_rows = [(V_FG + j, io["ffn_ln_g"][:, j * P:(j + 1) * P]) for j in range(KD)]
            layer_rows += [(V_FB + j, io["ffn_ln_b"][:, j * P:(j + 1) * P]) for j in range(KD)]
            layer_rows += [(V_B1A + m, io["ffn_b1"][:, FAT[m]:FAT[m] + FWIDE[m]]) for m in range(FM)]
            layer_rows += [(V_B1G + m, io["ffn_b1"][:, FF + FAT[m]:FF + FAT[m] + FWIDE[m]]) for m in range(FM)]
            for kind, src in layer_rows:
                r = R_LAYER + kind * LAYERS
                sp.dma_start(rows[r:r + LAYERS, 0:src.shape[1]], src).then_inc(rows_in, 16)
            sp.wait_ge(words_out, 1)
            sp.dma_start(word[0:1, :], word_col[:, :]).then_inc(words_in, 16)
            sp.wait_ge(words_in, 16)
            sp.wait_ge(w_split, 2 * KD)
            k.load_linear_weights(sp)
            uc_reg = sp.alloc_register("sp_uc")
            sp.reg_mov(uc_reg, U)
            with sp.Fori(1, B + 1) as turn:
                b = turn - 1
                def load(c):
                    uc = sp.snap(uc_reg)
                    sp.wait_ge(xn_ready, uc)
                    sp.dma_start(ctx_raw[:, :, :], ctx_dram[bass.ds(b * CHUNKS + c, 1)].rearrange("o p t d -> (o p) t d"))\
                        .then_inc(ctx_in, 16)
                    sp.wait_ge(bias_done, uc)
                    hold(sp, sp_held)
                    sp.dma_start(chunk_mask[:, :], mask_dram[bass.ds(b * CHUNKS + c, 1)].broadcast_to([P, CHUNK]))\
                        .then_inc(chunk_mask_in, 16)
                    sp.reg_add(uc_reg, uc_reg, U)
                chunks(sp, attended(sp, b), load)

        @block.tensor
        def _(pe):
            u_reg, uc_reg = pe.alloc_register("pe_u"), pe.alloc_register("pe_uc")
            pe.reg_mov(u_reg, U)
            pe.reg_mov(uc_reg, U)
            pe.wait_ge(const_in, 16)
            pe.wait_ge(rows_in, 16 * N_ROW_DMAS)
            pe.transpose(ps[:, OUT, 0:ROWS], rows[0:ROWS, :], k.ident[0:ROWS, 0:ROWS]).then_inc(cols_full, 1)

            def turn_input(src):
                for kk in range(KD):
                    for t in range(KT):
                        ins = pe.transpose(ps[:, TURN + kk, t * P:(t + 1) * P], src(t, kk), k.ident)
                    ins.then_inc(inT_full, U // KD)

            def project_q(u, turn):
                pe.wait_ge(inT_done, u + U)
                for j in range(4):
                    if j >= 2:
                        pe.wait_ge(q_done, turn * 4 + j - 1)
                    for i in range(2):
                        pair = 2 * j + i
                        for kk in range(KD):
                            ins = pe.matmul(ps[:, PROJ + j % 2, i * T:(i + 1) * T], wq[:, kk, pair * P:(pair + 1) * P],
                                            inT[:, kk, :], start=kk == 0, stop=kk == KD - 1)
                    ins.then_inc(q_full, 1)

            def keys(u, turn):
                pe.wait_ge(parts_done, u + U)
                pe.wait_ge(w_split, KD)
                for j in range(4):
                    if j < 2:
                        pe.wait_ge(q_done, turn * 4 + 3 + j)
                        pe.wait_ge(v_done, u - 4 + 4 * j)
                    else:
                        pe.wait_ge(k01_done, u + 8 * (j - 1))
                    for i in range(2):
                        pair = 2 * j + i
                        for n, (w, x) in enumerate(PARTS):
                            for kk in range(KD):
                                ins = pe.matmul(ps[:, PROJ + j % 2, i * CHUNK:(i + 1) * CHUNK],
                                                wkv[:, w, kk, pair * P:(pair + 1) * P], inT_parts[:, x, kk, :],
                                                start=n + kk == 0, stop=n + kk == len(PARTS) + KD - 2)
                    ins.then_inc(k_full, U // 4)

            def scores(u, t, pair):
                s = t * PAIRS + pair
                if t == 0 and pair % 2 == 0:
                    pe.wait_ge(k01_done if pair < 4 else k_done, u + 8 * (pair // 2 % 2 + 1))
                pe.wait_ge(s_read, u + (s - 1 if s >= 2 else 0))
                for i in range(2):
                    ins = pe.matmul(ps[:, SCORE + s % 2, i * CHUNK:(i + 1) * CHUNK],
                                    qT[:, 2 * pair + i, t * P:(t + 1) * P], kT[:, pair, :], start=True, stop=True)
                ins.then_inc(s_full, 1)

            def values(u, js):
                for j in js:
                    t, part = divmod(j, 2)
                    if j == 0:
                        pe.wait_ge(w_split, 2 * KD)
                        pe.wait_ge(inT_copied, u + U)
                    if j >= 2:
                        pe.wait_ge(v_done, u + 4 * (j - 1))
                    for n, (w, x) in enumerate(PARTS):
                        for kk in range(KD):
                            ins = pe.matmul(ps[:, PROJ + j % 2, :], inT_v[:, x, kk, t * P:(t + 1) * P],
                                            wkv[:, w, kk, INNER + part * 512:INNER + (part + 1) * 512],
                                            start=n + kk == 0, stop=n + kk == len(PARTS) + KD - 2)
                    ins.then_inc(v_full, U // 4)

            def turn_probs(u, pair):
                pe.wait_ge(p_ready, u + PAIRS + pair + 1)
                for t in range(KT):
                    s = 2 * pair + t
                    pe.wait_ge(pT_done, u + (s - 1 if s >= 2 else 0))
                    for i in range(2):
                        for lt in range(TT):
                            ins = pe.transpose(ps[:, TURN + t, (i * TT + lt) * P:(i * TT + lt + 1) * P],
                                               prob[:, lt, 2 * pair + i, t * P:(t + 1) * P], k.ident)
                    ins.then_inc(pT_full, 1)

            def weigh(u, pair):
                if pair == 0:
                    pe.wait_ge(v_done, u + U)
                pe.wait_ge(pT_done, u + 2 * pair + 2)
                pe.wait_ge(oT_done, u + (2 * (pair - 1) if pair >= 2 else 0))
                for t in range(KT):
                    for i in range(2):
                        ins = pe.matmul(ps[i * DH:(i + 1) * DH, OUT + pair % 2, 0:T],
                                        v[:, t, (2 * pair + i) * DH:(2 * pair + i + 1) * DH],
                                        probT[:, pair % 2, t, i * T:(i + 1) * T], start=t == 0, stop=t == KT - 1)
                ins.then_inc(o_full, 2)

            def back(u, part):
                pe.wait_ge(oT_done, u + 8 * (part + 1))
                for t in range(TT):
                    if part:
                        pe.wait_ge(back_done, u + 4 * (t + 1))
                    for i in range(4):
                        ins = pe.transpose(ps[:, PROJ + t, i * P:(i + 1) * P],
                                           oT[:, 4 * part + i, t * P:(t + 1) * P], k.ident)
                    ins.then_inc(back_full, 4)

            def turn_next(u, more):
                with pe.If(more):
                    uc = pe.snap(uc_reg)
                    pe.wait_ge(xn_ready, uc + U)
                    pe.wait_ge(pT_done, u)
                    turn_input(lambda t, kk: xn[:, t, kk * P:(kk + 1) * P])
                    pe.reg_add(uc_reg, uc_reg, U)

            def turn_latents(turn):
                pe.wait_ge(lat_ready, turn)
                turn_input(lambda t, kk: lat[:, t, kk * P:(kk + 1) * P])

            turn_latents(1)
            pe.wait_ge(w_in, 32)
            pe.wait_ge(words_in, 16)
            with pe.Fori(1, B + 1) as turn:
                b = turn - 1
                bits = attended(pe, b)
                u = pe.snap(u_reg)
                pe.wait_ge(v_done, u)
                pe.wait_ge(back_done, u)
                project_q(u, turn)
                keys(u, turn)
                for pair in range(PAIRS):
                    scores(u, 0, pair)
                for pair in range(PAIRS):
                    scores(u, 1, pair)
                    if pair == 3:
                        turn_next(u, bits > 0)
                    if pair in (5, 6):
                        values(u, (0, 1) if pair == 5 else (2,))
                values(u, (3,))
                pe.reg_add(u_reg, u_reg, U)

                def step(c):
                    u, last = pe.snap(u_reg), pe.snap(pe.snap(u_reg) - U)
                    keys(u, turn)
                    for pair in range(PAIRS):
                        turn_probs(last, pair)
                        if pair:
                            weigh(last, pair - 1)
                        scores(u, 0, pair)
                        if pair == 6:
                            pe.wait_ge(k_done, u + U)
                            back(last, 0)
                    weigh(last, PAIRS - 1)
                    for pair in range(PAIRS):
                        scores(u, 1, pair)
                        if pair == 2:
                            back(last, 1)
                        if pair == 3:
                            turn_next(u, (bits >> c) > 1)
                        if pair == 5:
                            pe.wait_ge(back_done, u)
                            values(u, (0, 1))
                        if pair == 6:
                            values(u, (2,))
                    values(u, (3,))
                    pe.reg_add(u_reg, u_reg, U)
                chunks(pe, bits, step)
                u, last = pe.snap(u_reg), pe.snap(pe.snap(u_reg) - U)
                for pair in range(PAIRS):
                    turn_probs(last, pair)
                    if pair:
                        weigh(last, pair - 1)
                    if pair == 5:
                        pe.wait_ge(v_done, u)
                        back(last, 0)
                weigh(last, PAIRS - 1)
                back(last, 1)
                with pe.If(turn < B):
                    pe.wait_ge(pT_done, u)
                    turn_latents(turn + 1)
                for j in range(4):
                    t, part = divmod(j, 2)
                    pe.wait_ge(fin_ready, turn * 2 + t + 1)
                    if j < 2:
                        pe.wait_ge(back_done, u)
                    else:
                        pe.wait_ge(fin_done, turn * 4 + j - 1)
                    for i in range(4):
                        ins = pe.transpose(ps[:, PROJ + j % 2, i * P:(i + 1) * P],
                                           o[:, t, (4 * part + i) * P:(4 * part + i + 1) * P], k.ident)
                    ins.then_inc(fin_full, 1)
                for t in range(TT):
                    pe.wait_ge(fin_done, turn * 4 + 2 * (t + 1))
                    for pair in range(PAIRS):
                        ins = pe.matmul(ps[:, OUT + t, 0:D], oT[:, pair, t * P:(t + 1) * P], wout[:, pair, :],
                                        start=pair == 0, stop=pair == PAIRS - 1)
                    ins.then_inc(x_full, 1)
                pe.wait_ge(x_done, turn * 2 + 2)

        @block.scalar
        def _(act):
            u_reg = act.alloc_register("act_u")
            act.reg_mov(u_reg, U)
            act.dma_start(wq[:, :, :], io["xattn_Wq"].rearrange("(k p) n -> p k n", p=P)).then_inc(w_in, 16)
            act.dma_start(wkv_in[:, :, :], io["xattn_Wkv"].rearrange("(k p) n -> p k n", p=P)).then_inc(wkv_loaded, 16)
            act.dma_start(wout[:, :, :], io["xattn_Wout"].rearrange("(k p) n -> p k n", p=P)).then_inc(w_in, 16)
            act.wait_ge(wkv_loaded, 16)
            for part in range(2):
                for kk in range(KD):
                    cols = slice(part * INNER, (part + 1) * INNER)
                    act.activation(wkv[:, HIGH, kk, cols], wkv_in[:, kk, cols], ACT.Copy).then_inc(w_high, 1)
            act.wait_ge(q_zero, 1)
            act.wait_ge(words_in, 16)

            def keys_out(u):
                act.wait_ge(s_full, u)
                for j in (2, 3):
                    act.wait_ge(k_full, u + 4 * (j + 1))
                    act.activation(kT[:, 2 * j:2 * j + 2, :], ps[:, PROJ + j % 2, :].rearrange("p (i n) -> p i n", i=2),
                                   ACT.Copy).then_inc(k_done, U // 2)
                act.wait_ge(parts_done, u + U)
                act.wait_ge(v_full, u)
                act.activation(inT_v[:, :, :, :], inT_parts[:, :, :, :], ACT.Copy).then_inc(inT_copied, U)

            def exps(u):
                act.wait_ge(o_scaled, u)
                act.wait_ge(total_done, u)
                for t in range(TT):
                    act.wait_ge(top_done, u + 8 * (t + 1))
                    act.activation(alpha[:, t, :], drop[:, t, :], ACT.Exp).then_inc(alpha_done, U // TT)
                    for h in range(H):
                        ins = act.activation(prob[:, t, h, :], prob[:, t, h, :], ACT.Exp, bias=new_top[:, t, h:h + 1],
                                             scale=-1.0, accum_out=chunk_sum[:, t, h:h + 1])
                        if h % 2:
                            ins.then_inc(p_ready, 1)

            def output_out(u):
                act.wait_ge(back_full, u)
                for pair in range(PAIRS):
                    act.wait_ge(o_full, u + 2 * (pair + 1))
                    act.activation(oT[:, pair, :], ps[:, OUT + pair % 2, 0:T], ACT.Copy).then_inc(oT_done, 2)

            with act.Fori(1, B + 1) as turn:
                b = turn - 1
                u = act.snap(u_reg)
                act.wait_ge(s_full, u)
                for j in range(4):
                    act.wait_ge(q_full, turn * 4 + j + 1)
                    for i in range(2):
                        half_q = qT[i * DH:(i + 1) * DH, :, :].rearrange("p (g e) n -> p g e n", e=2)
                        ins = act.activation(half_q[:, 2 * j:2 * j + 2, i, :],
                                             ps[i * DH:(i + 1) * DH, PROJ + j % 2, :].rearrange("p (g n) -> p g n", g=2),
                                             ACT.Copy, scale=-float(DH) ** -0.5)
                    ins.then_inc(q_done, 1)
                keys_out(u)
                exps(u)
                act.wait_ge(x_full, turn * 2)
                act.reg_add(u_reg, u_reg, U)

                def step(c):
                    u = act.snap(u_reg)
                    keys_out(u)
                    output_out(act.snap(act.snap(u_reg) - U))
                    exps(u)
                    act.reg_add(u_reg, u_reg, U)
                chunks(act, attended(act, b), step)
                output_out(act.snap(act.snap(u_reg) - U))
                for j in range(4):
                    t, part = divmod(j, 2)
                    act.wait_ge(fin_full, turn * 4 + j + 1)
                    if j == 0:
                        act.wait_ge(back_full, act.snap(u_reg))
                    act.activation(oT[:, 4 * part:4 * part + 4, t * P:(t + 1) * P],
                                   ps[:, PROJ + j % 2, :].rearrange("p (i n) -> p i n", i=4), ACT.Copy)\
                        .then_inc(fin_done, 1)

        @block.vector
        def _(dve):
            u_reg, uc_reg, ln_reg, step_reg = (dve.alloc_register(f"dve_{n}") for n in ("u", "uc", "ln", "step"))
            for r, first in ((u_reg, U), (uc_reg, U), (ln_reg, 4)):
                dve.reg_mov(r, first)
            chain = Chain(dve, dve_step)
            chain.link(dve.memset(no_bias[:, :], 0.0))

            def norm(ch, src, dst, ln, tiles):
                for i, t in enumerate(tiles):
                    ins = dve.bn_stats(stats[:, i, :], src(t))
                ch.link(ins)
                hold(dve, dve_held)
                for i in range(len(tiles)):
                    ins = dve.bn_aggr(mv[:, i, :], stats[:, i, :])
                ch.link(ins)
                dve.tensor_scalar(var[:, 0:len(tiles)], mv[:, 0:len(tiles), 1], EPS, None, ALU.add).then_inc(ln_var, 1)
                dve.wait_ge(ln_rstd, ln + 1)
                return [dve.tensor_scalar(dst[:, t, :], src(t), mv[:, i, 0:1], rstd[:, i:i + 1], ALU.subtract, ALU.mult)
                        for i, t in enumerate(tiles)]

            def latents(ln, tiles):
                *_, last = norm(chain, lambda t: k.x[:, t, :], lats, ln, tiles)
                chain.link(last)
                *_, last = norm(chain, lambda t: lats[:, t, :], lats, ln + 1, tiles)
                last.then_inc(lats_done, 1)

            dve.wait_ge(x_in, 16)
            latents(0, range(TT))
            dve.wait_ge(mask_in, 16)
            dve.wait_ge(const_in, 16)
            chain.link(dve.tensor_reduce(chunk_any[:, :], mask_rows[:, :].rearrange("b (c n) -> b c n", n=CHUNK), AX.X, ALU.max))
            chain.link(dve.tensor_tensor(chunk_any[:, :], chunk_any[:, :], k.const[0:B, C_BIT:C_BIT + CHUNKS], ALU.mult))
            chain.link(dve.tensor_reduce(word_f[:, :], chunk_any[:, :], AX.X, ALU.add))
            dve.tensor_copy(word_col[:, :], word_f[:, :]).then_inc(words_out, 1)
            dve.wait_ge(cols_full, 1)
            chain.link(dve.tensor_copy(k.cols[:, :], ps[:, OUT, 0:ROWS]))

            def input_out(u, g, bb):
                dve.wait_ge(k_full, u)
                dve.wait_ge(inT_copied, u)
                for kk in range(KD):
                    dve.wait_ge(inT_full, u + 8 * (kk + 1))
                    dve.tensor_scalar(inT[:, kk, :], ps[:, TURN + kk, 0:CHUNK], k.cols[:, g + kk:g + kk + 1],
                                      k.cols[:, bb + kk:bb + kk + 1], ALU.mult, ALU.add).then_inc(inT_done, U // KD)
                dve.wait_ge(inT_done, u + U)
                dve.tensor_copy(inT_parts[:, HIGH, :, :], inT[:, :, :]).then_inc(high_done, U)
                dve.wait_ge(high_done, u + U)
                dve.tensor_tensor(inT_parts[:, LOW, :, :], inT[:, :, :], inT_parts[:, HIGH, :, :], ALU.subtract)\
                    .then_inc(parts_done, U)

            def keys_out(u):
                dve.wait_ge(s_full, u)
                for j in (0, 1):
                    dve.wait_ge(k_full, u + 4 * (j + 1))
                    dve.tensor_copy(kT[:, 2 * j:2 * j + 2, :], ps[:, PROJ + j % 2, :].rearrange("p (i n) -> p i n", i=2))\
                        .then_inc(k01_done, U // 2)

            def minima(u, t, pair, key_bias):
                s = t * PAIRS + pair
                dve.wait_ge(s_full, u + s + 1)
                hold(dve, dve_held)
                for i in range(2):
                    h = 2 * pair + i
                    ins = dve.tensor_tensor_reduce(
                        out=prob[:, t, h, :], in0=ps[:, SCORE + s % 2, i * CHUNK:(i + 1) * CHUNK], in1=key_bias,
                        scale=1.0, scalar=FAR, op0=ALU.add, op1=ALU.min, accum_out=chunk_top[:, t, h:h + 1])
                ins.then_inc(s_read, 1)

            def running(ch, u, t):
                dve.wait_ge(s_read, u + (t + 1) * PAIRS)
                if t == 0:
                    dve.wait_ge(p_ready, u)
                ch.link(dve.tensor_tensor(new_top[:, t, :], top[:, t, :], chunk_top[:, t, :], ALU.min))
                dve.tensor_tensor(drop[:, t, :], new_top[:, t, :], top[:, t, :], ALU.subtract).then_inc(top_done, U // TT)
                dve.wait_ge(top_done, u + (t + 1) * (U // TT))
                ch.link(dve.tensor_copy(top[:, t, :], new_top[:, t, :]))

            def values_out(u, js):
                dve.wait_ge(o_full, u)
                for j in js:
                    t, part = divmod(j, 2)
                    dve.wait_ge(v_full, u + 4 * (j + 1))
                    dve.tensor_copy(v[:, t, part * 512:(part + 1) * 512], ps[:, PROJ + j % 2, :]).then_inc(v_done, U // 4)

            def probs_out(u, pair):
                if pair >= 2:
                    dve.wait_ge(o_full, u + 2 * (pair - 1))
                for t in range(KT):
                    dve.wait_ge(pT_full, u + 2 * pair + t + 1)
                    dve.tensor_copy(probT[:, pair % 2, t, :], ps[:, TURN + t, :]).then_inc(pT_done, 1)

            def back(u, part):
                for t in range(TT):
                    dve.wait_ge(back_full, u + 4 * (2 * part + t + 1))
                    dve.wait_ge(o_scaled, u + 8 * (t + 1))
                    out = o[:, t, part * 512:(part + 1) * 512]
                    dve.tensor_tensor(out, ps[:, PROJ + t, :], out, ALU.add).then_inc(back_done, 4)

            def input_next(u, more):
                with dve.If(more):
                    input_out(dve.snap(u + U), R_G1, R_B1)

            def prepare_next(more):
                with dve.If(more):
                    uc, ln = dve.snap(uc_reg), dve.snap(ln_reg)
                    ch = Chain(dve, dve_step, dve.snap(step_reg))
                    dve.wait_ge(ctx_in, uc + U)
                    hold(dve, dve_held)
                    for ins in norm(ch, lambda t: ctx_raw[:, t, :], xn, ln, range(KT)):
                        ins.then_inc(xn_ready, U // KT)
                    dve.reg_add(uc_reg, uc_reg, U)
                    dve.reg_add(ln_reg, ln_reg, 1)
                    done(ch)

            def done(ch):
                dve.reg_add(step_reg, step_reg, ch.n)

            input_out(U, R_G2, R_B2)
            latents(2, range(TT, B * TT))
            dve.reg_mov(step_reg, chain.n)
            dve.wait_ge(words_in, 16)
            with dve.Fori(1, B + 1) as turn:
                b = turn - 1
                u = dve.snap(u_reg)
                ch = Chain(dve, dve_step, dve.snap(step_reg))
                dve.wait_ge(p_ready, u)
                hold(dve, dve_held)
                ch.link(dve.memset(top[:, :, :], FAR))
                done(ch)
                bits = attended(dve, b)
                keys_out(u)
                prepare_next(bits > 0)
                ch = Chain(dve, dve_step, dve.snap(step_reg))
                for pair in range(PAIRS):
                    minima(u, 0, pair, no_bias[:, :])
                running(ch, u, 0)
                for pair in range(PAIRS):
                    minima(u, 1, pair, no_bias[:, :])
                    if pair == 4:
                        input_next(u, bits > 0)
                    if pair in (5, 6):
                        values_out(u, (0, 1) if pair == 5 else (2,))
                running(ch, u, 1)
                values_out(u, (3,))
                done(ch)
                dve.reg_add(u_reg, u_reg, U)

                def step(c):
                    u, last, uc = dve.snap(u_reg), dve.snap(dve.snap(u_reg) - U), dve.snap(uc_reg)
                    keys_out(u)
                    dve.wait_ge(chunk_mask_in, uc)
                    dve.tensor_scalar(bias[:, :], chunk_mask[:, :], -1.0, -FAR, ALU.add, ALU.mult).then_inc(bias_done, U)
                    prepare_next((bits >> c) > 1)
                    ch = Chain(dve, dve_step, dve.snap(step_reg))
                    for pair in range(PAIRS):
                        probs_out(last, pair)
                        if pair == 0:
                            dve.wait_ge(bias_done, uc)
                        minima(u, 0, pair, bias[:, :])
                    running(ch, u, 0)
                    for pair in range(PAIRS):
                        minima(u, 1, pair, bias[:, :])
                        if pair in (1, 3):
                            back(last, pair // 2)
                        if pair == 4:
                            input_next(u, (bits >> c) > 1)
                        if pair in (5, 6):
                            values_out(u, (0, 1) if pair == 5 else (2,))
                    running(ch, u, 1)
                    values_out(u, (3,))
                    done(ch)
                    dve.reg_add(u_reg, u_reg, U)
                chunks(dve, bits, step)
                last = dve.snap(dve.snap(u_reg) - U)
                for pair in range(PAIRS):
                    probs_out(last, pair)
                back(last, 0)
                back(last, 1)
                u = dve.snap(u_reg)
                ch = Chain(dve, dve_step, dve.snap(step_reg))
                dve.wait_ge(total_done, u)
                dve.wait_ge(back_done, u)
                ch.link(dve.reciprocal(rtotal[:, :, :], total[:, :, :]))
                for t in range(TT):
                    by_head = o[:, t, :].rearrange("p (h d) -> p h d", d=DH)
                    dve.tensor_tensor(by_head, by_head, rtotal[:, t, :].unsqueeze(2).broadcast_to([P, H, DH]), ALU.mult)\
                        .then_inc(fin_ready, 1)
                with dve.If(turn < B):
                    input_out(u, R_G2, R_B2)
                for t in range(TT):
                    dve.wait_ge(x_full, turn * 2 + t + 1)
                    xt = k.x[:, bass.ds(b * TT + t, 1), :].rearrange("p o d -> p (o d)")
                    dve.tensor_tensor(xt, ps[:, OUT + t, 0:D], xt, ALU.add).then_inc(x_done, 1)
                done(ch)

        @block.gpsimd
        def _(pool):
            u_reg, ln_reg, step_reg = (pool.alloc_register(f"pool_{n}") for n in ("u", "ln", "step"))
            for r, first in ((u_reg, U), (ln_reg, 4)):
                pool.reg_mov(r, first)
            chain = Chain(pool, pool_step)
            pool.memset(rows[:, :], 0.0).then_inc(rows_zero, 1)
            pool.memset(qT[:, :, :], 0.0).then_inc(q_zero, 1)
            chain.link(pool.memset(half[:, :], -0.5))
            pool.reg_mov(step_reg, chain.n)
            def root(ln, n):
                pool.wait_ge(ln_var, ln + 1)
                pool.tensor_tensor(rstd[:, 0:n], var[:, 0:n], half[:, 0:n], ALU.pow).then_inc(ln_rstd, 1)

            def rescale(ch, u, t):
                pool.wait_ge(alpha_done, u + 8 * (t + 1))
                by_head = o[:, t, :].rearrange("p (h d) -> p h d", d=DH)
                pool.tensor_tensor(by_head, by_head, alpha[:, t, :].unsqueeze(2).broadcast_to([P, H, DH]), ALU.mult)\
                    .then_inc(o_scaled, U // TT)
                ch.link(pool.tensor_tensor(total[:, t, :], total[:, t, :], alpha[:, t, :], ALU.mult))

            def add_sums(u, t):
                pool.wait_ge(p_ready, u + 8 * (t + 1))
                pool.tensor_tensor(total[:, t, :], total[:, t, :], chunk_sum[:, t, :], ALU.add).then_inc(total_done, U // TT)

            def chunk_body(ch, u, more, last=None):
                with pool.If(more):
                    ln = pool.snap(ln_reg)
                    root(ln, KT)
                    pool.reg_add(ln_reg, ln_reg, 1)
                if last is not None:
                    add_sums(last, 1)
                pool.wait_ge(total_done, u)
                pool.wait_ge(back_done, u)
                rescale(ch, u, 0)
                rescale(ch, u, 1)
                add_sums(u, 0)
                pool.reg_add(u_reg, u_reg, U)

            for n in range(2):
                root(n, TT)
            pool.wait_ge(lats_done, 1)
            pool.tensor_copy(lat[:, :, :], lats[:, 0:TT, :]).then_inc(lat_ready, 1)
            for part in range(2):
                for kk in range(KD):
                    cols = slice(part * INNER, (part + 1) * INNER)
                    pool.wait_ge(w_high, part * KD + kk + 1)
                    pool.tensor_tensor(wkv[:, LOW, kk, cols], wkv_in[:, kk, cols], wkv[:, HIGH, kk, cols], ALU.subtract)\
                        .then_inc(w_split, 1)
            for n in range(2):
                root(2 + n, (B - 1) * TT)
            pool.wait_ge(lats_done, 2)
            pool.wait_ge(words_in, 16)
            with pool.Fori(1, B + 1) as turn:
                b = turn - 1
                ch = Chain(pool, pool_step, pool.snap(step_reg))
                u = pool.snap(u_reg)
                pool.wait_ge(fin_full, turn * 4)
                pool.wait_ge(fin_ready, turn * 2)
                hold(pool, pool_held)
                pool.memset(total[:, :, :], 0.0)
                ch.link(pool.memset(o[:, :, :], 0.0))
                bits = attended(pool, b)
                with pool.If(turn < B):
                    pool.wait_ge(inT_full, u + U)
                    hold(pool, pool_held)
                    pool.tensor_copy(lat[:, :, :], lats[:, bass.ds((turn & (B - 1)) * TT, TT), :]).then_inc(lat_ready, 1)
                chunk_body(ch, u, bits > 0)
                pool.reg_add(step_reg, step_reg, ch.n)

                def step(c):
                    ch = Chain(pool, pool_step, pool.snap(step_reg))
                    u = pool.snap(u_reg)
                    chunk_body(ch, u, (bits >> c) > 1, pool.snap(u - U))
                    pool.reg_add(step_reg, step_reg, ch.n)
                chunks(pool, bits, step)
                add_sums(pool.snap(pool.snap(u_reg) - U), 1)


N_ROW_DMAS = 7 + KINDS


def linear_attention(k):
    nc, io = k.nc, k.io
    k.place_layer_weights()
    U = 16
    STEPS = 9
    C = D
    with k.lin_place, ExitStack() as ctx:
        sb = lambda name, shape, dt=F32: k.sb(name, shape, dt, ctx)
        wq, wkv = k.lin_wq, k.lin_wkv
        wo = sb("lin_wo", [P, KD, C])
        bkv = sb("lin_bkv", [P, 2, 2, C])
        bo = sb("lin_bo", [P, C])
        xn = sb("lin_xn", [P, TT, C])
        xnT = sb("lin_xnT", [P, KD, T])
        qT = sb("lin_qT", [P, KD, T])
        kv = sb("lin_kv", [P, 2, TT, 2, C])
        state0 = sb("lin_state0", [P, KD, P])
        state = sb("lin_state", [P, KD, P])
        yn = sb("lin_yn", [P, TT, C])
        ynT = sb("lin_ynT", [P, KD, T])
        stats = sb("lin_stats", [P, TT, 6])
        mv = sb("lin_mv", [P, TT, 2])
        var = sb("lin_var", [P, TT])
        rstd = sb("lin_rstd", [P, TT])
        half = sb("lin_half", [P, TT])
        ps = k.banks("ps_lin", ctx)
        TURN, QUERY, KV, STATE, OUT, X, TURN_Y = 0, 1, 2, 4, 5, 6, 7

        sem = k.sem
        wo_in, bias_in = sem("lin_wo_in"), sem("lin_bias_in")
        xn_ready, xnT_full, xnT_done = sem("lin_xn_ready"), sem("lin_xnT_full"), sem("lin_xnT_done")
        q_full, q_done, kv_full, kv_done = sem("lin_q_full"), sem("lin_q_done"), sem("lin_kv_full"), sem("lin_kv_done")
        kv_read = sem("lin_kv_read")
        st_full, st_done, out_full = sem("lin_state_full"), sem("lin_state_done"), sem("lin_out_full")
        yn_ready, ynT_full, ynT_done = sem("lin_yn_ready"), sem("lin_ynT_full"), sem("lin_ynT_done")
        x_full, x_done = sem("lin_x_full"), sem("lin_x_done")
        ln_var, ln_rstd, dve_step, half_set, dve_held = sem("lin_ln_var"), sem("lin_ln_rstd"), sem("lin_dve_step"), sem("lin_half_set"), sem("lin_dve_held")

        block = ctx.enter_context(nc.Block())

        @block.sync
        def _(sp):
            begin_at(sp, U, (xn_ready, xnT_full, xnT_done, q_full, q_done, kv_full, kv_done, kv_read, st_full, st_done, out_full,
                             yn_ready, ynT_full, ynT_done, x_full, x_done))
            for s in range(2):
                for n, name in enumerate(("k", "v")):
                    sp.dma_start(bkv[:, s, n, :], io[f"attn_b{name}"][s:s + 1, :].broadcast_to([P, C])).then_inc(bias_in, 16)
            sp.dma_start(bo[:, :], io["attn_bo"].rearrange("(o n) -> o n", o=1).broadcast_to([P, C])).then_inc(bias_in, 16)
            sp.dma_start(wo[:, :, :], io["attn_Wo"].rearrange("(k p) n -> p k n", p=P)).then_inc(wo_in, 16)
            for which in ("qkv", "wo", "w1", "w2"):
                k.load_layer_weights(sp, 0, which)
            k.load_layer_vectors(sp)

        @block.tensor
        def _(pe):
            pe.wait_ge(k.lin_wq_in, 16)
            pe.wait_ge(k.lin_wkv_in, 64)
            pe.wait_ge(wo_in, 16)

            def turn_xn(u):
                pe.wait_ge(xn_ready, u + U)
                pe.wait_ge(xnT_done, u)
                for kk in range(KD):
                    for t in range(TT):
                        ins = pe.transpose(ps[:, TURN, kk * T + t * P:kk * T + (t + 1) * P],
                                           xn[:, t, kk * P:(kk + 1) * P], k.ident)
                ins.then_inc(xnT_full, U)

            def queries(u):
                pe.wait_ge(xnT_done, u + U)
                pe.wait_ge(q_done, u)
                for m in range(KD):
                    for kk in range(KD):
                        ins = pe.matmul(ps[:, QUERY, m * T:(m + 1) * T], wq[:, kk, m * P:(m + 1) * P], xnT[:, kk, :],
                                        start=kk == 0, stop=kk == KD - 1)
                ins.then_inc(q_full, U)

            def keys_values(u, s):
                for t in range(TT):
                    j = s * TT + t
                    pe.wait_ge(kv_read, u + (4 * (j - 1) if j >= 2 else 0))
                    for kk in range(KD):
                        ins = pe.matmul(ps[:, KV + j % 2, :], xnT[:, kk, t * P:(t + 1) * P],
                                        wkv[:, kk, s, :, :].rearrange("p n c -> p (n c)"),
                                        start=kk == 0, stop=kk == KD - 1)
                    ins.then_inc(kv_full, 4)

            def states(u):
                for s in range(2):
                    pe.wait_ge(kv_done, u + 8 * (s + 1))
                    for m in range(KD):
                        for t in range(TT):
                            ins = pe.matmul(ps[:, STATE, (s * KD + m) * P:(s * KD + m + 1) * P],
                                            kv[:, s, t, 0, m * P:(m + 1) * P], kv[:, s, t, 1, m * P:(m + 1) * P],
                                            start=t == 0, stop=t == TT - 1)
                ins.then_inc(st_full, U)

            def out(u):
                pe.wait_ge(st_done, u + U)
                pe.wait_ge(q_done, u + U)
                pe.wait_ge(yn_ready, u)
                for t in range(TT):
                    for m in range(KD):
                        ins = pe.matmul(ps[:, OUT, t * C + m * P:t * C + (m + 1) * P], qT[:, m, t * P:(t + 1) * P],
                                        state[:, m, :], start=True, stop=True)
                ins.then_inc(out_full, U)

            def turn_yn(u):
                pe.wait_ge(yn_ready, u + U)
                pe.wait_ge(ynT_done, u)
                for kk in range(KD):
                    for t in range(TT):
                        ins = pe.transpose(ps[:, TURN_Y, kk * T + t * P:kk * T + (t + 1) * P],
                                           yn[:, t, kk * P:(kk + 1) * P], k.ident)
                ins.then_inc(ynT_full, U)

            def project_out(u):
                pe.wait_ge(ynT_done, u + U)
                pe.wait_ge(x_done, u)
                for t in range(TT):
                    for kk in range(KD):
                        ins = pe.matmul(ps[:, X, t * C:(t + 1) * C], ynT[:, kk, t * P:(t + 1) * P], wo[:, kk, :],
                                        start=kk == 0, stop=kk == KD - 1)
                ins.then_inc(x_full, U)

            turn_xn(U)
            queries(U)
            keys_values(U, 0)
            keys_values(U, 1)
            states(U)
            with pe.Fori(2 * U, (B + 1) * U, U) as u:
                last = pe.snap(u - U)
                turn_xn(u)
                out(last)
                queries(u)
                keys_values(u, 0)
                turn_yn(last)
                keys_values(u, 1)
                project_out(last)
                states(u)
            out(B * U)
            turn_yn(B * U)
            project_out(B * U)

        @block.scalar
        def _(act):
            def xn_out(u):
                act.wait_ge(xnT_full, u + U)
                act.wait_ge(kv_full, u)
                act.wait_ge(q_done, u)
                act.activation(xnT[:, :, :], ps[:, TURN, :].rearrange("p (k t) -> p k t", k=KD), ACT.Copy).then_inc(xnT_done, U)

            def yn_out(u):
                act.wait_ge(ynT_full, u + U)
                act.wait_ge(x_full, u)
                for kk in range(KD):
                    ins = act.activation(ynT[:, kk, :], ps[:, TURN_Y, kk * T:(kk + 1) * T], ACT.Identity,
                                         bias=k.cols[:, R_LB + kk:R_LB + kk + 1], scale=k.cols[:, R_LG + kk:R_LG + kk + 1])
                ins.then_inc(ynT_done, U)

            xn_out(U)
            with act.Fori(2 * U, (B + 1) * U, U) as u:
                xn_out(u)
                yn_out(act.snap(u - U))
            yn_out(B * U)

        @block.vector
        def _(dve):
            xt = lambda b, t: k.x[:, bass.ds(b * TT + t, 1), :].rearrange("p o d -> p (o d)")
            yt = lambda b, t: k.y[:, bass.ds(b * TT + t, 1), :].rearrange("p o d -> p (o d)")

            def norm(ch, src, dst, n):
                hold(dve, dve_held)
                for t in range(TT):
                    ins = dve.bn_stats(stats[:, t, :], src(t))
                ch.link(ins)
                hold(dve, dve_held)
                for t in range(TT):
                    ins = dve.bn_aggr(mv[:, t, :], stats[:, t, :])
                ch.link(ins)
                dve.tensor_scalar(var[:, :], mv[:, :, 1], EPS, None, ALU.add).then_inc(ln_var, 1)
                dve.wait_ge(ln_rstd, n + 1)
                for t in range(TT):
                    ins = dve.tensor_scalar(dst(t), src(t), mv[:, t, 0:1], rstd[:, t:t + 1], ALU.subtract, ALU.mult)
                return ins

            def norm_x(ch, u, b, n):
                dve.wait_ge(xnT_full, u)
                dve.wait_ge(kv_done, u)
                norm(ch, lambda t: xt(b, t), lambda t: xn[:, t, :], n).then_inc(xn_ready, U)

            def queries_out(u):
                dve.wait_ge(q_full, u + U)
                dve.wait_ge(xnT_done, u + U)
                dve.wait_ge(out_full, u)
                for m in range(KD):
                    ins = dve.scalar_tensor_tensor(out=qT[:, m, :], in0=ps[:, QUERY, m * T:(m + 1) * T],
                                                   scalar=k.cols[:, R_BQ + m:R_BQ + m + 1], in1=xnT[:, m, :],
                                                   op0=ALU.add, op1=ALU.add)
                ins.then_inc(q_done, U)

            def keys_values_out(u):
                dve.wait_ge(xn_ready, u + U)
                dve.wait_ge(st_full, u)
                for s in range(2):
                    for t in range(TT):
                        j = s * TT + t
                        dve.wait_ge(kv_full, u + 4 * (j + 1))
                        dve.tensor_tensor(kv[:, s, t, :, :].rearrange("p n c -> p (n c)"), ps[:, KV + j % 2, :],
                                          bkv[:, s, :, :].rearrange("p n c -> p (n c)"), ALU.add).then_inc(kv_read, 4)
                        dve.wait_ge(kv_read, u + 4 * (j + 1))
                        dve.tensor_tensor(kv[:, s, t, :, :], kv[:, s, t, :, :],
                                          xn[:, t, :].unsqueeze(1).broadcast_to([P, 2, C]), ALU.add).then_inc(kv_done, 4)

            def states_out(ch, u):
                dve.wait_ge(st_full, u + U)
                dve.wait_ge(out_full, u)
                block_mask = k.const[:, C_BLOCK:C_BLOCK + P].unsqueeze(1).broadcast_to([P, KD, P])
                ch.link(dve.tensor_tensor(state0[:, :, :], ps[:, STATE, 0:KD * P].rearrange("p (m e) -> p m e", m=KD),
                                          block_mask, ALU.mult))
                dve.tensor_tensor(state[:, :, :], ps[:, STATE, KD * P:2 * KD * P].rearrange("p (m e) -> p m e", m=KD),
                                  state0[:, :, :], ALU.mult).then_inc(st_done, U)

            def norm_out(ch, u, n):
                dve.wait_ge(out_full, u + U)
                dve.wait_ge(ynT_full, u)
                norm(ch, lambda t: ps[:, OUT, t * C:(t + 1) * C], lambda t: yn[:, t, :], n).then_inc(yn_ready, U)

            def add_out(ch, u, b, n):
                both = k.x[:, bass.ds(b * TT, TT), :]
                ch.link(dve.tensor_tensor(both, both, bo[:, :].unsqueeze(1).broadcast_to([P, TT, C]), ALU.add))
                dve.wait_ge(x_full, u + U)
                dve.tensor_tensor(both, ps[:, X, :].rearrange("p (t c) -> p t c", t=TT), both, ALU.add).then_inc(x_done, U)
                dve.wait_ge(x_done, u + U)
                ch.link(norm(ch, lambda t: xt(b, t), lambda t: yt(b, t), n))

            def turn(ch, u, b, n, more):
                last = u - U if type(u) is int else dve.snap(u - U)
                queries_out(u)
                norm_out(ch, last, n)
                keys_values_out(u)
                if more:
                    norm_x(ch, u + U, b + 1, n + 1)
                states_out(ch, u)
                add_out(ch, last, b - 1, n + 1 + more)

            dve.wait_ge(bias_in, 80)
            first = Chain(dve, dve_step)
            norm_x(first, U, 0, 0)
            queries_out(U)
            keys_values_out(U)
            norm_x(first, 2 * U, 1, 1)
            states_out(first, U)
            with dve.Fori(1, B - 1) as b:
                ch = Chain(dve, dve_step, (b - 1) * STEPS + first.n)
                turn(ch, dve.snap(b * U + U), b, (b - 1) * 3 + 2, True)
                assert ch.n == STEPS
            ch = Chain(dve, dve_step, (B - 2) * STEPS + first.n)
            turn(ch, B * U, B - 1, (B - 2) * 3 + 2, False)
            norm_out(ch, B * U, 3 * B - 2)
            add_out(ch, B * U, B - 1, 3 * B - 1)

        @block.gpsimd
        def _(pool):
            pool.memset(half[:, :], -0.5).then_inc(half_set, 1)
            pool.wait_ge(half_set, 1)
            with pool.Fori(0, B * 3) as n:
                pool.wait_ge(ln_var, n + 1)
                pool.tensor_tensor(rstd[:, :], var[:, :], half[:, :], ALU.pow).then_inc(ln_rstd, 1)




def local_layers(k):
    nc = k.nc
    U = 16
    LAYER = B * U
    AHEAD = 4
    EARLY = 3
    SLOTS = 12
    with ExitStack() as ctx:
        sb = lambda name, shape, dt=F32: k.sb(name, shape, dt, ctx)
        wqkv, wo, w1, w2, b2, head_scale = k.wqkv, k.wo, k.w1, k.w2, k.b2, k.head_scale
        wqkv_in, wo_in, w1_in, w2_in, b2_in, scale_in = k.wqkv_in, k.wo_in, k.w1_in, k.w2_in, k.b2_in, k.scale_in
        cos = sb("cos", [P, TT, 2, DH])
        sin = sb("sin", [P, TT, 2, DH])
        vec = sb("vec", [P, KINDS])
        xT = sb("xT", [P, KD, T])
        qk = sb("qk", [P, TT, 2 * INNER])
        v = sb("v_loc", [P, 2, TT, INNER])
        work = sb("work", [P, 2, 2 * INNER])
        square = work[:, 0, :]
        twist = work[:, 1, :]
        norm2 = sb("norm2", [P, 2 * H])
        norm2_floor = sb("norm2_floor", [P, 2 * H])
        half = sb("half_loc", [P, 2 * H])
        rnorm = sb("rnorm", [P, 2, TT, 2 * H])
        qT = sb("qT_loc", [P, PAIRS, T])
        kT = sb("kT_loc", [P, PAIRS, 2, T])
        prob0 = sb("prob0", [P, H, P])
        uT = (qT[:, 0:FM, :], prob0[:, 0:2 * FM, :].rearrange("p (m a) t -> p m (a t)", a=2))
        prob1 = sb("prob1", [P, H, T])
        top = sb("top_loc", [P, TT, H])
        total = sb("total_loc", [P, TT, H])
        rtotal = sb("rtotal_loc", [P, TT, H])
        pT = sb("pT", [P, 2, 2 * T + 2 * P])
        oT = sb("oT_loc", [P, PAIRS, T])
        late = sb("late", [P, B * TT, P])
        xn = sb("xn_loc", [P, TT, D])
        xnT = sb("xnT_loc", [P, 2, KD, T])
        stats = sb("stats_loc", [P, TT, 2, 6])
        mv = sb("mv_loc", [P, TT, 2])
        var = sb("var_loc", [P, TT])
        rstd = sb("rstd_loc", [P, TT])
        gate = sb("gate", [P, 2, T])
        ps = k.banks("ps_loc", ctx)
        PROJ, PAIR, SCORE, TURN = 0, 2, 4, 6
        TURN_QK = (PAIR, PAIR + 1, TURN, TURN + 1)

        sem = k.sem
        zeros_set = sem("zeros_set")
        tables_done, vec_done = sem("tables_done"), sem("vec_done")
        xT_full, xT_done, qkv_full, qkv_done = sem("xT_full"), sem("xT_done"), sem("qkv_full"), sem("qkv_done")
        square_done, norm2_done, floor_done, rnorm_done = sem("square_done"), sem("norm2_done"), sem("floor_done"), sem("rnorm_done")
        twist_done, cos_done, sum_done, rope_done = sem("twist_done"), sem("cos_done"), sem("sum_done"), sem("rope_done")
        q_cos_done, q_rope_done = sem("q_cos_done"), sem("q_rope_done")
        qk_full, qk_done, k1_done = sem("qk_full"), sem("qk_done"), sem("k1_done")
        s_full, s_read, exp_done = sem("loc_s_full"), sem("loc_s_read"), sem("exp_done")
        rtotal_done, p_done, dve_held = sem("rtotal_done"), sem("p_done"), sem("loc_dve_held")
        pT_full, pT_done, o_full, o_done = sem("loc_pT_full"), sem("loc_pT_done"), sem("loc_o_full"), sem("loc_o_done")
        y_full, y_mid, y_out = sem("y_full"), sem("y_mid"), sem("y_out")
        late_in, edge_in = [sem(f"late_in{b}") for b in range(B)], [sem(f"edge_in{b}") for b in range(B)]
        bn_done, ln_stats, ln_var, ln_rstd, xn_done = sem("bn_done"), sem("loc_ln_stats"), sem("loc_ln_var"), sem("loc_ln_rstd"), sem("xn_done")
        xnT_full, xnT_done = sem("xnT_full"), sem("xnT_done")
        f_full, gate_done, u_done = sem("f_full"), sem("gate_done"), sem("u_done")
        f2_full, b2_done, x_sum = sem("f2_full"), sem("b2_done"), sem("x_sum")

        def after(n, last):
            return n + 1 if n < last else U

        def wide_bank(b, m):
            return (PAIR, PAIR + 1, TURN, TURN + 1, PROJ + 1, PROJ)[m] if b == 0 else PAIR + m % 2

        block = ctx.enter_context(nc.Block())

        @block.sync
        def _(sp):
            begin_at(sp, LAYER, (vec_done, tables_done, xT_full, xT_done, qkv_full, qkv_done, square_done, norm2_done, floor_done,
                                 rnorm_done, twist_done, cos_done, sum_done, rope_done, q_cos_done, q_rope_done, qk_full, qk_done, k1_done, s_full, s_read, exp_done,
                                 rtotal_done, p_done, pT_full, pT_done, o_full, o_done, y_full, y_mid, bn_done, ln_stats,
                                 ln_var, ln_rstd, xn_done, xnT_full, xnT_done, f_full, gate_done, u_done, f2_full, b2_done,
                                 wqkv_in, wo_in, w1_in, w2_in))
            begin_at(sp, 2 * LAYER, (y_out,))
            sp.wait_ge(zeros_set, 1)

            def shift(L, b):
                sp.wait_ge(y_mid, L + U * (b + 1))
                sp.dma_start(late[1:P, b * TT:(b + 1) * TT, :], k.y[0:P - 1, b * TT:(b + 1) * TT, P:D]).then_inc(late_in[b], 16)
                sp.dma_start(late[0:1, b * TT + 1, :], k.y[P - 1:P, b * TT, P:D]).then_inc(edge_in[b], 16)

            with sp.Fori(0, LAYERS - 1) as i:
                L = sp.snap(i * LAYER + LAYER)
                shift(L, 0)
                shift(L, 1)
                sp.wait_ge(qkv_full, L + LAYER)
                k.load_layer_weights(sp, i + 1, "qkv")
                shift(L, 2)
                shift(L, 3)
                k.load_layer_weights(sp, i + 1, "wo")
                sp.wait_ge(f_full, L + LAYER)
                k.load_layer_weights(sp, i + 1, "w1")
                sp.wait_ge(f2_full, L + LAYER)
                k.load_layer_weights(sp, i + 1, "w2")
            for b in range(B):
                shift(LAYERS * LAYER, b)

        @block.tensor
        def _(pe):
            def turn_x(L, b):
                pe.wait_ge(y_out, L + U * (b + 1))
                pe.wait_ge(qkv_done, L + U * b)
                if b == 0:
                    pe.wait_ge(xnT_done, L - U)
                for kk in range(KD):
                    for t in range(TT):
                        ins = pe.transpose(ps[:, PROJ, kk * T + t * P:kk * T + (t + 1) * P],
                                           k.y[:, b * TT + t, kk * P:(kk + 1) * P], k.ident)
                ins.then_inc(xT_full, U)

            def project(L, b, j):
                if j == 0:
                    if b == 0:
                        pe.wait_ge(wqkv_in, L + LAYER)
                        pe.wait_ge(xnT_done, L)
                    pe.wait_ge(xT_done, L + U * (b + 1))
                t, part = divmod(j, 4) if j < 8 else divmod(j - 8, 2)
                col = part * 512 if j < 8 else 2 * INNER + part * 512
                if j >= 2:
                    pe.wait_ge(qkv_done, L + U * b + j - 1)
                for kk in range(KD):
                    ins = pe.matmul(ps[:, PROJ + j % 2, :], xT[:, kk, t * P:(t + 1) * P], wqkv[:, kk, col:col + 512],
                                    start=kk == 0, stop=kk == KD - 1)
                ins.then_inc(qkv_full, 1 if j < SLOTS - 1 else U - SLOTS + 1)

            def turn_qk(L, b):
                pe.wait_ge(rope_done, L + U * (b + 1))
                pe.wait_ge(q_rope_done, L + U * (b + 1))
                pe.wait_ge(o_done, L + U * b)
                pe.wait_ge(pT_done, L + U * b)
                if b == 0:
                    pe.wait_ge(u_done, L)
                for g in range(8):
                    two, s = divmod(g, 2)
                    if g >= 4:
                        pe.wait_ge(qk_done, L + U * b + 2 * (g - 3))
                        if s:
                            pe.wait_ge(k1_done, L + U * b + 4 * (two - 1))
                    for i in range(2):
                        for t in range(TT):
                            col = s * INNER + (2 * two + i) * P
                            ins = pe.transpose(ps[:, TURN_QK[g % 4], i * T + t * P:i * T + (t + 1) * P],
                                               qk[:, t, col:col + P], k.ident)
                    ins.then_inc(qk_full, 2)

            def scores(L, b, s):
                pair, t = divmod(s, TT)
                if s == 0:
                    pe.wait_ge(y_mid, L + U * min(b, B - 2))
                    pe.wait_ge(y_out, L + LAYER)
                if s % (2 * TT) == 0:
                    pe.wait_ge(qk_done, L + U * b + 4 * (pair // 2 + 1))
                    pe.wait_ge(k1_done, L + U * b + 4 * (pair // 2 + 1))
                pe.wait_ge(s_read, L + U * b + (s - 1 if s >= 2 else 0))
                k0, k1 = (0, P) if t == 0 else (WINDOW, T)
                pe.matmul(ps[:, SCORE + t, 0:2 * (k1 - k0)], qT[:, pair, t * P:(t + 1) * P], kT[:, pair, :, k0:k1],
                          start=True, stop=True).then_inc(s_full, 1)

            def out(L, b, pair):
                pe.wait_ge(pT_done, L + U * b + 2 * pair + 2)
                pe.wait_ge(o_done, L + U * b + (2 * (pair - 1) if pair >= 2 else 0))
                for i in range(2):
                    col = (2 * pair + i) * DH
                    pe.matmul(ps[i * DH:(i + 1) * DH, PAIR + pair % 2, 0:T], v[:, b % 2, 0, col:col + DH],
                              pT[:, pair % 2, i * T:(i + 1) * T], start=True, stop=False)
                for i in range(2):
                    col = (2 * pair + i) * DH
                    ins = pe.matmul(ps[i * DH:(i + 1) * DH, PAIR + pair % 2, P:T], v[:, b % 2, 1, col:col + DH],
                                    pT[:, pair % 2, 2 * T + i * P:2 * T + (i + 1) * P], start=False, stop=True)
                ins.then_inc(o_full, 2)

            def weigh(L, b, pair):
                if pair == 0:
                    pe.wait_ge(qk_done, L + U * (b + 1))
                    pe.wait_ge(k1_done, L + U * (b + 1))
                    pe.wait_ge(u_done, L + (U if b == B - 1 else 0))
                    pe.wait_ge(qkv_done, L + U * (b + 1))
                pe.wait_ge(p_done, L + U * b + 2 * pair + 2)
                pe.wait_ge(pT_done, L + U * b + max(2 * pair - 1, 0))
                for i in range(2):
                    h = 2 * pair + i
                    pe.transpose(ps[:, TURN, i * T:i * T + P], prob0[:, h, :], k.ident)
                    ins = pe.transpose(ps[:, TURN, i * T + P:(i + 1) * T], prob1[:, h, 0:P], k.ident)
                ins.then_inc(pT_full, 1)
                pe.wait_ge(pT_done, L + U * b + 2 * pair)
                for i in range(2):
                    ins = pe.transpose(ps[:, TURN + 1, i * P:(i + 1) * P], prob1[:, 2 * pair + i, P:T], k.ident)
                ins.then_inc(pT_full, 1)
                if pair:
                    out(L, b, pair - 1)

            def project_out(L, b):
                if b == 0:
                    pe.wait_ge(wo_in, L + LAYER)
                if b == B - 1:
                    pe.wait_ge(y_mid, L + U * b)
                for pairs in (range(PAIRS - 1), (PAIRS - 1,)):
                    for t in range(TT):
                        pe.wait_ge(s_read, L + U * (b + 1 if b < B - 2 else B) - (TT - 1 - t))
                        for pair in pairs:
                            if t == 0:
                                pe.wait_ge(o_done, L + U * b + 2 * (pair + 1))
                            ins = pe.matmul(ps[:, SCORE + t, 0:D], oT[:, pair, t * P:(t + 1) * P], wo[:, pair, :],
                                            start=pair == 0, stop=pair == PAIRS - 1)
                ins.then_inc(y_full, U)

            def turn_xn(L, b):
                pe.wait_ge(xn_done, L + U * (b + 1))
                pe.wait_ge(qkv_done, L + LAYER)
                if b:
                    pe.wait_ge(u_done, L + U)
                if b >= 2:
                    pe.wait_ge(xnT_done, L + U * (b - 1))
                for kk in range(KD):
                    for t in range(TT):
                        ins = pe.transpose(ps[:, PROJ + b % 2, kk * T + t * P:kk * T + (t + 1) * P],
                                           xn[:, t, kk * P:(kk + 1) * P], k.ident)
                ins.then_inc(xnT_full, U)

            def widen(L, b, m):
                n = FWIDE[m]
                if m == 0:
                    if b == 0:
                        pe.wait_ge(w1_in, L + LAYER)
                        pe.wait_ge(qk_done, L + LAYER)
                        pe.wait_ge(k1_done, L + LAYER)
                    else:
                        pe.wait_ge(o_done, L + LAYER)
                    pe.wait_ge(xnT_done, L + U * (b + 1))
                if b:
                    pe.wait_ge(u_done, L + U * b + (m - 1 if m >= 2 else 0))
                for part in range(2):
                    for kk in range(KD):
                        ins = pe.matmul(ps[0:n, wide_bank(b, m), part * T:(part + 1) * T],
                                        w1[:, kk, part * FF + FAT[m]:part * FF + FAT[m] + n], xnT[:, b % 2, kk, :],
                                        start=kk == 0, stop=kk == KD - 1)
                ins.then_inc(f_full, 1 if m < FM - 1 else U - FM + 1)

            def narrow(L, b):
                if b == 0:
                    pe.wait_ge(w2_in, L + LAYER)
                pe.wait_ge(u_done, L + U * (b + 1))
                pe.wait_ge(y_mid, L + LAYER)
                if b >= 2:
                    pe.wait_ge(y_out, L + LAYER + U * (b - 1))
                for t in range(TT):
                    for m in range(FM):
                        ins = pe.matmul(ps[:, SCORE + b % 2, t * D:(t + 1) * D], uT[b % 2][0:FWIDE[m], m, t * P:(t + 1) * P], w2[0:FWIDE[m], m, :],
                                        start=m == 0, stop=m == FM - 1)
                ins.then_inc(f2_full, U)

            def weigh_rest(L, b, first=1):
                for pair in range(first, PAIRS):
                    weigh(L, b, pair)
                out(L, b, PAIRS - 1)

            def widen_all(L, b):
                for m in range(FM):
                    widen(L, b, m)

            def layer(L, last):
                for b in range(B):
                    if b:
                        weigh_rest(L, b - 1)
                    if 0 < b < B - 1:
                        project_out(L, b - 1)
                    turn_qk(L, b)
                    if b < B - 1:
                        turn_x(L, b + 1)
                        for s in range(U):
                            scores(L, b, s)
                            if s == U - 1:
                                weigh(L, b, 0)
                            if 0 <= s - AHEAD < SLOTS:
                                project(L, b + 1, s - AHEAD)
                    else:
                        turn_xn(L, 0)
                        for s in range(U):
                            scores(L, b, s)
                            if s % 2 and s < 2 * FM:
                                widen(L, 0, s // 2)
                project_out(L, B - 2)
                for pair in range(EARLY):
                    weigh(L, B - 1, pair)
                turn_xn(L, 1)
                weigh_rest(L, B - 1, EARLY)
                project_out(L, B - 1)
                widen_all(L, 1)
                turn_xn(L, 2)
                narrow(L, 0)
                widen_all(L, 2)
                turn_xn(L, 3)
                if not last:
                    turn_x(L + LAYER, 0)
                narrow(L, 1)
                if not last:
                    for j in range(SLOTS):
                        project(L + LAYER, 0, j)
                widen_all(L, 3)
                narrow(L, 2)
                narrow(L, 3)

            turn_x(LAYER, 0)
            for j in range(SLOTS):
                project(LAYER, 0, j)
            with pe.Fori(0, LAYERS - 1) as i:
                layer(pe.snap(i * LAYER + LAYER), False)
            layer(LAYERS * LAYER, True)

        @block.scalar
        def _(act):
            def x_out(L, b):
                act.wait_ge(qkv_full, L + U * b)
                act.wait_ge(xT_full, L + U * (b + 1))
                act.activation(xT[:, 0, :], ps[:, PROJ, 0:T], ACT.Copy)
                act.activation(xT[:, 1, 1:T], ps[:, PROJ, T:2 * T - 1], ACT.Copy).then_inc(xT_done, U)

            def qkv_out(L, b, j):
                if j == 0:
                    act.wait_ge(qk_full, L + U * b)
                    act.wait_ge(o_full, L + U * max(b - 1, 0))
                act.wait_ge(qkv_full, L + U * b + after(j, SLOTS - 1))
                t, part = divmod(j, 4) if j < 8 else divmod(j - 8, 2)
                dst = qk[:, t, part * 512:(part + 1) * 512] if j < 8 else v[:, b % 2, t, part * 512:(part + 1) * 512]
                act.activation(dst, ps[:, PROJ + j % 2, :], ACT.Copy).then_inc(qkv_done, 1 if j < SLOTS - 1 else U - SLOTS + 1)
                if j in (3, 7):
                    act.wait_ge(qkv_done, L + U * b + j + 1)
                    act.wait_ge(norm2_done, L + U * b + 8 * t)
                    act.activation(square, qk[:, t, :], ACT.Square).then_inc(square_done, 8)

            def qk_out(L, b):
                act.wait_ge(s_full, L + U * b)
                if b == 0:
                    act.wait_ge(f2_full, L - U)
                for g in range(8):
                    two, s = divmod(g, 2)
                    act.wait_ge(qk_full, L + U * b + 2 * (g + 1))
                    bank = ps[:, TURN_QK[g % 4], :].rearrange("p (i t) -> p i t", i=2)
                    if s == 0:
                        ins = act.activation(qT[:, 2 * two:2 * two + 2, :], bank, ACT.Copy)
                    else:
                        ins = act.activation(kT[0:DH, 2 * two:2 * two + 2, 0, :], bank[0:DH], ACT.Copy)
                    ins.then_inc(qk_done, 2)

            def exps(L, b, s):
                pair, t = divmod(s, TT)
                act.wait_ge(s_read, L + U * b + s + 1)
                for h in (2 * pair, 2 * pair + 1):
                    pr = prob0[:, h, :] if t == 0 else prob1[:, h, WINDOW:T]
                    ins = act.activation(pr, pr, ACT.Exp, bias=top[:, t, h:h + 1], scale=-1.0, accum_out=total[:, t, h:h + 1])
                ins.then_inc(exp_done, 1)

            def o_out(L, b, pair):
                act.wait_ge(o_full, L + U * b + 2 * (pair + 1))
                act.activation(oT[:, pair, :], ps[:, PAIR + pair % 2, 0:T], ACT.Copy).then_inc(o_done, 2)

            def weigh_out(L, b, pair):
                if pair == 0:
                    act.wait_ge(y_full, L + U * b)
                act.wait_ge(o_full, L + U * b + (2 * (pair - 1) if pair >= 2 else 0))
                act.wait_ge(pT_full, L + U * b + 2 * pair + 1)
                act.activation(pT[:, pair % 2, 0:2 * T], ps[:, TURN, :], ACT.Copy).then_inc(pT_done, 1)
                act.wait_ge(pT_full, L + U * b + 2 * pair + 2)
                act.activation(pT[:, pair % 2, 2 * T:], ps[:, TURN + 1, 0:2 * P], ACT.Copy).then_inc(pT_done, 1)
                if pair:
                    o_out(L, b, pair - 1)

            def widen_in(L, b):
                if b == 0:
                    act.wait_ge(vec_done, L + LAYER)
                act.wait_ge(f_full, L + U * max(b - 1, 0))
                act.wait_ge(xnT_full, L + U * (b + 1))
                for kk in range(KD):
                    ins = act.activation(xnT[:, b % 2, kk, :], ps[:, PROJ + b % 2, kk * T:(kk + 1) * T], ACT.Identity,
                                         bias=vec[:, V_FB + kk:V_FB + kk + 1], scale=vec[:, V_FG + kk:V_FG + kk + 1])
                ins.then_inc(xnT_done, U)

            def gates(L, b):
                for m in range(FM):
                    n = FWIDE[m]
                    if b == 0 and m >= 2:
                        act.wait_ge(u_done, L + m - 1)
                    act.wait_ge(f_full, L + U * b + after(m, FM - 1))
                    act.activation(gate[0:n, m % 2, :], ps[0:n, wide_bank(b, m), T:2 * T], ACT.Gelu,
                                   bias=vec[0:n, V_B1G + m:V_B1G + m + 1]).then_inc(gate_done, 1 if m < FM - 1 else U - FM + 1)

            def first(L):
                x_out(L, 0)
                for j in range(SLOTS):
                    qkv_out(L, 0, j)

            def weigh_out_rest(L, b, first=1):
                for pair in range(first, PAIRS):
                    weigh_out(L, b, pair)
                o_out(L, b, PAIRS - 1)

            def layer(L, last):
                for b in range(B):
                    if b:
                        weigh_out_rest(L, b - 1)
                    qk_out(L, b)
                    if b < B - 1:
                        x_out(L, b + 1)
                    else:
                        widen_in(L, 0)
                    for s in range(U):
                        exps(L, b, s)
                        if s == U - 1 and b < B - 1:
                            weigh_out(L, b, 0)
                        if b < B - 1 and 0 <= s - AHEAD < SLOTS:
                            qkv_out(L, b + 1, s - AHEAD)
                gates(L, 0)
                for pair in range(EARLY):
                    weigh_out(L, B - 1, pair)
                widen_in(L, 1)
                weigh_out_rest(L, B - 1, EARLY)
                gates(L, 1)
                widen_in(L, 2)
                gates(L, 2)
                widen_in(L, 3)
                if not last:
                    first(L + LAYER)
                gates(L, 3)

            act.wait_ge(zeros_set, 1)
            first(LAYER)
            with act.Fori(0, LAYERS - 1) as i:
                layer(act.snap(i * LAYER + LAYER), False)
            layer(LAYERS * LAYER, True)

        @block.vector
        def _(dve):
            def rotate(L, b, t, step):
                at = L + U * b + 8 * t
                by_head = qk[:, t, :].rearrange("p (s h d) -> p s h d", s=2, d=DH)
                if step == 0:
                    dve.wait_ge(square_done, at + 8)
                    dve.wait_ge(rnorm_done, at)
                    dve.tensor_reduce(norm2[:, :], square.rearrange("p (h d) -> p h d", d=DH), AX.X, ALU.add)\
                        .then_inc(norm2_done, 8)
                    dve.wait_ge(norm2_done, at + 8)
                    dve.tensor_scalar(norm2_floor[:, :], norm2[:, :], 1e-24, None, ALU.max).then_inc(floor_done, 8)
                elif step == 1:
                    dve.wait_ge(tables_done, L + LAYER)
                    dve.wait_ge(sum_done, at)
                    to_head = twist.rearrange("p (s h d) -> p s h d", s=2, d=DH)
                    lo, hi = slice(0, DH // 2), slice(DH // 2, DH)
                    for dst, src in ((lo, hi), (hi, lo)):
                        ins = dve.tensor_tensor(to_head[:, :, :, dst], by_head[:, :, :, src],
                                                sin[:, t, :, dst].unsqueeze(2).broadcast_to([P, 2, H, DH // 2]), ALU.mult)
                    ins.then_inc(twist_done, 8)
                elif t == TT - 1:
                    dve.wait_ge(twist_done, at + 8)
                    for n in (1, 0):
                        ins = dve.tensor_tensor(by_head[:, n], by_head[:, n], cos[:, t, n, :].unsqueeze(1).broadcast_to([P, H, DH]), ALU.mult)
                        if n:
                            ins.then_inc(cos_done, 8)
                    ins.then_inc(q_cos_done, U)
                    dve.wait_ge(q_cos_done, L + U * (b + 1))
                    dve.tensor_tensor(qk[:, t, 0:INNER], qk[:, t, 0:INNER], work[:, 1, 0:INNER], ALU.add).then_inc(q_rope_done, U)
                else:
                    dve.wait_ge(twist_done, at + 8)
                    dve.tensor_tensor(by_head, by_head, cos[:, t, :, :].unsqueeze(2).broadcast_to([P, 2, H, DH]), ALU.mult)\
                        .then_inc(cos_done, 8)

            def k1_out(L, b):
                dve.wait_ge(s_full, L + U * b)
                for two in range(4):
                    dve.wait_ge(qk_full, L + U * b + 4 * (two + 1))
                    bank = ps[DH:P, TURN_QK[(2 * two + 1) % 4], :].rearrange("p (i t) -> p i t", i=2)
                    dve.tensor_copy(kT[DH:P, 2 * two:2 * two + 2, 1, :], bank).then_inc(k1_done, 4)

            def softmax(L, b):
                def share(s):
                    if s < U:
                        pair, t = divmod(s, TT)
                        h = 2 * pair
                        dve.wait_ge(exp_done, L + U * b + s + 1)
                        dve.reciprocal(rtotal[:, t, h:h + 2], total[:, t, h:h + 2]).then_inc(rtotal_done, 1)
                    if s:
                        pair, t = divmod(s - 1, TT)
                        h = 2 * pair
                        dve.wait_ge(rtotal_done, L + U * b + s)
                        for n in range(2):
                            pr = prob0[:, h + n, :] if t == 0 else prob1[:, h + n, WINDOW:T]
                            ins = dve.tensor_scalar(pr, pr, rtotal[:, t, h + n:h + n + 1], None, ALU.mult)
                        ins.then_inc(p_done, 1)

                LAG = 3
                dve.wait_ge(rnorm_done, L + U * (b + 1))
                if b == 0:
                    dve.wait_ge(pT_full, L)
                    dve.wait_ge(f2_full, L)
                between = {9: (0, 0), 11: (0, 1), 13: (0, 2)} if b < B - 1 else {}
                for s in range(U):
                    pair, t = divmod(s, TT)
                    if b and t == 0:
                        dve.wait_ge(pT_full, L + U * (b - 1) + 2 * (pair + 1))
                    n = P if t == 0 else T - WINDOW
                    band = k.const[:, C_BAND0:C_BAND0 + n] if t == 0 else k.const[:, C_BAND1:C_BAND1 + n]
                    dve.wait_ge(s_full, L + U * b + s + 1)
                    hold(dve, dve_held)
                    for e in range(2):
                        h = 2 * pair + e
                        ins = dve.tensor_tensor_reduce(
                            out=prob0[:, h, :] if t == 0 else prob1[:, h, WINDOW:T],
                            in0=ps[:, SCORE + t, e * n:(e + 1) * n], in1=band, scale=rnorm[:, b % 2, t, h:h + 1],
                            scalar=FAR, op0=ALU.add, op1=ALU.min, accum_out=top[:, t, h:h + 1])
                    ins.then_inc(s_read, 1)
                    if s >= LAG:
                        share(s - LAG)
                    if s in between:
                        rotate(L, b + 1, *between[s])
                for s in range(U - LAG, U + 1):
                    share(s)
                if b < B - 1:
                    for t in range(TT):
                        for step in range(3):
                            if (t, step) not in between.values():
                                rotate(L, b + 1, t, step)

            def add_attention(L, b):
                dve.wait_ge(y_full, L + U * (b + 1))
                both = k.y[:, b * TT:(b + 1) * TT, :]
                dve.tensor_tensor(both, ps[:, SCORE:SCORE + TT, 0:D], both, ALU.add).then_inc(y_mid, U)

            def norm(L, shifts, b):
                dve.wait_ge(y_mid, L + U * (b + 1))
                dve.wait_ge(late_in[b], shifts)
                dve.wait_ge(edge_in[b], shifts)
                dve.wait_ge(xnT_full, L + U * b)
                halves = lambda t: (k.y[:, b * TT + t, 0:P], late[:, b * TT + t, :])
                for t in range(TT):
                    for n, part in enumerate(halves(t)):
                        ins = dve.bn_stats(stats[:, t, n, :], part)
                ins.then_inc(bn_done, U)
                dve.wait_ge(bn_done, L + U * (b + 1))
                hold(dve, dve_held)
                for t in range(TT):
                    ins = dve.bn_aggr(mv[:, t, :], stats[:, t, :, :].rearrange("p n s -> p (n s)"))
                ins.then_inc(ln_stats, U)
                dve.wait_ge(ln_stats, L + U * (b + 1))
                dve.tensor_scalar(var[:, :], mv[:, :, 1], EPS, None, ALU.add).then_inc(ln_var, U)
                dve.wait_ge(ln_rstd, L + U * (b + 1))
                for t in range(TT):
                    for n, part in enumerate(halves(t)):
                        ins = dve.tensor_scalar(xn[:, t, n * P:(n + 1) * P], part, mv[:, t, 0:1], rstd[:, t:t + 1],
                                                ALU.subtract, ALU.mult)
                ins.then_inc(xn_done, U)

            def gated(L, b, ms=range(FM)):
                if b >= 2:
                    dve.wait_ge(f2_full, L + U * (b - 1))
                elif b == 1:
                    dve.wait_ge(pT_full, L + LAYER)
                else:
                    dve.wait_ge(s_full, L + LAYER)
                for m in ms:
                    n = FWIDE[m]
                    dve.wait_ge(gate_done, L + U * b + after(m, FM - 1))
                    dve.scalar_tensor_tensor(out=uT[b % 2][0:n, m, :], in0=ps[0:n, wide_bank(b, m), 0:T],
                                             scalar=vec[0:n, V_B1A + m:V_B1A + m + 1], in1=gate[0:n, m % 2, :],
                                             op0=ALU.add, op1=ALU.mult).then_inc(u_done, 1 if m < FM - 1 else U - FM + 1)

            def add_ffn(L, b):
                dve.wait_ge(b2_done, L + U * (b + 1))
                dve.wait_ge(f2_full, L + U * (b + 1))
                both = k.y[:, b * TT:(b + 1) * TT, :]
                dve.tensor_tensor(both, ps[:, SCORE + b % 2, :].rearrange("p (t c) -> p t c", t=TT), both, ALU.add).then_inc(y_out, U)

            dve.wait_ge(zeros_set, 1)
            def first(L):
                for t in range(TT):
                    for step in range(3):
                        rotate(L, 0, t, step)

            def first_and_gated(L):
                for t in range(TT):
                    for step in range(3):
                        rotate(L + LAYER, 0, t, step)
                        if t == TT - 1:
                            gated(L, B - 1, range(step * FM // 3, (step + 1) * FM // 3))

            def layer(i, L, shifts, last):
                dve.wait_ge(gate_done, L)
                dve.wait_ge(u_done, L)
                kinds = k.cols[:, R_LAYER:ROWS].rearrange("p (v i) -> p v i", i=LAYERS)
                dve.tensor_copy(vec[:, :], kinds[:, :, bass.ds(i, 1)].rearrange("p v o -> p (v o)")).then_inc(vec_done, LAYER)
                dve.wait_ge(vec_done, L + LAYER)
                for b in range(B):
                    if 0 < b < B - 1:
                        add_attention(L, b - 1)
                    if b == B - 1:
                        norm(L, shifts, 0)
                    k1_out(L, b)
                    softmax(L, b)
                gated(L, 0)
                norm(L, shifts, 1)
                add_attention(L, B - 2)
                add_attention(L, B - 1)
                norm(L, shifts, 2)
                gated(L, 1)
                norm(L, shifts, 3)
                add_ffn(L, 0)
                gated(L, 2)
                add_ffn(L, 1)
                if last:
                    gated(L, B - 1)
                else:
                    first_and_gated(L)
                add_ffn(L, 2)
                add_ffn(L, 3)

            first(LAYER)
            with dve.Fori(0, LAYERS - 1) as i:
                layer(i, dve.snap(i * LAYER + LAYER), dve.snap(i * 16 + 16), False)
            layer(LAYERS - 1, LAYERS * LAYER, LAYERS * 16, True)
            dve.wait_ge(y_out, (LAYERS + 2) * LAYER)
            dve.tensor_tensor(k.x[:, :, :], k.x[:, :, :], k.y[:, :, :], ALU.add).then_inc(x_sum, 1)

        @block.gpsimd
        def _(pool):
            pool.memset(half[:, :], -0.5)
            for buf in (kT[:, :, :, :], prob1[:, :, :], xT[:, 1, 0:1], late[0:1, :, :]):
                ins = pool.memset(buf, 0.0)
            ins.then_inc(zeros_set, 1)
            pool.wait_ge(zeros_set, 1)
            pool.wait_ge(scale_in, 32)
            pool.wait_ge(b2_in, 16)

            def tables(L, i):
                pool.wait_ge(cos_done, L)
                pool.wait_ge(q_cos_done, L)
                scale = head_scale[:, bass.ds(i, 1), :, :].rearrange("p o s d -> p (o s) d")
                for t in range(TT):
                    row = lambda at: k.const[:, at + t * 2 * DH:at + (t + 1) * 2 * DH].rearrange("p (s d) -> p s d", s=2)
                    pool.tensor_tensor(cos[:, t, :, :], row(C_COS), scale, ALU.mult)
                    lo, hi = slice(0, DH // 2), slice(DH // 2, DH)
                    for dst, src in ((lo, hi), (hi, lo)):
                        ins = pool.tensor_tensor(sin[:, t, :, dst], row(C_SIN)[:, :, dst], scale[:, :, src], ALU.mult)
                ins.then_inc(tables_done, LAYER)

            def rotate(L, b):
                for t in range(TT):
                    at = L + U * b + 8 * t
                    pool.wait_ge(floor_done, at + 8)
                    pool.wait_ge(s_read, L + U * max(b - 1, 0))
                    pool.tensor_tensor(rnorm[:, b % 2, t, :], norm2_floor[:, :], half[:, :], ALU.pow).then_inc(rnorm_done, 8)
                    pool.wait_ge(cos_done, at + 8)
                    cols = slice(INNER if t == TT - 1 else 0, 2 * INNER)
                    pool.tensor_tensor(qk[:, t, cols], qk[:, t, cols], work[:, 1, cols], ALU.add).then_inc(sum_done, 8)
                    pool.wait_ge(rnorm_done, at + 8)
                    pool.wait_ge(sum_done, at + 8)
                    keys = qk[:, t, INNER:].rearrange("p (h d) -> p h d", d=DH)
                    pool.tensor_tensor(keys, keys, rnorm[:, b % 2, t, H:].unsqueeze(2).broadcast_to([P, H, DH]), ALU.mult)\
                        .then_inc(rope_done, 8)

            def norm(L, i, b):
                pool.wait_ge(ln_var, L + U * (b + 1))
                pool.tensor_tensor(rstd[:, :], var[:, :], half[:, 0:TT], ALU.pow).then_inc(ln_rstd, U)
                pool.wait_ge(xn_done, L + U * (b + 1))
                both = k.y[:, b * TT:(b + 1) * TT, :]
                pool.tensor_tensor(both, both, b2[:, bass.ds(i, 1), :].broadcast_to([P, TT, D]), ALU.add).then_inc(b2_done, U)

            def layer(i, L, last):
                for b in range(1, B):
                    rotate(L, b)
                if not last:
                    tables(L + LAYER, i + 1)
                for b in range(B):
                    norm(L, i, b)
                if not last:
                    rotate(L + LAYER, 0)

            tables(LAYER, 0)
            rotate(LAYER, 0)
            with pool.Fori(0, LAYERS - 1) as i:
                layer(i, pool.snap(i * LAYER + LAYER), False)
            layer(LAYERS - 1, LAYERS * LAYER, True)




def store(k):
    nc, io = k.nc, k.io
    with ExitStack() as ctx:
        out_done = k.sem("out_done")
        block = ctx.enter_context(nc.Block())

        @block.sync
        def _(sp):
            sp.dma_start(io["out"].rearrange("b (t p) c -> p (b t) c", p=P), k.x[:, :, :]).then_inc(out_done, 16)
            sp.wait_ge(out_done, 16)


STAGES = (cross_attention, linear_attention, local_layers, store)


def build(nc, io, stages=None):
    with ExitStack() as ctx:
        k = Kernel(nc, ctx, io)
        for stage in stages or STAGES:
            stage(k)


_INS = ["x", "ctx_1024", "xattn_g1", "xattn_b1", "xattn_g2", "xattn_b2", "xattn_Wq", "xattn_Wkv", "xattn_Wout",
        "attn_Wq", "attn_bq", "attn_Wk", "attn_bk", "attn_Wv", "attn_bv", "attn_Wo", "attn_bo", "attn_ln_g", "attn_ln_b",
        "ffn_Wqkv", "ffn_q_scale", "ffn_k_scale", "ffn_Wo", "ffn_ln_g", "ffn_ln_b", "ffn_W1", "ffn_b1", "ffn_W2", "ffn_b2"]


def prepare(nc, inputs):
    arrays, io = {}, {}

    def add(name, a):
        a = np.ascontiguousarray(a)
        arrays[f"in_{name}_dram"] = a
        io[name] = nc.dram_tensor(f"in_{name}_dram", a.shape, mybir.dt.from_np(a.dtype), kind="ExternalInput").ap()

    for name in _INS:
        add(name, inputs[name if name in ("x", "ctx_1024") else f"L0_{name}"])
    add("mask", np.asarray(inputs["mask_BxS2_bk0"]))
    add("const", constants())
    io["out"] = nc.dram_tensor("out_0_dram", (B, T, D), F32, kind="ExternalOutput").ap()
    return arrays, io


def kernel(**inputs):
    import concourse.bacc as _bacc
    from concourse.bass_utils import run_bass_kernel_spmd as _run

    nc = _bacc.Bacc("TRN2", target_bir_lowering=False, num_devices=1)
    arrays, io = prepare(nc, inputs)
    build(nc, io)
    r = _run(nc, [arrays], core_ids=[0])
    return r.results[0]["out_0_dram"]
```
